# Optimizing a Trainium2 kernel written in Bass

```python
import numpy as np
import jax
import jax.numpy as jnp

def _softmax(x, axis=-1):
    return jax.nn.softmax(x, axis=axis)

def _gelu(x):
    return jax.nn.gelu(x, approximate=True)

def _silu(x):
    return jax.nn.silu(x)

def _sigmoid(x):
    return jax.nn.sigmoid(x)

def _layernorm(x, axis=-1, eps=1e-05):
    m = jnp.mean(x, axis=axis, keepdims=True)
    v = jnp.var(x, axis=axis, keepdims=True)
    return (x - m) / jnp.sqrt(v + eps)

def _scatter_add(tgt, idx, src, axis=0):
    return tgt.at[idx].add(src)

def _segment_sum(src, seg, n):
    return jax.ops.segment_sum(src, seg, n)
kernel_name = 'mk_gnn_preln_d2_gnn_r64_64d637'

def setup_inputs(seed: int=0):
    np.random.seed(seed)
    _w = jnp.asarray

    def _rec_inputs():
        import jax
        import jax.numpy as jnp
        _gk = jax.random.key(seed)
        x = -0.0005121 + 1.001 * jax.random.normal(jax.random.fold_in(_gk, 1), (100000, 64), jnp.float32)
        src = jax.random.randint(jax.random.fold_in(_gk, 2), (50000,), 0, 100000, jnp.int32)
        dst = jax.random.randint(jax.random.fold_in(_gk, 3), (50000,), 0, 100000, jnp.int32)
        _o = jnp.argsort(dst, stable=True)
        src = src[_o]
        dst = dst[_o]
        edge_attr_32 = -5.16925e-05 + 1.00005 * jax.random.normal(jax.random.fold_in(_gk, 13), (50000, 32), jnp.float32)
        edge_weight = jax.random.uniform(jax.random.fold_in(_gk, 15), (50000,), jnp.float32, 0.0, 0.999999)
        return (x, src, dst, edge_attr_32, edge_weight)
    x, src, dst, edge_attr_32, edge_weight = _rec_inputs()

    def _L0_gnn_setup():
        import jax, jax.numpy as jnp
        import numpy as np
        N_NODES = 50000
        N_EDGES = 12500
        D_IN = 64
        D_OUT = 64
        key = jax.random.key(seed)
        k_feat, k_src, k_dst, k_ew, k_wn, k_bn, k_ws = jax.random.split(key, 7)
        feat = jax.random.normal(k_feat, (N_NODES, D_IN), dtype=jnp.float32)
        src = jax.random.randint(k_src, (N_EDGES,), 0, N_NODES, dtype=jnp.int64)
        dst = jax.random.randint(k_dst, (N_EDGES,), 0, N_NODES, dtype=jnp.int64)
        edge_weight = jax.random.uniform(k_ew, (N_EDGES,), dtype=jnp.float32)
        W_neigh = jax.random.normal(k_wn, (D_IN, D_OUT), dtype=jnp.float32) / np.sqrt(D_IN)
        b_neigh = jax.random.normal(k_bn, (D_OUT,), dtype=jnp.float32) * 0.01
        W_self = jax.random.normal(k_ws, (D_OUT, D_IN), dtype=jnp.float32) / np.sqrt(D_IN)
        return {'feat': feat, 'src': src, 'dst': dst, 'edge_weight': edge_weight, 'W_neigh': W_neigh, 'b_neigh': b_neigh, 'W_self': W_self}
    _L0_gnn_all = _L0_gnn_setup()
    _L0_gnn_in = {k: v for k, v in _L0_gnn_all.items() if k in ('W_neigh', 'b_neigh', 'W_self')}
    del _L0_gnn_all

    def _L1_gnn_setup():
        import jax, jax.numpy as jnp
        import numpy as np
        N_NODES = 100000
        N_EDGES = 50000
        EDGE_OUT = 32
        HID = 128
        NODE_OUT = 64
        N_GRAPHS = 16
        key = jax.random.key(seed)
        ks = jax.random.split(key, 9)
        x = jax.random.normal(ks[0], (N_NODES, 64), dtype=jnp.float32)
        edge_index = jax.random.randint(ks[1], (2, N_EDGES), 0, N_NODES, dtype=jnp.int64)
        edge_attr = jax.random.normal(ks[2], (N_EDGES, EDGE_OUT), dtype=jnp.float32)
        u = jax.random.normal(ks[3], (N_GRAPHS, 1), dtype=jnp.float32)
        batch = jnp.sort(jax.random.randint(ks[4], (N_NODES,), 0, N_GRAPHS, dtype=jnp.int64))
        d_in = 3 * EDGE_OUT + 1
        W1 = jax.random.normal(ks[5], (d_in, HID), dtype=jnp.float32) / np.sqrt(d_in)
        b1 = jnp.zeros((HID,), dtype=jnp.float32)
        W2 = jax.random.normal(ks[6], (HID, NODE_OUT), dtype=jnp.float32) / np.sqrt(HID)
        b2 = jnp.zeros((NODE_OUT,), dtype=jnp.float32)
        return {'x': x, 'edge_index': edge_index, 'edge_attr': edge_attr, 'u': u, 'batch': batch, 'W1': W1, 'b1': b1, 'W2': W2, 'b2': b2}
    _L1_gnn_all = _L1_gnn_setup()
    _L1_gnn_in = {k: v for k, v in _L1_gnn_all.items() if k in ('u', 'W1', 'b1', 'W2', 'b2')}
    del _L1_gnn_all
    return {'x': x, 'src': src, 'dst': dst, 'edge_attr_32': edge_attr_32, 'edge_weight': edge_weight, 'L0_gnn_W_neigh': _L0_gnn_in['W_neigh'], 'L0_gnn_b_neigh': _L0_gnn_in['b_neigh'], 'L0_gnn_W_self': _L0_gnn_in['W_self'], 'L1_gnn_u': _L1_gnn_in['u'], 'L1_gnn_W1': _L1_gnn_in['W1'], 'L1_gnn_b1': _L1_gnn_in['b1'], 'L1_gnn_W2': _L1_gnn_in['W2'], 'L1_gnn_b2': _L1_gnn_in['b2']}

def reference(x, src, dst, edge_attr_32, edge_weight, L0_gnn_W_neigh, L0_gnn_b_neigh, L0_gnn_W_self, L1_gnn_u, L1_gnn_W1, L1_gnn_b1, L1_gnn_W2, L1_gnn_b2):
    import jax
    import jax.numpy as jnp

    def _L0_gnn_ref(feat, src, dst, edge_weight, W_neigh, b_neigh, W_self):
        import jax, jax.numpy as jnp
        import numpy as np
        N_NODES = 50000
        N_EDGES = 12500
        D_IN = 64
        D_OUT = 64
        msg = feat[src] * edge_weight[:, None]
        agg = jax.ops.segment_sum(msg, dst, num_segments=feat.shape[0])
        neigh_feat = agg @ W_neigh + b_neigh
        self_feat = feat @ W_self.T
        return neigh_feat + self_feat

    def _L1_gnn_ref(x, edge_index, edge_attr, u, batch, W1, b1, W2, b2):
        import jax, jax.numpy as jnp
        import numpy as np
        N_NODES = 100000
        N_EDGES = 50000
        EDGE_OUT = 32
        HID = 128
        NODE_OUT = 64
        N_GRAPHS = 16
        N = x.shape[0]
        row = edge_index[0]
        seg_sum = jax.ops.segment_sum(edge_attr, row, num_segments=N)
        seg_max = jax.ops.segment_max(edge_attr, row, num_segments=N)
        cnt = jax.ops.segment_sum(jnp.ones((edge_attr.shape[0], 1), edge_attr.dtype), row, num_segments=N)
        seg_mean = seg_sum / jnp.maximum(cnt, 1.0)
        seg_max = jnp.where(cnt > 0, seg_max, 0.0)
        h = jnp.concatenate([seg_sum, seg_max, seg_mean, u[batch]], axis=1)
        h = jax.nn.relu(h @ W1 + b1)
        return h @ W2 + b2
    edge_index = jnp.stack([src, dst])
    batch0 = jnp.zeros((100000,), jnp.int32)
    h = jnp.maximum(_layernorm(x, axis=-1), 0.0)
    x = x + _L0_gnn_ref(h, src, dst, edge_weight, L0_gnn_W_neigh, L0_gnn_b_neigh, L0_gnn_W_self)
    h = jnp.maximum(_layernorm(x, axis=-1), 0.0)
    x = x + _L1_gnn_ref(h, edge_index, edge_attr_32, L1_gnn_u, batch0, L1_gnn_W1, L1_gnn_b1, L1_gnn_W2, L1_gnn_b2)
    return x

_drawn_inputs = setup_inputs


def setup_inputs(seed=0):
    import zlib

    import numpy as np

    out = dict(_drawn_inputs(seed))
    spreads = {'L1_gnn_b1': (0.0, 0.1), 'L1_gnn_b2': (0.0, 0.1)}
    factors = {'L0_gnn_b_neigh': 6.786}
    for name, (base, spread) in spreads.items():
        noise = np.random.default_rng([zlib.crc32(name.encode()), seed]).standard_normal(out[name].shape)
        drawn = base * np.exp(spread * noise) if base else spread * noise
        out[name] = jnp.asarray(drawn.astype(out[name].dtype))
    for name, factor in factors.items():
        out[name] = (out[name] * factor).astype(out[name].dtype)
    return out
```

```python
from contextlib import ExitStack

import concourse.bass as bass
from concourse import mybir

F32 = mybir.dt.float32
BF16 = mybir.dt.bfloat16
F16 = mybir.dt.float16
I32 = mybir.dt.int32
U32 = mybir.dt.uint32
ALU = mybir.AluOpType
ACT = mybir.ActivationFunctionType
AX = mybir.AxisListType.X

P = 128
GT = 8
DIGIT = 32
FLT_MAX = 3.4028234663852886e38
EPS = 1e-5


class Own:

    def __init__(self, sem, paced):
        self.sem, self.paced, self.done, self.n, self.at, self.per = sem, paced, 0, 0, None, 0

    def loop(self, i, per):
        self.done += self.n
        self.at, self.per, self.n = i, per, 0

    def end(self, trips):
        assert self.n == self.per, (self.n, self.per)
        self.done += trips * self.per
        self.at, self.n = None, 0

    def __call__(self, ins):
        self.n += 1
        ins.then_inc(self.sem, 1)
        value = self.done + self.n
        self.eng.wait_ge(self.sem, value if self.at is None else self.at * self.per + value)
        if self.paced is not None and self.at is not None:
            self.eng.sem_inc(self.paced, 1)


def graph_layers(nc, x, src, dst, attr, weight, w_neigh, b_neigh, w_self, u, w1, b1, w2, b2, out):
    N, D = x.shape
    E, DE = attr.shape
    HID = w1.shape[1]
    KU = 3 * DE
    FT = E // P
    TAIL = E - FT * P
    NW = -(-N // P)
    LASTN = N - (NW - 1) * P
    NG = 2 * (-(-(FT + 1) // (2 * GT)))
    NT = NG * GT
    FG = FT // GT
    RT = FT - FG * GT
    RE = DE + 1
    RM = D + 1
    LANES = DIGIT * DIGIT
    NCODE = LANES
    assert D == 64 and DE == 32 and HID == P and 0 < TAIL < P and NW <= LANES and FG % 2 == 0
    XG = 4 * D

    ctx = ExitStack()
    with ctx:
        def sb(name, shape, dt=F32):
            return ctx.enter_context(nc.sbuf_tensor(name, shape, dt))

        def sem(name):
            return ctx.enter_context(nc.semaphore(name))

        def dram(name, shape, dt=F32):
            return nc.dram_tensor(name, shape, dt, kind="Internal").ap()

        ROWS = E + P + 48
        by_lane = dram("by_lane", [P, NT, RE])
        by_node = dram("by_node", [P, NT, RE])
        message = dram("message", [ROWS, RM])
        mlp_row = dram("mlp_row", [ROWS, RM])
        spare = dram("spare", [2, 1])
        starts_d = dram("starts_d", [2, LANES], I32)

        ident = sb("ident", [P, P])
        identb = sb("identb", [P, P], BF16)
        identh = sb("identh", [P, P], F16)
        later = sb("later", [P, P], F16)
        before = sb("before", [P, DIGIT])
        iota_d = sb("iota_d", [P, DIGIT], BF16)
        iota_n = sb("iota_n", [P, P])
        first_of = sb("first_of", [P, NW + GT])
        chain_mask = sb("chain_mask", [DIGIT, DIGIT, GT + 1])
        ones = sb("ones", [P, 512])
        eps_t = sb("eps_t", [P, 1])

        wn2 = sb("wn2", [P, P])
        ws_raw = sb("ws_raw", [D, 2, D])
        wsT2 = sb("wsT2", [P, P])
        w1_sb = sb("w1_sb", [KU, HID])
        w1u = sb("w1u", [P, 1])
        u0 = sb("u0", [P, 1])
        b1c = sb("b1c", [P, 1])
        hbias = sb("hbias", [P, 1])
        hrelu = sb("hrelu", [P, 1])
        hrelu_b = sb("hrelu_b", [P, P])
        w2_sb = sb("w2_sb", [P, D])
        b2b = sb("b2b", [P, D])
        bnb = sb("bnb", [P, D])
        c0b = sb("c0b", [P, D])
        biasb = sb("biasb", [P, D])

        src_i = sb("src_i", [P, NT + GT], I32)
        dst_i = sb("dst_i", [P, NT + GT], I32)
        ew = sb("ew", [P, NT])
        src_f = sb("src_f", [P, NT])
        dst_f = sb("dst_f", [P, NT])
        node_f = sb("node_f", [P, NT])
        near_f = sb("near_f", [P, NT])
        sign_b = sb("sign_b", [P, NT], BF16)
        key_v = sb("key_v", [P, NT])
        code_i = sb("code_i", [P, NT + GT], I32)
        digit_i = sb("digit_i", [P, NT + GT], I32)
        code_f = sb("code_f", [P, NT + GT])
        code_h = sb("code_h", [P, NT + GT], F16)
        hi_b = sb("hi_b", [P, NT + GT], BF16)
        lo_b = sb("lo_b", [P, NT + GT], BF16)
        earlier = sb("earlier", [P, NT])
        base_e = sb("base_e", [P, NT])
        pos_i = sb("pos_i", [P, NT], I32)
        pos_lo = sb("pos_lo", [P, NT], I32)
        idx_lane = sb("idx_lane", [P, NT], U32)
        idx_node = sb("idx_node", [P, NT], U32)
        idx_msg = sb("idx_msg", [P, NT], U32)
        idx_src = sb("idx_src", [P, NT], U32)
        rows = sb("rows", [P, NT, RE])

        oh_hi = [sb(f"oh_hi{b}", [P, GT, DIGIT], BF16) for b in range(2)]
        oh_lo = [sb(f"oh_lo{b}", [P, GT, DIGIT], BF16) for b in range(2)]
        code_s = [sb(f"code_s{b}", [P, GT], F16) for b in range(2)]
        ohT = [sb(f"ohT{b}", [DIGIT, GT, P]) for b in range(2)]
        hist = [sb(f"hist{b}", [DIGIT, DIGIT, GT + 1]) for b in range(2)]
        begin = [sb(f"begin{b}", [DIGIT, DIGIT, GT + 1]) for b in range(2)]
        eq_out = sb("eq_out", [P, GT, P], BF16)
        prod = sb("prod", [P, GT, DIGIT])
        total = sb("total", [DIGIT, DIGIT])
        row_total = sb("row_total", [DIGIT, 1])
        row_base = sb("row_base", [DIGIT, 1])
        inclusive = sb("inclusive", [DIGIT, DIGIT])
        start0 = sb("start0", [DIGIT, DIGIT])
        start_i = [sb(f"start_i{n}", [DIGIT, DIGIT], I32) for n in range(2)]
        starts = sb("starts", [1, 2, LANES], I32)
        counts = sb("counts", [1, 2, NW], I32)
        longest = sb("longest", [1, 1], I32)

        row_st = [sb(f"row_st{b}", [P, GT, RE]) for b in range(2)]
        idx_st = [sb(f"idx_st{b}", [P, GT], U32) for b in range(2)]
        gx_idx = [sb(f"gx_idx{b}", [P, GT], U32) for b in range(2)]
        xb = [sb(f"xb{b}", [P, GT, D]) for b in range(2)]
        xs = [sb(f"xs{b}", [P, GT, D]) for b in range(2)]
        xc = [sb(f"xc{b}", [P, GT, D]) for b in range(2)]
        sq = sb("sq", [P, GT, D])
        stat = [sb(f"stat{b}", [P, 4, GT]) for b in range(2)]
        h = [sb(f"h{b}", [P, GT, D]) for b in range(2)]
        hT = [sb(f"hT{b}", [P, 4, P]) for b in range(2)]
        m_row = [sb(f"m_row{b}", [P, GT, RM]) for b in range(2)]
        mc = [sb(f"mc{b}", [P, 2, GT, RM]) for b in range(2)]
        near = [sb(f"near{b}", [P, 2, GT]) for b in range(2)]
        pick = [sb(f"pick{b}", [P, 2, GT, P]) for b in range(2)]
        fill = sb("fill", [ROWS - E >> 1, 2, RM])

        a_st = [sb(f"a_st{b}", [P, 4, KU]) for b in range(2)]
        s_st = [sb(f"s_st{b}", [P, 4, KU], BF16) for b in range(2)]
        aT = [sb(f"aT{b}", [KU, 512]) for b in range(2)]
        cnt = [sb(f"cnt{b}", [KU, 512]) for b in range(2)]
        inv = sb("inv", [KU, 512])
        uT = [sb(f"uT{b}", [KU, 512]) for b in range(2)]
        part = lambda b, n, k: pick[b][:, n, k:k + 4, :].rearrange("p k c -> p (k c)")
        hid = [part(b, 0, 0) for b in range(2)]
        run = [part(b, 0, 4)[0:KU, :] for b in range(2)]
        cut = [part(b, 1, 0)[0:KU, :] for b in range(2)]
        keep = [part(b, 1, 4)[0:KU, :] for b in range(2)]
        v_row = [sb(f"v_row{b}", [P, 4, RM]) for b in range(2)]

        ps = [ctx.enter_context(nc.psum_tensor(f"ps{n}", [P, 512], F32)) for n in range(8)]

        paced = {e: sem(f"paced_{e}") for e in ("sp", "pool", "act", "dve", "pe")}
        owns = {e: Own(sem(f"own_{e}"), paced[e] if e in ("pool", "act") else None) for e in ("pool", "act", "dve", "pe")}

        def own_waits(eng, name):
            owns[name].eng = eng
            return owns[name]

        RANK_SEMS = ("oh", "hist", "total", "row_base", "oh2", "done", "eq", "h", "t", "t_used",
                     "ohT", "w", "begin", "look")

        def ranking(name):
            return {s: sem(f"{name}_{s}") for s in RANK_SEMS}

        TRIPS = NG // 2
        h_ps = [ps[6][0:DIGIT, 256 * b:256 * b + 256].rearrange("p (k l) -> p k l", l=DIGIT) for b in range(2)]
        g_ps = [ps[7][:, 256 * b:256 * b + 256].rearrange("p (k l) -> p k l", l=DIGIT) for b in range(2)]

        def digits_of(dve, own, code):
            own(nc.vector.tensor_copy(code_f[:, :], code[:, :]))
            own(nc.vector.tensor_copy(code_h[:, :], code_f[:, :]))
            own(nc.vector.tensor_scalar(digit_i[:, :], code[:, :], 5, None, ALU.arith_shift_right))
            own(nc.vector.tensor_copy(hi_b[:, :], digit_i[:, :]))
            own(nc.vector.tensor_scalar(digit_i[:, :], code[:, :], DIGIT - 1, None, ALU.bitwise_and))
            own(nc.vector.tensor_copy(lo_b[:, :], digit_i[:, :]))

        def one_hots(g, b):
            grid = iota_d[:, :].unsqueeze(1).to_broadcast([P, GT, DIGIT])
            hi = hi_b[:, bass.ds(g * GT, GT)].unsqueeze(2).to_broadcast([P, GT, DIGIT])
            lo = lo_b[:, bass.ds(g * GT, GT)].unsqueeze(2).to_broadcast([P, GT, DIGIT])
            nc.vector.tensor_tensor(oh_hi[b][:, :, :], grid, hi, ALU.is_equal)
            nc.vector.tensor_copy(code_s[b][:, :], code_h[:, bass.ds(g * GT, GT)])
            return nc.vector.tensor_tensor(oh_lo[b][:, :, :], grid, lo, ALU.is_equal)

        def rank_dve(dve, own, r, code, out_address, start_row):
            digits_of(dve, own, code)
            own(nc.vector.memset(total[:, :], 0.0))
            with dve.Fori(0, TRIPS) as i:
                own.loop(i, 2)
                for b in range(2):
                    g = i * 2 + b
                    one_hots(g, b).then_inc(r["oh"], 1)
                    dve.wait_ge(r["hist"], g + 1)
                    own(nc.vector.tensor_tensor(total[:, :], total[:, :], h_ps[b][:, 0, :], ALU.add))
                own.end(TRIPS)
            own(nc.vector.tensor_reduce(row_total[:, :], total[:, :], AX, ALU.add))
            nc.vector.memset(inclusive[:, :], 0.0).then_inc(r["total"], 1)
            dve.wait_ge(r["row_base"], 1)
            own(nc.vector.tensor_copy(row_base[:, :], g_ps[0][0:DIGIT, 0, 0:1]))
            own(nc.vector.tensor_tensor_scan(inclusive[:, :], ones[0:DIGIT, 0:DIGIT], total[:, :],
                                             row_base[:, :], ALU.mult, ALU.add))
            own(nc.vector.tensor_tensor(start0[:, :], inclusive[:, :], total[:, :], ALU.subtract))
            if start_row is not None:
                nc.vector.tensor_copy(start_i[start_row][:, :], start0[:, :]).then_inc(starts_made[start_row], 1)
            own(nc.vector.tensor_copy(begin[1][:, :, GT], start0[:, :]))
            own(one_hots(0, 0))
            dve.sem_inc(r["oh2"], 1)
            with dve.Fori(0, TRIPS) as i:
                own.loop(i, 6)
                for b in range(2):
                    g = i * 2 + b
                    dve.wait_ge(r["eq"], g + 1)
                    for k in range(GT):
                        last = nc.vector.tensor_scalar(
                            eq_out[:, k, :], ps[2 * b + k // 4][:, P * (k % 4):P * (k % 4) + P],
                            code_f[:, bass.ds(g * GT + k, 1)], 0.0, ALU.is_equal, ALU.add,
                            accum_out=earlier[:, bass.ds(g * GT + k, 1)])
                    dve.wait_ge(r["w"], g + 1)
                    own(nc.vector.tensor_copy(hist[b][:, :, 0], begin[1 - b][:, :, GT]))
                    nc.vector.tensor_tensor_scan(begin[b][:, :, :].rearrange("p l k -> p (l k)"),
                                                 chain_mask[:, :, :].rearrange("p l k -> p (l k)"),
                                                 hist[b][:, :, :].rearrange("p l k -> p (l k)"),
                                                 0.0, ALU.mult, ALU.add).then_inc(r["begin"], 1)
                    dve.wait_ge(r["begin"], g + 1)
                    one_hots(g + 1, 1 - b).then_inc(r["oh2"], 1)
                    dve.wait_ge(r["look"], g + 1)
                    own(nc.vector.tensor_tensor(prod[:, :, :], g_ps[b], oh_lo[b][:, :, :], ALU.mult))
                    own(nc.vector.tensor_reduce(base_e[:, bass.ds(g * GT, GT)], prod[:, :, :], AX, ALU.add))
                    dve.sem_inc(r["done"], 1)
                own.end(TRIPS)
            own(nc.vector.tensor_tensor(base_e[:, :], base_e[:, :], earlier[:, :], ALU.add))
            own(nc.vector.tensor_copy(pos_i[:, :], base_e[:, :]))
            if out_address is idx_msg:
                own(nc.vector.tensor_copy(out_address[:, :], pos_i[:, :]))
                return
            own(nc.vector.tensor_scalar(pos_lo[:, :], pos_i[:, :], P - 1, None, ALU.bitwise_and))
            own(nc.vector.tensor_scalar(pos_i[:, :], pos_i[:, :], 7, None, ALU.arith_shift_right))
            own(nc.vector.tensor_scalar(pos_lo[:, :], pos_lo[:, :], float(NT), None, ALU.mult))
            own(nc.vector.tensor_tensor(out_address[:, :], pos_lo[:, :], pos_i[:, :], ALU.add))

        def rank_pe(pe, r):
            with pe.Fori(0, TRIPS) as i:
                for b in range(2):
                    g = i * 2 + b
                    pe.wait_ge(r["oh"], g + 1)
                    for k in range(GT):
                        last = nc.tensor.matmul(h_ps[b][:, 0, :], oh_hi[b][:, k, :], oh_lo[b][:, k, :],
                                                start=(k == 0), stop=(k == GT - 1))
                    last.then_inc(r["hist"], 1)
            pe.wait_ge(r["total"], 1)
            nc.tensor.matmul(g_ps[0][0:DIGIT, 0, 0:1], before[0:DIGIT, :], row_total[:, :],
                             start=True, stop=True).then_inc(r["row_base"], 1)
            with pe.Fori(0, TRIPS) as i:
                for b in range(2):
                    g = i * 2 + b
                    pe.wait_ge(r["oh2"], g + 1)
                    pe.wait_ge(r["done"], g + 1)
                    for half in range(2):
                        bank = ps[2 * b + half]
                        nc.tensor.matmul(bank[:, :].rearrange("p (k c) -> p k c", c=P), identh[:, :],
                                         later[:, :].unsqueeze(1).to_broadcast([P, 4, P]), start=True, stop=False)
                        for k in range(4):
                            last = nc.tensor.matmul(
                                bank[:, P * k:P * k + P],
                                code_s[b][:, 4 * half + k:4 * half + k + 1].to_broadcast([P, P]),
                                identh[:, :], start=False, stop=(k == 3))
                    last.then_inc(r["eq"], 1)
                    for k in range(GT):
                        last = nc.tensor.matmul(h_ps[b][:, k, :], oh_hi[b][:, k, :], oh_lo[b][:, k, :],
                                                start=True, stop=True)
                    last.then_inc(r["h"], 1)
                    pe.wait_ge(r["t_used"], g + 1)
                    for k in range(GT):
                        last = nc.tensor.matmul(ps[4 + k // 4][0:DIGIT, P * (k % 4):P * (k % 4) + P],
                                                oh_hi[b][:, k, :], identb[:, :], start=True, stop=True)
                    last.then_inc(r["t"], 1)
                    pe.wait_ge(r["ohT"], g + 1)
                    pe.wait_ge(r["begin"], g + 1)
                    for k in range(GT):
                        last = nc.tensor.matmul(g_ps[b][:, k, :], ohT[b][:, k, :], begin[b][:, :, k],
                                                start=True, stop=True)
                    last.then_inc(r["look"], 1)

        def rank_act(act, own, r):
            act.sem_inc(r["done"], 2)
            act.sem_inc(r["t_used"], 1)
            with act.Fori(0, TRIPS) as i:
                own.loop(i, 2)
                for b in range(2):
                    g = i * 2 + b
                    act.wait_ge(r["h"], g + 1)
                    act.sem_inc(paced["act"], 1)
                    act.wait_ge(r["done"], g + 1)
                    act.sem_inc(paced["act"], 1)
                    nc.scalar.activation(hist[b][:, :, 1:GT + 1], h_ps[b].rearrange("p k l -> p l k"),
                                         ACT.Copy).then_inc(r["w"], 1)
                    act.wait_ge(r["t"], g + 1)
                    act.sem_inc(paced["act"], 1)
                    nc.scalar.activation(ohT[b][:, 0:4, :], ps[4][0:DIGIT, :].rearrange("p (k c) -> p k c", c=P), ACT.Copy)
                    own(nc.scalar.activation(ohT[b][:, 4:8, :], ps[5][0:DIGIT, :].rearrange("p (k c) -> p k c", c=P), ACT.Copy))
                    act.sem_inc(r["ohT"], 1)
                    act.sem_inc(r["t_used"], 1)
                own.end(TRIPS)

        def prime(eng, sems):
            for n, s in enumerate(sems):
                eng.dma_start(spare[n:n + 1, :], eps_t[0:1, 0:1]).then_inc(s, 16)
                eng.wait_ge(s, 16)

        def scatter_rows(pool, own, index, row_tile, width, table, stage, staged, sent):
            flat = table

            def send(b, k, parts):
                nc.gpsimd.indirect_dma_start(
                    out=flat, out_offset=bass.IndirectOffsetOnAxis(ap=idx_st[b][0:parts, k:k + 1], axis=0),
                    in_=stage[b][0:parts, k, :], in_offset=None).then_inc(sent[b], 16)

            def put(g, b):
                nc.gpsimd.tensor_copy(idx_st[b][:, :], index[:, bass.ds(g * GT, GT)])
                own(nc.gpsimd.tensor_copy(stage[b][:, :, :], row_tile[:, bass.ds(g * GT, GT), :]))

            prime(pool, sent)
            with pool.Fori(0, FG // 2) as i:
                own.loop(i, 2)
                for b in range(2):
                    pool.wait_ge(sent[b], i * (16 * GT) + 16)
                    pool.sem_inc(paced["pool"], 1)
                    put(i * 2 + b, b)
                    for k in range(GT):
                        send(b, k, P)
                own.end(FG // 2)
            pool.wait_ge(sent[0], FG // 2 * 16 * GT + 16)
            put(FG, 0)
            for k in range(RT):
                send(0, k, P)
            send(0, RT, TAIL)
            pool.wait_ge(sent[0], FG // 2 * 16 * GT + 16 + 16 * (RT + 1))
            pool.wait_ge(sent[1], FG // 2 * 16 * GT + 16)

        ln_sems = {s: sem(f"ln_{s}") for s in ("centred", "squared", "summed", "root")}
        ln_count = [0]

        def norm_dve(dve, own, b, step, base, x_in, scale):
            s0, mean, rs = stat[b][:, 0, :], stat[b][:, 1, :], stat[b][:, 2, :]
            wide = lambda a: a.unsqueeze(2).to_broadcast([P, GT, D])
            own(nc.vector.tensor_reduce(s0, x_in, AX, ALU.add))
            own(nc.vector.tensor_scalar(mean, s0, 1.0 / D, None, ALU.mult))
            nc.vector.tensor_tensor(xc[b][:, :, :], x_in, wide(mean), ALU.subtract).then_inc(ln_sems["centred"], 1)
            dve.wait_ge(ln_sems["squared"], step + (base + 1))
            nc.vector.tensor_reduce(stat[b][:, 3, :], sq[:, :, :], AX, ALU.add).then_inc(ln_sems["summed"], 1)
            dve.wait_ge(ln_sems["root"], step + (base + 1))
            own(nc.vector.reciprocal(rs, stat[b][:, 3, :]))
            if scale is not None:
                own(nc.vector.tensor_tensor(rs, rs, scale, ALU.mult))
            return nc.vector.scalar_tensor_tensor(h[b][:, :, :], xc[b][:, :, :], 0.0, wide(rs), ALU.max, ALU.mult)

        def norm_act(act, b, step, base):
            act.wait_ge(ln_sems["centred"], step + (base + 1))
            act.sem_inc(paced["act"], 1)
            nc.scalar.activation(sq[:, :, :], xc[b][:, :, :], ACT.Square).then_inc(ln_sems["squared"], 1)
            act.wait_ge(ln_sems["summed"], step + (base + 1))
            act.sem_inc(paced["act"], 1)
            nc.scalar.activation(stat[b][:, 3, :], stat[b][:, 3, :], ACT.Sqrt, bias=eps_t[:, :],
                                 scale=1.0 / D).then_inc(ln_sems["root"], 1)

        loaded = {n: sem(f"loaded_{n}") for n in ("weights", "edges", "attr", "lane", "node", "starts", "shift")}
        made = {n: sem(f"made_{n}") for n in ("const", "pads", "wsT_ps", "wsT", "c0_ps", "hbias", "c0",
                                              "node_copy", "sign", "codes")}
        starts_made = [sem(f"starts_made{n}") for n in range(2)]
        starts_out = sem("starts_out")
        filled = sem("filled")
        sent_lane = [sem(f"sent_lane{b}") for b in range(2)]
        sent_node = [sem(f"sent_node{b}") for b in range(2)]
        r_lane, r_dst, r_node = ranking("lane"), ranking("dst"), ranking("node")

        def edge_load(eng, tile, source):
            eng.dma_start(tile[:, 0:FT], source[0:FT * P].rearrange("(p t) -> p t", p=P)).then_inc(loaded["edges"], 16)
            eng.dma_start(tile[0:TAIL, FT:FT + 1],
                          source[FT * P:E].rearrange("(p o) -> p o", o=1)).then_inc(loaded["edges"], 16)

        with nc.Block() as block:
            @block.sync
            def _(sp):
                sp.wait_ge(made["pads"], 1)
                edge_load(sp, src_i, src)
                edge_load(sp, dst_i, dst)
                edge_load(sp, ew, weight)
                sp.dma_start(wn2[0:D, 0:D], w_neigh).then_inc(loaded["weights"], 16)
                sp.dma_start(wn2[D:P, D:P], w_neigh).then_inc(loaded["weights"], 16)
                for n in range(2):
                    sp.dma_start(ws_raw[:, n, :], w_self).then_inc(loaded["weights"], 16)
                sp.dma_start(w1_sb[:, :], w1[0:KU, :]).then_inc(loaded["weights"], 16)
                sp.dma_start(w1u[:, :], w1[KU, :].rearrange("(p o) -> p o", o=1)).then_inc(loaded["weights"], 16)
                sp.dma_start(b1c[:, :], b1.rearrange("(p o) -> p o", o=1)).then_inc(loaded["weights"], 16)
                sp.dma_start(u0[:, :], u[0:1, :].to_broadcast([P, 1])).then_inc(loaded["weights"], 16)
                sp.dma_start(w2_sb[:, :], w2).then_inc(loaded["weights"], 16)
                sp.dma_start(b2b[:, :], b2.unsqueeze(0).to_broadcast([P, D])).then_inc(loaded["weights"], 16)
                sp.dma_start(bnb[:, :], b_neigh.unsqueeze(0).to_broadcast([P, D])).then_inc(loaded["weights"], 16)
                sp.dma_start(rows[:, 0:FT, 0:DE],
                             attr[0:FT * P, :].rearrange("(p t) c -> p t c", p=P)).then_inc(loaded["attr"], 16)
                sp.dma_start(rows[0:TAIL, FT, 0:DE], attr[FT * P:E, :]).then_inc(loaded["attr"], 16)
                for table in (message, mlp_row):
                    sp.dma_start(table[E:ROWS, :].rearrange("(p a) c -> p a c", a=2), fill[:, :, :]).then_inc(filled, 16)
                sp.wait_ge(loaded["weights"], 16 * 11)
                sp.wait_ge(loaded["edges"], 16 * 6)
                sp.wait_ge(loaded["attr"], 32)
                sp.wait_ge(filled, 32)

            @block.gpsimd
            def _(pool):
                own = own_waits(pool, "pool")
                nc.gpsimd.memset(src_i[:, :], -1)
                nc.gpsimd.memset(dst_i[:, :], -1)
                nc.gpsimd.memset(code_i[:, :], -1)
                nc.gpsimd.memset(ew[:, :], 0.0)
                nc.gpsimd.memset(wn2[:, :], 0.0)
                nc.gpsimd.memset(wsT2[:, :], 0.0)
                nc.gpsimd.memset(fill[:, :, :], 0.0)
                own(nc.gpsimd.memset(rows[:, :, :], 0.0))
                own(nc.gpsimd.memset(fill[:, :, D:RM], -1.0))
                pool.sem_inc(made["pads"], 1)
                for t, one, tri in ((ident, 1.0, False), (identb, 1.0, False), (identh, 1.0, False), (later, 2048.0, True)):
                    own(nc.gpsimd.memset(t[:, :], 2048.0 if tri else 0.0))
                    if tri:
                        own(nc.gpsimd.affine_select(out=t[:, :], in_=t[:, :], compare_op=ALU.is_ge, fill=0.0,
                                                    base=0, pattern=[[1, P]], channel_multiplier=-1))
                    else:
                        own(nc.gpsimd.affine_select(out=t[:, :], in_=t[:, :], compare_op=ALU.not_equal, fill=1.0,
                                                    base=0, pattern=[[-1, P]], channel_multiplier=1))
                own(nc.gpsimd.memset(before[:, :], 1.0))
                own(nc.gpsimd.affine_select(out=before[:, :], in_=before[:, :], compare_op=ALU.is_gt, fill=0.0,
                                            base=0, pattern=[[1, DIGIT]], channel_multiplier=-1))
                own(nc.gpsimd.iota(iota_d[:, :], [[1, DIGIT]], base=0, channel_multiplier=0,
                                   allow_small_or_imprecise_dtypes=True))
                own(nc.gpsimd.iota(iota_n[:, :], [[1, P]], base=0, channel_multiplier=0,
                                   allow_small_or_imprecise_dtypes=True))
                own(nc.gpsimd.iota(first_of[:, :], [[P, NW + GT]], base=0, channel_multiplier=0,
                                   allow_small_or_imprecise_dtypes=True))
                own(nc.gpsimd.memset(chain_mask[:, :, :], 1.0))
                own(nc.gpsimd.memset(chain_mask[:, :, 0:1], 0.0))
                own(nc.gpsimd.memset(eps_t[:, :], EPS))
                own(nc.gpsimd.memset(ones[:, :], 1.0))
                pool.sem_inc(made["const"], 1)

            @block.vector
            def _(dve):
                own = own_waits(dve, "dve")
                dve.wait_ge(made["const"], 1)
                dve.wait_ge(made["pads"], 1)
                dve.wait_ge(loaded["weights"], 16 * 11)
                own(nc.vector.tensor_tensor(hbias[:, :], w1u[:, :], u0[:, :], ALU.mult))
                own(nc.vector.tensor_tensor(hbias[:, :], hbias[:, :], b1c[:, :], ALU.add))
                own(nc.vector.tensor_scalar(hrelu[:, :], hbias[:, :], 0.0, None, ALU.max))
                own(nc.vector.tensor_copy(hrelu_b[:, :], hrelu[:, :].to_broadcast([P, P])))
                dve.sem_inc(made["hbias"], 1)
                dve.wait_ge(made["wsT_ps"], 1)
                for half in (0, D):
                    own(nc.vector.tensor_copy(wsT2[half:half + D, half:half + D], ps[0][half:half + D, 0:D]))
                dve.wait_ge(made["c0_ps"], 1)
                own(nc.vector.tensor_copy(c0b[:, :], ps[1][:, 0:D]))
                own(nc.vector.tensor_tensor(biasb[:, :], b2b[:, :], bnb[:, :], ALU.add))
                own(nc.vector.tensor_tensor(biasb[:, :], biasb[:, :], c0b[:, :], ALU.add))
                dve.sem_inc(made["c0"], 1)
                dve.wait_ge(loaded["edges"], 16 * 6)
                own(nc.vector.tensor_copy(src_f[:, :], src_i[:, 0:NT]))
                own(nc.vector.tensor_copy(dst_f[:, :], dst_i[:, 0:NT]))
                own(nc.vector.tensor_scalar(idx_src[:, :], src_i[:, 0:NT], 0.0, None, ALU.max))
                dve.wait_ge(loaded["attr"], 32)
                own(nc.vector.tensor_copy(rows[:, :, DE], src_f[:, :]))
                own(nc.vector.tensor_scalar(code_i[:, 0:FT], src_i[:, 0:FT], P - 1, None, ALU.bitwise_and))
                own(nc.vector.tensor_scalar(code_i[0:TAIL, FT:FT + 1], src_i[0:TAIL, FT:FT + 1], P - 1, None,
                                            ALU.bitwise_and))
                rank_dve(dve, own, r_lane, code_i, idx_lane, None)

            @block.tensor
            def _(pe):
                own = own_waits(pe, "pe")
                pe.wait_ge(made["const"], 1)
                pe.wait_ge(loaded["weights"], 16 * 11)
                nc.tensor.matmul(ps[0][:, 0:D], ws_raw[:, :, :].rearrange("p a c -> p (a c)"), ident[0:D, 0:D],
                                 start=True, stop=True).then_inc(made["wsT_ps"], 1)
                pe.wait_ge(made["hbias"], 1)
                nc.tensor.matmul(ps[1][:, 0:D], hrelu_b[:, :], w2_sb[:, :], start=True, stop=True).then_inc(made["c0_ps"], 1)
                pe.wait_ge(made["c0"], 1)
                rank_pe(pe, r_lane)

            @block.scalar
            def _(act):
                own = own_waits(act, "act")
                rank_act(act, own, r_lane)

        with nc.Block() as block:
            @block.gpsimd
            def _(pool):
                own = own_waits(pool, "pool")
                scatter_rows(pool, own, idx_lane, rows, RE, by_lane.rearrange("p t c -> (p t) c"), row_st, None, sent_lane)

            @block.vector
            def _(dve):
                own = own_waits(dve, "dve")
                own(nc.vector.tensor_scalar(code_i[:, :], dst_i[:, :], 7, None, ALU.arith_shift_right))
                rank_dve(dve, own, r_dst, code_i, idx_msg, 0)

            @block.tensor
            def _(pe):
                own = own_waits(pe, "pe")
                rank_pe(pe, r_dst)

            @block.scalar
            def _(act):
                own = own_waits(act, "act")
                rank_act(act, own, r_dst)

        gathered = [sem(f"gathered{b}") for b in range(2)]
        msg_sent = [sem(f"msg_sent{b}") for b in range(2)]
        msg = {n: sem(f"msg_{n}") for n in ("x_used", "h", "hT_ps", "hT", "m_ps", "row")}
        MG = FG + 1
        ln_step0 = 0
        with nc.Block() as block:
            @block.gpsimd
            def _(pool):
                own = own_waits(pool, "pool")

                def gather(b, k, parts):
                    nc.gpsimd.indirect_dma_start(
                        out=xb[b][0:parts, k, :], out_offset=None, in_=x,
                        in_offset=bass.IndirectOffsetOnAxis(ap=gx_idx[b][0:parts, k:k + 1], axis=0)).then_inc(gathered[b], 16)

                def put(b, k, parts):
                    nc.gpsimd.indirect_dma_start(
                        out=message, out_offset=bass.IndirectOffsetOnAxis(ap=idx_st[b][0:parts, k:k + 1], axis=0),
                        in_=m_row[b][0:parts, k, :], in_offset=None).then_inc(msg_sent[b], 16)

                def stage_gather(g, b):
                    own(nc.gpsimd.tensor_copy(gx_idx[b][:, :], idx_src[:, bass.ds(g * GT, GT)]))

                prime(pool, msg_sent)
                pool.sem_inc(msg["x_used"], 1)
                stage_gather(0, 0)
                for k in range(GT):
                    gather(0, k, P)

                def step(g, b):
                    pool.wait_ge(msg["x_used"], g + 1)
                    pool.sem_inc(paced["pool"], 1)
                    stage_gather(g + 1, 1 - b)
                    for k in range(GT):
                        gather(1 - b, k, P)
                    pool.wait_ge(msg["row"], g + 1)
                    pool.sem_inc(paced["pool"], 1)
                    own(nc.gpsimd.tensor_copy(idx_st[b][:, :], idx_msg[:, bass.ds(g * GT, GT)]))
                    for k in range(GT):
                        put(b, k, P)

                with pool.Fori(0, FG // 2) as i:
                    own.loop(i, 4)
                    for b in range(2):
                        step(i * 2 + b, b)
                    own.end(FG // 2)
                pool.wait_ge(msg["row"], MG)
                own(nc.gpsimd.tensor_copy(idx_st[0][:, :], idx_msg[:, FG * GT:FG * GT + GT]))
                for k in range(RT):
                    put(0, k, P)
                put(0, RT, TAIL)
                pool.wait_ge(msg_sent[0], FG // 2 * 16 * GT + 16 + 16 * (RT + 1))
                pool.wait_ge(msg_sent[1], FG // 2 * 16 * GT + 16)
                pool.wait_ge(made["codes"], 1)
                scatter_rows(pool, own, idx_node, rows, RE, by_node.rearrange("p t c -> (p t) c"), row_st, None, sent_node)

            @block.sync
            def _(sp):
                sp.dma_start(rows[:, 0:FT, :], by_lane[:, 0:FT, :]).then_inc(loaded["lane"], 16)
                sp.dma_start(rows[0:TAIL, FT, :], by_lane[0:TAIL, FT, :]).then_inc(loaded["lane"], 16)
                sp.dma_start(starts_d[0, :].rearrange("(p l) -> p l", p=DIGIT), start_i[0][:, :]).then_inc(starts_out, 16)
                sp.wait_ge(starts_out, 16)
                sp.wait_ge(loaded["lane"], 32)

            @block.vector
            def _(dve):
                own = own_waits(dve, "dve")

                def step(g, b, i):
                    dve.wait_ge(gathered[b], (i + 1) * (16 * GT))
                    norm_dve(dve, own, b, g, 0, xb[b][:, :, :], ew[:, bass.ds(g * GT, GT)]).then_inc(msg["h"], 1)
                    dve.sem_inc(msg["x_used"], 1)
                    dve.wait_ge(msg["m_ps"], g + 1)
                    dve.wait_ge(msg_sent[b], i * (16 * GT) + 16)
                    nc.vector.tensor_copy(m_row[b][:, :, D], dst_f[:, bass.ds(g * GT, GT)])
                    own(nc.vector.tensor_copy(m_row[b][:, :, 0:D], ps[1 + b][:, :].rearrange("p (k c) -> p k c", c=D)))
                    dve.sem_inc(msg["row"], 1)

                with dve.Fori(0, FG // 2) as i:
                    own.loop(i, 10)
                    for b in range(2):
                        step(i * 2 + b, b, i)
                    own.end(FG // 2)
                step(FG, 0, FG // 2)
                dve.wait_ge(loaded["lane"], 32)
                own(nc.vector.tensor_copy(code_i[:, 0:NT], rows[:, :, DE]))
                own(nc.vector.tensor_scalar(code_i[:, :], code_i[:, :], 7, None, ALU.arith_shift_right))
                rank_dve(dve, own, r_node, code_i, idx_node, 1)
                dve.sem_inc(made["codes"], 1)

            @block.tensor
            def _(pe):
                own = own_waits(pe, "pe")

                def step(g, b):
                    pe.wait_ge(msg["h"], g + 1)
                    for k in range(4):
                        last = nc.tensor.transpose(ps[0][:, P * k:P * k + P],
                                                   h[b][:, 2 * k:2 * k + 2, :].rearrange("p a c -> p (a c)"), ident[:, :])
                    last.then_inc(msg["hT_ps"], 1)
                    pe.wait_ge(msg["hT"], g + 1)
                    for k in range(4):
                        last = nc.tensor.matmul(ps[1 + b][:, P * k:P * k + P], hT[b][:, k, :], wn2[:, :],
                                                start=True, stop=True)
                    last.then_inc(msg["m_ps"], 1)

                with pe.Fori(0, FG // 2) as i:
                    for b in range(2):
                        step(i * 2 + b, b)
                step(FG, 0)
                rank_pe(pe, r_node)

            @block.scalar
            def _(act):
                own = own_waits(act, "act")

                def step(g, b):
                    norm_act(act, b, g, 0)
                    act.wait_ge(msg["hT_ps"], g + 1)
                    act.sem_inc(paced["act"], 1)
                    nc.scalar.activation(hT[b][:, :, :], ps[0][:, :].rearrange("p (k c) -> p k c", c=P),
                                         ACT.Copy).then_inc(msg["hT"], 1)

                with act.Fori(0, FG // 2) as i:
                    for b in range(2):
                        step(i * 2 + b, b)
                step(FG, 0)
                rank_act(act, own, r_node)

        QT = 4
        QG = -(-(FT + 1) // QT)
        QF = QG - 1
        QR = FT - QF * QT
        q = {n: sem(f"q_{n}") for n in ("staged", "a_ps", "a_used", "s_used", "aT", "flags", "run", "u", "h_ps", "hid", "v_ps", "sum")}
        v_sent = [sem(f"v_sent{b}") for b in range(2)]
        assert QG % 2 == 0
        with nc.Block() as block:
            @block.sync
            def _(sp):
                sp.dma_start(rows[:, 0:FT, :], by_node[:, 0:FT, :]).then_inc(loaded["node"], 16)
                sp.dma_start(rows[0:TAIL, FT, :], by_node[0:TAIL, FT, :]).then_inc(loaded["node"], 16)
                sp.dma_start(starts_d[1, :].rearrange("(p l) -> p l", p=DIGIT), start_i[1][:, :]).then_inc(starts_out, 16)
                sp.wait_ge(made["node_copy"], 1)
                sp.dma_start(near_f[1:P, :], node_f[0:P - 1, :]).then_inc(loaded["shift"], 16)
                sp.dma_start(near_f[0:1, 1:NT], node_f[P - 1:P, 0:NT - 1]).then_inc(loaded["shift"], 16)
                sp.wait_ge(made["sign"], 1)
                sp.dma_start(near_f[0:P - 1, :], node_f[1:P, :]).then_inc(loaded["shift"], 16)
                sp.dma_start(near_f[P - 1:P, 0:NT - 1], node_f[0:1, 1:NT]).then_inc(loaded["shift"], 16)
                sp.wait_ge(starts_out, 32)
                sp.dma_start(starts[:, :, :], starts_d.unsqueeze(0)).then_inc(loaded["starts"], 16)

                def store(g, b):
                    sp.wait_ge(q["sum"], g + 1)
                    sp.sem_inc(paced["sp"], 1)
                    sp.dma_start(mlp_row[bass.ds(g * (QT * P), QT * P), :].rearrange("(t p) c -> p t c", p=P),
                                 v_row[b][:, :, :]).then_inc(v_sent[b], 16)

                prime(sp, v_sent)
                with sp.Fori(0, QF // 2) as i:
                    for b in range(2):
                        store(i * 2 + b, b)
                store(QF - 1, 0)
                sp.wait_ge(q["sum"], QG)
                sp.dma_start(mlp_row[QF * QT * P:FT * P, :].rearrange("(t p) c -> p t c", p=P),
                             v_row[1][:, 0:QR, :]).then_inc(v_sent[1], 16)
                sp.dma_start(mlp_row[FT * P:E, :], v_row[1][0:TAIL, QR, :]).then_inc(v_sent[1], 16)
                sp.wait_ge(v_sent[0], 16 * (QG // 2 + 1))
                sp.wait_ge(v_sent[1], 16 * (QG // 2 + 2))
                sp.wait_ge(loaded["starts"], 16)

            @block.gpsimd
            def _(pool):
                own = own_waits(pool, "pool")
                pool.wait_ge(made["codes"], 2)
                with pool.Fori(0, QG // 2) as i:
                    own.loop(i, 2)
                    for b in range(2):
                        g = i * 2 + b
                        pool.wait_ge(q["a_used"], g + 1)
                        pool.sem_inc(paced["pool"], 1)
                        nc.gpsimd.tensor_copy(
                            s_st[b][:, :, :], sign_b[:, bass.ds(g * QT, QT)].unsqueeze(2).to_broadcast([P, QT, KU]))
                        own(nc.gpsimd.tensor_copy(
                            a_st[b][:, :, :].rearrange("p t (n c) -> p t n c", n=3),
                            rows[:, bass.ds(g * QT, QT), 0:DE].unsqueeze(2).to_broadcast([P, QT, 3, DE])))
                        pool.sem_inc(q["staged"], 1)
                    own.end(QG // 2)

            @block.vector
            def _(dve):
                own = own_waits(dve, "dve")
                own(nc.vector.memset(near_f[0:1, 0:1], -3.0))
                dve.wait_ge(loaded["node"], 32)
                own(nc.vector.tensor_copy(node_f[:, :], rows[:, :, DE]))
                dve.sem_inc(made["node_copy"], 1)
                for t in (run[1], cnt[1], uT[1]):
                    own(nc.vector.memset(t[:, :], 0.0))
                dve.wait_ge(loaded["shift"], 32)
                own(nc.vector.tensor_tensor(near_f[:, :], near_f[:, :], node_f[:, :], ALU.is_equal))
                own(nc.vector.tensor_scalar(sign_b[:, :], near_f[:, :], 2.0, -1.0, ALU.mult, ALU.add))
                own(nc.vector.memset(near_f[:, :], -3.0))
                dve.sem_inc(made["sign"], 1)
                dve.wait_ge(loaded["shift"], 64)
                own(nc.vector.tensor_tensor(near_f[:, :], near_f[:, :], node_f[:, :], ALU.is_equal))
                own(nc.vector.tensor_scalar(key_v[:, :], node_f[:, :], 1.0, None, ALU.add))
                own(nc.vector.tensor_tensor(near_f[:, :], near_f[:, :], key_v[:, :], ALU.mult))
                own(nc.vector.tensor_tensor(key_v[:, :], node_f[:, :], near_f[:, :], ALU.subtract))
                dve.sem_inc(made["codes"], 1)
                with dve.Fori(0, QG // 2) as i:
                    own.loop(i, 12)
                    for b in range(2):
                        g = i * 2 + b
                        dve.wait_ge(q["flags"], g + 1)
                        c = 1 - b
                        own(nc.vector.tensor_tensor_scan(run[b][:, :], keep[b][:, :], aT[b][:, :], run[c][:, 511:512],
                                                         ALU.mult, ALU.add))
                        dve.sem_inc(q["run"], 1)
                        own(nc.vector.tensor_tensor_scan(cnt[b][2 * DE:KU, :], keep[b][2 * DE:KU, :], ones[2 * DE:KU, :],
                                                         cnt[c][2 * DE:KU, 511:512], ALU.mult, ALU.add))
                        own(nc.vector.reciprocal(inv[2 * DE:KU, :], cnt[b][2 * DE:KU, :]))
                        own(nc.vector.tensor_tensor_scan(uT[b][DE:2 * DE, :], cut[b][DE:2 * DE, :], aT[b][DE:2 * DE, :],
                                                         uT[c][DE:2 * DE, 511:512], ALU.min, ALU.max))
                        own(nc.vector.tensor_tensor(uT[b][2 * DE:KU, :], run[b][2 * DE:KU, :], inv[2 * DE:KU, :], ALU.mult))
                        dve.sem_inc(q["u"], 1)
                        dve.wait_ge(q["v_ps"], g + 1)
                        dve.wait_ge(v_sent[b], (i + 1) * 16)
                        nc.vector.tensor_copy(v_row[b][:, :, D], key_v[:, bass.ds(g * QT, QT)])
                        own(nc.vector.tensor_tensor(v_row[b][:, :, 0:D], ps[5 + b][:, 0:QT * D].rearrange("p (k c) -> p k c", c=D),
                                                    c0b[:, :].unsqueeze(1).to_broadcast([P, QT, D]), ALU.subtract))
                        dve.sem_inc(q["sum"], 1)
                    own.end(QG // 2)

            @block.tensor
            def _(pe):
                own = own_waits(pe, "pe")

                with pe.Fori(0, QG // 2) as i:
                    for b in range(2):
                        g = i * 2 + b
                        pe.wait_ge(q["staged"], g + 1)
                        pe.wait_ge(q["s_used"], g + 1)
                        for k in range(QT):
                            nc.tensor.matmul(ps[0][0:KU, P * k:P * k + P], a_st[b][:, k, :], ident[:, :], start=True, stop=True)
                        for k in range(QT):
                            last = nc.tensor.matmul(ps[1][0:KU, P * k:P * k + P], s_st[b][:, k, :], identb[:, :],
                                                    start=True, stop=True)
                        last.then_inc(q["a_ps"], 1)
                        pe.wait_ge(q["u"], g + 1)
                        pe.wait_ge(q["aT"], g + 1)
                        nc.tensor.matmul(ps[2 + b][:, :], w1_sb[:, :], uT[b][:, :], start=True, stop=True).then_inc(q["h_ps"], 1)
                        pe.wait_ge(q["hid"], g + 1)
                        for k in range(QT):
                            last = nc.tensor.matmul(ps[5 + b][:, D * k:D * k + D], hid[b][:, P * k:P * k + P], w2_sb[:, :],
                                                    start=True, stop=True)
                        last.then_inc(q["v_ps"], 1)

            @block.scalar
            def _(act):
                own = own_waits(act, "act")
                act.sem_inc(q["a_used"], 2)
                act.sem_inc(q["s_used"], 1)
                with act.Fori(0, QG // 2) as i:
                    own.loop(i, 4)
                    for b in range(2):
                        g = i * 2 + b
                        act.wait_ge(q["a_ps"], g + 1)
                        act.sem_inc(paced["act"], 1)
                        nc.scalar.activation(aT[b][:, :], ps[0][0:KU, :], ACT.Copy)
                        nc.scalar.activation(keep[b][:, :], ps[1][0:KU, :], ACT.Relu)
                        own(nc.scalar.activation(cut[b][:, :], ps[1][0:KU, :], ACT.Copy, scale=FLT_MAX))
                        act.sem_inc(q["flags"], 1)
                        act.sem_inc(q["s_used"], 1)
                        act.sem_inc(q["a_used"], 1)
                        act.wait_ge(q["run"], g + 1)
                        act.sem_inc(paced["act"], 1)
                        own(nc.scalar.activation(uT[b][0:DE, :], run[b][0:DE, :], ACT.Copy))
                        act.sem_inc(q["aT"], 1)
                        act.wait_ge(q["h_ps"], g + 1)
                        act.sem_inc(paced["act"], 1)
                        nc.scalar.activation(hid[b][:, :], ps[2 + b][:, :], ACT.Relu, bias=hbias[:, :]).then_inc(q["hid"], 1)
                    own.end(QG // 2)

        WG = -(-NW // GT)
        WF = (N // P) // GT
        WR = N // P - WF * GT
        assert WG % 2 == 0 and WF == WG - 1
        win = {n: sem(f"win_{n}") for n in ("x_used", "rows_used", "xs", "pick", "h", "hT_ps", "hT", "o_ps", "y")}
        x_in = [sem(f"x_in{b}") for b in range(2)]
        rows_in = [sem(f"rows_in{b}") for b in range(2)]
        y_out = [sem(f"y_out{b}") for b in range(2)]
        tables = (message, mlp_row)
        with nc.Block() as block:
            @block.sync
            def _(sp):
                sp.sem_inc(win["x_used"], 2)
                sp.sem_inc(win["rows_used"], 2)

                def step(g, b, last=False):
                    sp.wait_ge(win["x_used"], g + 1)
                    sp.sem_inc(paced["sp"], 1)
                    if last:
                        sp.dma_start(xb[b][:, 0:WR, :], x[WF * GT * P:(WF * GT + WR) * P, :].rearrange(
                            "(k p) c -> p k c", p=P)).then_inc(x_in[b], 16)
                        sp.dma_start(xb[b][0:N % P, WR, :], x[N - N % P:N, :]).then_inc(x_in[b], 16)
                    else:
                        sp.dma_start(xb[b][:, :, :], x[bass.ds(g * (GT * P), GT * P), :].rearrange(
                            "(k p) c -> p k c", p=P)).then_inc(x_in[b], 16)
                    sp.wait_ge(win["rows_used"], g + 1)
                    sp.sem_inc(paced["sp"], 1)
                    for n in range(2):
                        for k in range(GT):
                            at = sp.value_load(starts[0:1, n, bass.ds(g * GT + k, 1)], min_val=0, max_val=E)
                            sp.dma_start(mc[b][:, n, k, :], tables[n][bass.ds(at, P), :]).then_inc(rows_in[b], 16)

                with sp.Fori(0, WG // 2 - 1) as i:
                    for b in range(2):
                        step(i * 2 + b, b)
                step(WG - 2, 0)
                step(WG - 1, 1, last=True)

            @block.gpsimd
            def _(pool):
                own = own_waits(pool, "pool")

                def step(g, b, i, more=0):
                    pool.wait_ge(x_in[b], (i + 1) * 16 + more)
                    pool.sem_inc(paced["pool"], 1)
                    pool.wait_ge(y_out[b], (i + 1) * 16)
                    pool.sem_inc(paced["pool"], 1)
                    own(nc.gpsimd.tensor_tensor(xs[b][:, :, :], xb[b][:, :, :],
                                                biasb[:, :].unsqueeze(1).to_broadcast([P, GT, D]), ALU.add))
                    pool.sem_inc(win["xs"], 1)
                    pool.wait_ge(win["h"], g + 1)
                    pool.sem_inc(win["x_used"], 1)

                with pool.Fori(0, WG // 2 - 1) as i:
                    own.loop(i, 2)
                    for b in range(2):
                        step(i * 2 + b, b, i)
                    own.end(WG // 2 - 1)
                step(WG - 2, 0, WG // 2 - 1)
                step(WG - 1, 1, WG // 2 - 1, 16)

            @block.vector
            def _(dve):
                own = own_waits(dve, "dve")

                def step(g, b, i, more=0):
                    dve.wait_ge(rows_in[b], (i + 1) * (16 * 2 * GT))
                    own(nc.vector.tensor_tensor(near[b][:, :, :], mc[b][:, :, :, D],
                                                first_of[:, bass.ds(g * GT, GT)].unsqueeze(1).to_broadcast([P, 2, GT]),
                                                ALU.subtract))
                    nc.vector.tensor_tensor(pick[b][:, :, :, :].rearrange("p n k c -> p (n k) c"),
                                            iota_n[:, :].unsqueeze(1).to_broadcast([P, 2 * GT, P]),
                                            near[b][:, :, :].rearrange("p n k -> p (n k)").unsqueeze(2).to_broadcast([P, 2 * GT, P]),
                                            ALU.is_equal).then_inc(win["pick"], 1)
                    dve.wait_ge(x_in[b], (i + 1) * 16 + more)
                    norm_dve(dve, own, b, g, MG, xb[b][:, :, :], None).then_inc(win["h"], 1)
                    dve.wait_ge(win["o_ps"], g + 1)
                    dve.sem_inc(win["rows_used"], 1)
                    dve.wait_ge(win["xs"], g + 1)
                    own(nc.vector.tensor_tensor(xs[b][:, :, :], xs[b][:, :, :],
                                                ps[1 + b][:, :].rearrange("p (k c) -> p k c", c=D), ALU.add))
                    dve.sem_inc(win["y"], 1)

                with dve.Fori(0, WG // 2 - 1) as i:
                    own.loop(i, 10)
                    for b in range(2):
                        step(i * 2 + b, b, i)
                    own.end(WG // 2 - 1)
                step(WG - 2, 0, WG // 2 - 1)
                step(WG - 1, 1, WG // 2 - 1, 16)

            @block.tensor
            def _(pe):
                own = own_waits(pe, "pe")

                def step(g, b):
                    pe.wait_ge(win["h"], g + 1)
                    for k in range(4):
                        last = nc.tensor.transpose(ps[0][:, P * k:P * k + P],
                                                   h[b][:, 2 * k:2 * k + 2, :].rearrange("p a c -> p (a c)"), ident[:, :])
                    last.then_inc(win["hT_ps"], 1)
                    pe.wait_ge(win["pick"], g + 1)
                    pe.wait_ge(win["hT"], g + 1)
                    for k in range(GT):
                        o = ps[1 + b][:, D * k:D * k + D]
                        half = D * (k % 2)
                        nc.tensor.matmul(o, hT[b][:, k // 2, :], wsT2[:, half:half + D], start=True, stop=False)
                        nc.tensor.matmul(o, pick[b][:, 0, k, :], mc[b][:, 0, k, 0:D], start=False, stop=False)
                        last = nc.tensor.matmul(o, pick[b][:, 1, k, :], mc[b][:, 1, k, 0:D], start=False, stop=True)
                    last.then_inc(win["o_ps"], 1)

                with pe.Fori(0, WG // 2 - 1) as i:
                    for b in range(2):
                        step(i * 2 + b, b)
                step(WG - 2, 0)
                step(WG - 1, 1)

            @block.scalar
            def _(act):
                own = own_waits(act, "act")
                prime(act, y_out)

                def step(g, b, last=False):
                    norm_act(act, b, g, MG)
                    act.wait_ge(win["hT_ps"], g + 1)
                    act.sem_inc(paced["act"], 1)
                    nc.scalar.activation(hT[b][:, :, :], ps[0][:, :].rearrange("p (k c) -> p k c", c=P),
                                         ACT.Copy).then_inc(win["hT"], 1)
                    act.wait_ge(win["y"], g + 1)
                    act.sem_inc(paced["act"], 1)
                    if last:
                        act.dma_start(out[WF * GT * P:(WF * GT + WR) * P, :].rearrange("(k p) c -> p k c", p=P),
                                      xs[b][:, 0:WR, :]).then_inc(y_out[b], 16)
                        act.dma_start(out[N - N % P:N, :], xs[b][0:N % P, WR, :]).then_inc(y_out[b], 16)
                    else:
                        act.dma_start(out[bass.ds(g * (GT * P), GT * P), :].rearrange("(k p) c -> p k c", p=P),
                                      xs[b][:, :, :]).then_inc(y_out[b], 16)

                with act.Fori(0, WG // 2 - 1) as i:
                    for b in range(2):
                        step(i * 2 + b, b)
                step(WG - 2, 0)
                step(WG - 1, 1, last=True)
                act.wait_ge(y_out[0], 16 * (WG // 2 + 1))
                act.wait_ge(y_out[1], 16 * (WG // 2 + 2))

        more = {n: sem(f"more_{n}") for n in ("longest", "in", "near", "pick", "ps", "y", "out")}

        with nc.Block() as block:
            def beyond(eng, body):
                eng.wait_ge(more["longest"], 1)
                with eng.If(eng.value_load(longest[0:1, 0:1], min_val=0, max_val=E) > P):
                    each_beyond(eng, body)
                with eng.Else():
                    pass

            def each_beyond(eng, body):
                n_done = eng.alloc_register(f"further_{eng.engine}".replace(".", "_"))
                eng.reg_mov(n_done, 0)
                for n in range(2):
                    for lo, hi, closing in ((0, NW - 1, False), (NW - 1, NW, True)):
                        with eng.Fori(lo, hi) as v:
                            first = eng.value_load(starts[0:1, n, bass.ds(v, 1)], min_val=0, max_val=E)
                            behind = eng.value_load(starts[0:1, n, bass.ds(v + 1, 1)], min_val=0, max_val=E)
                            with eng.If(behind - first > P):
                                with eng.Fori(first + P, behind, P) as at:
                                    eng.reg_add(n_done, n_done, 1)
                                    body(n, at, v, closing, eng.snap(n_done))
                            with eng.Else():
                                pass

            @block.sync
            def _(sp):

                def body(n, at, v, closing, count):
                    row0 = N - P if closing else v * P
                    sp.dma_start(mc[0][:, 0, 0, :], tables[n][bass.ds(at, P), :]).then_inc(more["in"], 16)
                    sp.dma_start(xs[0][:, 0, :], out[bass.ds(row0, P), :]).then_inc(more["in"], 16)
                    sp.wait_ge(more["y"], count)
                    sp.sem_inc(paced["sp"], 1)
                    sp.dma_start(out[bass.ds(row0, P), :], xs[0][:, 0, :]).then_inc(more["out"], 16)
                    sp.wait_ge(more["out"], count * 16)
                    sp.sem_inc(paced["sp"], 1)

                beyond(sp, body)

            @block.vector
            def _(dve):
                own = own_waits(dve, "dve")

                def body(n, at, v, closing, count):
                    dve.wait_ge(more["in"], count * 32)
                    if closing:
                        nc.vector.tensor_scalar(near[0][:, 0, 0:1], mc[0][:, 0, 0, D:RM], float(N - P), None,
                                                ALU.subtract).then_inc(more["near"], 1)
                    else:
                        nc.vector.tensor_tensor(near[0][:, 0, 0:1], mc[0][:, 0, 0, D:RM], first_of[:, bass.ds(v, 1)],
                                                ALU.subtract).then_inc(more["near"], 1)
                    dve.wait_ge(more["near"], count)
                    nc.vector.tensor_scalar(pick[0][:, 0, 0, :], iota_n[:, :], near[0][:, 0, 0:1], None,
                                            ALU.is_equal).then_inc(more["pick"], 1)
                    dve.wait_ge(more["ps"], count)
                    nc.vector.tensor_tensor(xs[0][:, 0, :], xs[0][:, 0, :], ps[1][:, 0:D], ALU.add).then_inc(more["y"], 1)

                own(nc.vector.tensor_tensor(counts[:, :, :], starts[:, :, 1:NW + 1], starts[:, :, 0:NW], ALU.subtract))
                own(nc.vector.tensor_reduce(longest[:, :], counts[:, :, :].rearrange("p n l -> p (n l)"), AX, ALU.max))
                dve.sem_inc(more["longest"], 1)
                beyond(dve, body)

            @block.tensor
            def _(pe):
                own = own_waits(pe, "pe")

                def body(n, at, v, closing, count):
                    pe.wait_ge(more["pick"], count)
                    nc.tensor.matmul(ps[1][:, 0:D], pick[0][:, 0, 0, :], mc[0][:, 0, 0, 0:D],
                                     start=True, stop=True).then_inc(more["ps"], 1)

                beyond(pe, body)


_INS = ['x', 'src', 'dst', 'edge_attr_32', 'edge_weight', 'L0_gnn_W_neigh', 'L0_gnn_b_neigh', 'L0_gnn_W_self',
        'L1_gnn_u', 'L1_gnn_W1', 'L1_gnn_b1', 'L1_gnn_W2', 'L1_gnn_b2']
_OUTS = [((100000, 64), 'float32')]


def kernel(**inputs):
    import numpy as _np
    import concourse.bacc as _bacc
    from concourse import mybir as _mybir
    from concourse.bass_utils import run_bass_kernel_spmd as _run

    nc = _bacc.Bacc("TRN2", target_bir_lowering=False, num_devices=1)
    arrays, args = {}, []
    for name in _INS:
        a = _np.ascontiguousarray(inputs[name])
        arrays[f"in_{name}_dram"] = a
        args.append(nc.dram_tensor(f"in_{name}_dram", a.shape, _mybir.dt.from_np(a.dtype), kind="ExternalInput").ap())
    for i, (shape, dtype) in enumerate(_OUTS):
        dt = _mybir.dt.from_np(_np.dtype(dtype))
        args.append(nc.dram_tensor(f"out_{i}_dram", shape, dt, kind="ExternalOutput").ap())
    graph_layers(nc, *args)
    r = _run(nc, [arrays], core_ids=[0])
    return r.results[0]["out_0_dram"]
```

```python
from contextlib import ExitStack

import concourse.bass as bass
from concourse import mybir

F32 = mybir.dt.float32
BF16 = mybir.dt.bfloat16
F16 = mybir.dt.float16
I32 = mybir.dt.int32
U32 = mybir.dt.uint32
ALU = mybir.AluOpType
ACT = mybir.ActivationFunctionType
AX = mybir.AxisListType.X

P = 128
GT = 8
DIGIT = 32
FLT_MAX = 3.4028234663852886e38
EPS = 1e-5


class Own:

    def __init__(self, sem, paced):
        self.sem, self.paced, self.done, self.n, self.at, self.per = sem, paced, 0, 0, None, 0

    def fold(self):
        self.done += self.n
        self.at, self.n = None, 0

    def loop(self, i, per):
        self.fold()
        self.at, self.per = i, per

    def end(self, trips):
        assert self.n == self.per, (self.n, self.per)
        self.done += trips * self.per
        self.at, self.n = None, 0

    def step(self, g, per):
        assert self.at is None or self.n == self.per, (self.n, self.per)
        self.at, self.per, self.n = g, per, 0

    steps_end = end

    def skip(self):
        self.n += 1
        self.eng.sem_inc(self.sem, 1)

    def __call__(self, ins):
        self.n += 1
        ins.then_inc(self.sem, 1)
        value = self.done + self.n
        if self.at is not None:
            value = self.at * self.per + value
        self.eng.wait_ge(self.sem, value)
        if self.paced is not None and not isinstance(value, int):
            self.eng.sem_inc(self.paced, 1)


def graph_layers(nc, x, src, dst, attr, weight, w_neigh, b_neigh, w_self, u, w1, b1, w2, b2, out):
    N, D = x.shape
    E, DE = attr.shape
    HID = w1.shape[1]
    KU = 3 * DE
    FT = E // P
    TAIL = E - FT * P
    NW = -(-N // P)
    LASTN = N - (NW - 1) * P
    NG = 2 * (-(-(FT + 1) // (2 * GT)))
    NT = NG * GT
    FG = FT // GT
    RT = FT - FG * GT
    RE = DE + 1
    RM = D + 1
    LANES = DIGIT * DIGIT
    assert D == 64 and DE == 32 and HID == P and 0 < TAIL < P and NW <= LANES and FG % 2 == 0

    ctx = ExitStack()
    with ctx:
        def sb(name, shape, dt=F32):
            return ctx.enter_context(nc.sbuf_tensor(name, shape, dt))

        def sem(name):
            return ctx.enter_context(nc.semaphore(name))

        def dram(name, shape, dt=F32):
            return nc.dram_tensor(name, shape, dt, kind="Internal").ap()

        ROWS = E + P + 48
        by_lane = dram("by_lane", [P, NT, RE])
        by_node = dram("by_node", [P, NT, RE])
        message = dram("message", [2 * ROWS, RM])
        x_of_src = dram("x_of_src", [P, NT, D])
        mlp_row = dram("mlp_row", [ROWS, RM])
        spare = dram("spare", [16, 1])
        starts_d = dram("starts_d", [2, LANES], I32)

        ident = sb("ident", [P, P])
        identb = sb("identb", [P, P], BF16)
        identh = sb("identh", [P, P], F16)
        later = sb("later", [P, P], F16)
        before = sb("before", [P, DIGIT])
        iota_d = sb("iota_d", [P, DIGIT], BF16)
        iota_n = sb("iota_n", [P, P])
        first_of = sb("first_of", [P, NW + GT])
        chain_mask = sb("chain_mask", [DIGIT, DIGIT, GT + 1])
        ones = sb("ones", [P, 512])
        eps_t = sb("eps_t", [P, 1])

        wn2 = sb("wn2", [P, P])
        ws_raw = sb("ws_raw", [D, 2, D])
        wsT2 = sb("wsT2", [P, P])
        w1_sb = sb("w1_sb", [KU, HID])
        w1u = sb("w1u", [P, 1])
        u0 = sb("u0", [P, 1])
        b1c = sb("b1c", [P, 1])
        hbias = sb("hbias", [P, 1])
        hrelu = sb("hrelu", [P, 1])
        hrelu_b = sb("hrelu_b", [P, P])
        w2_sb = sb("w2_sb", [P, D])
        b2b = sb("b2b", [P, D])
        bnb = sb("bnb", [P, D])
        c0b = sb("c0b", [P, D])
        biasb = sb("biasb", [P, D])

        src_i = sb("src_i", [P, NT + GT], I32)
        dst_i = sb("dst_i", [P, NT + GT], I32)
        ew = sb("ew", [P, NT])
        src_f = sb("src_f", [P, NT])
        dst_f = sb("dst_f", [P, NT])
        node_f = sb("node_f", [P, NT])
        near_f = sb("near_f", [P, NT])
        sign_b = sb("sign_b", [P, NT], BF16)
        key_v = sb("key_v", [P, NT])
        next_i = sb("next_i", [P, NT], I32)
        code_i = sb("code_i", [P, NT + GT], I32)
        digit_i = sb("digit_i", [P, NT + GT], I32)
        CODES = ("lane", "dst", "node")
        code_h = {n: sb(f"code_h_{n}", [P, NT + GT], F16) for n in CODES}
        hi_b = {n: sb(f"hi_b_{n}", [P, NT + GT], BF16) for n in CODES}
        lo_b = {n: sb(f"lo_b_{n}", [P, NT + GT], BF16) for n in CODES}
        idx_lane = sb("idx_lane", [P, NT], U32)
        idx_node = sb("idx_node", [P, NT], U32)
        idx_msg = sb("idx_msg", [P, NT], U32)
        idx_src = sb("idx_src", [P, NT], U32)
        rows = sb("rows", [P, NT, RE])

        oh_hi = [sb(f"oh_hi{b}", [P, 3, GT, DIGIT], BF16) for b in range(2)]
        oh_lo = [sb(f"oh_lo{b}", [P, 3, GT, DIGIT], BF16) for b in range(2)]
        code_s = [sb(f"code_s{b}", [P, GT], F16) for b in range(2)]
        ohT = [sb(f"ohT{b}", [DIGIT, GT, P]) for b in range(2)]
        hist = [sb(f"hist{b}", [DIGIT, DIGIT, GT + 1]) for b in range(2)]
        begin = [sb(f"begin{b}", [DIGIT, DIGIT, GT + 1]) for b in range(2)]
        same = [sb(f"same{b}", [P, GT, P], BF16) for b in range(2)]
        pos_base = sb("pos_base", [P, GT])
        pos_i = sb("pos_i", [P, GT], I32)
        pos_part = sb("pos_part", [P, 2, GT], I32)
        ones_b = sb("ones_b", [P, 2], BF16)
        prod = sb("prod", [P, GT, DIGIT])
        total = {n: sb(f"total_{n}", [DIGIT, DIGIT]) for n in CODES}
        row_total = sb("row_total", [DIGIT, 3])
        row_base = sb("row_base", [DIGIT, 3])
        inclusive = {n: sb(f"inclusive_{n}", [DIGIT, DIGIT]) for n in CODES}
        start0 = {n: sb(f"start0_{n}", [DIGIT, DIGIT]) for n in CODES}
        start_i = {n: sb(f"start_i_{n}", [DIGIT, DIGIT], I32) for n in ("dst", "node")}
        falls = sb("falls", [P, 1])
        unsorted_f = sb("unsorted_f", [DIGIT, 1])
        table_off = sb("table_off", [DIGIT, 1])
        unsorted_i = sb("unsorted_i", [1, 1], I32)
        starts = sb("starts", [1, 2, LANES], I32)
        counts = sb("counts", [1, 2, NW], I32)
        longest = sb("longest", [1, 1], I32)

        row_st = [sb(f"row_st{b}", [P, GT, RE]) for b in range(2)]
        idx_st = [sb(f"idx_st{b}", [P, GT], U32) for b in range(2)]
        gx_idx = [sb(f"gx_idx{b}", [P, GT], U32) for b in range(2)]
        xb = [sb(f"xb{b}", [P, GT, D]) for b in range(2)]
        xs = [sb(f"xs{b}", [P, GT, D]) for b in range(2)]
        xc = [sb(f"xc{b}", [P, GT, D]) for b in range(2)]
        sq = sb("sq", [P, GT, D])
        stat = [sb(f"stat{b}", [P, 4, GT]) for b in range(2)]
        h = [sb(f"h{b}", [P, GT, D]) for b in range(2)]
        hT = [sb(f"hT{b}", [P, 4, P]) for b in range(2)]
        m_row = [sb(f"m_row{b}", [P, GT, RM]) for b in range(2)]
        m_key = [sb(f"m_key{b}", [P, GT]) for b in range(2)]
        mc = [sb(f"mc{b}", [P, GT, RM]) for b in range(2)]
        near = [sb(f"near{b}", [P, GT]) for b in range(2)]
        pick = [sb(f"pick{b}", [P, 2, GT, P]) for b in range(2)]
        fill = sb("fill", [ROWS - E >> 1, 2, RM])

        a_st = [sb(f"a_st{b}", [P, 4, KU]) for b in range(2)]
        s_st = [sb(f"s_st{b}", [P, 4, KU], BF16) for b in range(2)]
        aT = [sb(f"aT{b}", [KU, 512]) for b in range(2)]
        inv = [sb(f"inv{b}", [P, 4]) for b in range(2)]
        uT = [sb(f"uT{b}", [KU, 512]) for b in range(2)]
        part = lambda b, n, k: pick[b][:, n, k:k + 4, :].rearrange("p k c -> p (k c)")
        hid = [part(b, 0, 0) for b in range(2)]
        run = [part(b, 0, 4)[0:KU, :] for b in range(2)]
        cut = [part(b, 1, 0)[0:KU, :] for b in range(2)]
        keep = [part(b, 1, 4)[0:KU, :] for b in range(2)]
        v_row = [sb(f"v_row{b}", [P, 4, RM]) for b in range(2)]

        ps = [ctx.enter_context(nc.psum_tensor(f"ps{n}", [P, 512], F32)) for n in range(8)]

        paced = {e: sem(f"paced_{e}") for e in ("sp", "pool", "act", "dve", "pe")}
        owns = {e: Own(sem(f"own_{e}"), paced[e] if e in ("pool", "act") else None) for e in ("pool", "act", "dve", "pe")}

        def own_waits(eng, name):
            owns[name].eng = eng
            return owns[name]

        TRIPS = NG // 2
        h_ps = ps[6][0:DIGIT, 0:256].rearrange("p (k l) -> p k l", l=DIGIT)
        g_ps = ps[7][:, 0:256].rearrange("p (k l) -> p k l", l=DIGIT)
        e_ps = ps[7][:, 256:256 + GT]

        def ranking(name):
            return {s: sem(f"{name}_{s}") for s in (
                "oh", "done", "eq", "same", "h", "h_used", "t", "t_used", "ohT", "w", "begin", "look", "idx")}

        def digits_of(own, name, code):
            nc.vector.tensor_copy(code_h[name][:, :], code[:, :])
            own(nc.vector.tensor_scalar(digit_i[:, :], code[:, :], 5, None, ALU.arith_shift_right))
            own(nc.vector.tensor_copy(hi_b[name][:, :], digit_i[:, :]))
            own(nc.vector.tensor_scalar(digit_i[:, :], code[:, :], DIGIT - 1, None, ALU.bitwise_and))
            own(nc.vector.tensor_copy(lo_b[name][:, :], digit_i[:, :]))

        def one_hots(g, b, name, c):
            grid = iota_d[:, :].unsqueeze(1).to_broadcast([P, GT, DIGIT])
            hi = hi_b[name][:, bass.ds(g * GT, GT)].unsqueeze(2).to_broadcast([P, GT, DIGIT])
            lo = lo_b[name][:, bass.ds(g * GT, GT)].unsqueeze(2).to_broadcast([P, GT, DIGIT])
            nc.vector.tensor_tensor(oh_hi[b][:, c, :, :], grid, hi, ALU.is_equal)
            return nc.vector.tensor_tensor(oh_lo[b][:, c, :, :], grid, lo, ALU.is_equal)

        def ranked_tiles(g, b, name):
            nc.vector.tensor_copy(code_s[b][:, :], code_h[name][:, bass.ds(g * GT, GT)])
            return one_hots(g, b, name, 0)

        def rank_dve(dve, own, r, name, index):
            own(nc.vector.tensor_copy(begin[1][:, :, GT], start0[name][:, :]))
            own(ranked_tiles(0, 0, name))
            dve.sem_inc(r["oh"], 1)
            with dve.Fori(0, TRIPS) as i:
                own.loop(i, 12)
                for b in range(2):
                    g = i * 2 + b
                    dve.wait_ge(r["eq"], g + 1)
                    for half in range(2):
                        last = nc.vector.tensor_tensor(
                            same[b][:, 4 * half:4 * half + 4, :], ps[2 * b + half][:, :].rearrange("p (k c) -> p k c", c=P),
                            code_h[name][:, bass.ds(g * GT + 4 * half, 4)].unsqueeze(2).to_broadcast([P, 4, P]), ALU.is_equal)
                    last.then_inc(r["same"], 1)
                    dve.wait_ge(r["w"], g + 1)
                    own(nc.vector.tensor_copy(hist[b][:, :, 0], begin[1 - b][:, :, GT]))
                    nc.vector.tensor_tensor_scan(begin[b][:, :, :].rearrange("p l k -> p (l k)"),
                                                 chain_mask[:, :, :].rearrange("p l k -> p (l k)"),
                                                 hist[b][:, :, :].rearrange("p l k -> p (l k)"),
                                                 0.0, ALU.mult, ALU.add).then_inc(r["begin"], 1)
                    ranked_tiles(g + 1, 1 - b, name).then_inc(r["oh"], 1)
                    dve.wait_ge(r["look"], g + 1)
                    own(nc.vector.tensor_tensor(prod[:, :, :], g_ps, oh_lo[b][:, 0, :, :], ALU.mult))
                    own(nc.vector.tensor_reduce(pos_base[:, :], prod[:, :, :], AX, ALU.add))
                    if name == "dst":
                        own(nc.vector.tensor_tensor(pos_i[:, :], pos_base[:, :], e_ps, ALU.add))
                        nc.vector.tensor_copy(pos_part[:, 0, :], pos_i[:, :])
                        own(nc.vector.tensor_copy(pos_part[:, 1, :], pos_i[:, :]))
                        own(nc.vector.tensor_scalar(index[:, bass.ds(g * GT, GT)], pos_i[:, :], float(ROWS), None, ALU.add))
                    else:
                        own(nc.vector.tensor_tensor(pos_i[:, :], pos_base[:, :], e_ps, ALU.add))
                        nc.vector.tensor_scalar(pos_part[:, 0, :], pos_i[:, :], P - 1, None, ALU.bitwise_and)
                        own(nc.vector.tensor_scalar(pos_part[:, 1, :], pos_i[:, :], 7, None, ALU.arith_shift_right))
                        own(nc.vector.scalar_tensor_tensor(index[:, bass.ds(g * GT, GT)], pos_part[:, 0, :], float(NT),
                                                           pos_part[:, 1, :], ALU.mult, ALU.add))
                    dve.sem_inc(r["idx"], 1)
                    dve.sem_inc(r["done"], 1)
                own.end(TRIPS)

        def rank_pe(pe, r):
            with pe.Fori(0, TRIPS) as i:
                for b in range(2):
                    g = i * 2 + b
                    pe.wait_ge(r["oh"], g + 1)
                    pe.wait_ge(r["done"], g + 1)
                    for half in range(2):
                        bank = ps[2 * b + half]
                        nc.tensor.matmul(bank[:, :].rearrange("p (k c) -> p k c", c=P), identh[:, :],
                                         later[:, :].unsqueeze(1).to_broadcast([P, 4, P]), start=True, stop=False)
                        for k in range(4):
                            last = nc.tensor.matmul(
                                bank[:, P * k:P * k + P],
                                code_s[b][:, 4 * half + k:4 * half + k + 1].to_broadcast([P, P]),
                                identh[:, :], start=False, stop=(k == 3))
                    last.then_inc(r["eq"], 1)
                    pe.wait_ge(r["h_used"], g + 1)
                    for k in range(GT):
                        last = nc.tensor.matmul(h_ps[:, k, :], oh_hi[b][:, 0, k, :], oh_lo[b][:, 0, k, :],
                                                start=True, stop=True)
                    last.then_inc(r["h"], 1)
                    pe.wait_ge(r["t_used"], g + 1)
                    for k in range(GT):
                        last = nc.tensor.matmul(ps[4 + k // 4][0:DIGIT, P * (k % 4):P * (k % 4) + P],
                                                oh_hi[b][:, 0, k, :], identb[:, :], start=True, stop=True)
                    last.then_inc(r["t"], 1)
                    pe.wait_ge(r["same"], g + 1)
                    for k in range(GT):
                        nc.tensor.matmul(e_ps[:, k:k + 1], same[b][:, k, :], ones_b[:, 0:1], start=True, stop=True)
                    pe.wait_ge(r["ohT"], g + 1)
                    pe.wait_ge(r["begin"], g + 1)
                    for k in range(GT):
                        last = nc.tensor.matmul(g_ps[:, k, :], ohT[b][:, k, :], begin[b][:, :, k],
                                                start=True, stop=True)
                    last.then_inc(r["look"], 1)

        def rank_act(act, own, r):
            act.sem_inc(r["done"], 2)
            act.sem_inc(r["t_used"], 1)
            act.sem_inc(r["h_used"], 1)
            with act.Fori(0, TRIPS) as i:
                own.loop(i, 4)
                for b in range(2):
                    g = i * 2 + b
                    act.wait_ge(r["h"], g + 1)
                    act.sem_inc(paced["act"], 1)
                    act.wait_ge(r["done"], g + 1)
                    act.sem_inc(paced["act"], 1)
                    own(nc.scalar.activation(hist[b][:, :, 1:GT + 1], h_ps.rearrange("p k l -> p l k"), ACT.Copy))
                    act.sem_inc(r["w"], 1)
                    act.sem_inc(r["h_used"], 1)
                    act.wait_ge(r["t"], g + 1)
                    act.sem_inc(paced["act"], 1)
                    nc.scalar.activation(ohT[b][:, 0:4, :], ps[4][0:DIGIT, :].rearrange("p (k c) -> p k c", c=P), ACT.Copy)
                    own(nc.scalar.activation(ohT[b][:, 4:8, :], ps[5][0:DIGIT, :].rearrange("p (k c) -> p k c", c=P), ACT.Copy))
                    act.sem_inc(r["ohT"], 1)
                    act.sem_inc(r["t_used"], 1)
                own.end(TRIPS)

        spare_rows = list(range(spare.shape[0]))

        def prime(eng, sems):
            for s in sems:
                n = spare_rows.pop()
                eng.dma_start(spare[n:n + 1, :], eps_t[0:1, 0:1]).then_inc(s, 16)
                eng.wait_ge(s, 16)

        def scatter_rows(pool, own, r, index, table, sent):
            def send(b, k, parts):
                nc.gpsimd.indirect_dma_start(
                    out=table, out_offset=bass.IndirectOffsetOnAxis(ap=idx_st[b][0:parts, k:k + 1], axis=0),
                    in_=row_st[b][0:parts, k, :], in_offset=None).then_inc(sent[b], 16)

            def put(g, b):
                nc.gpsimd.tensor_copy(idx_st[b][:, :], index[:, bass.ds(g * GT, GT)])
                own(nc.gpsimd.tensor_copy(row_st[b][:, :, :], rows[:, bass.ds(g * GT, GT), :]))

            prime(pool, sent)
            with pool.Fori(0, FG // 2) as i:
                own.loop(i, 2)
                for b in range(2):
                    pool.wait_ge(r["idx"], i * 2 + (b + 1))
                    pool.sem_inc(paced["pool"], 1)
                    pool.wait_ge(sent[b], i * (16 * GT) + 16)
                    pool.sem_inc(paced["pool"], 1)
                    put(i * 2 + b, b)
                    for k in range(GT):
                        send(b, k, P)
                own.end(FG // 2)
            pool.wait_ge(r["idx"], FG + 1)
            pool.wait_ge(sent[0], FG // 2 * 16 * GT + 16)
            put(FG, 0)
            for k in range(RT):
                send(0, k, P)
            send(0, RT, TAIL)
            pool.wait_ge(sent[0], FG // 2 * 16 * GT + 16 + 16 * (RT + 1))
            pool.wait_ge(sent[1], FG // 2 * 16 * GT + 16)

        ln = {s: sem(f"ln_{s}") for s in ("centred", "squared", "summed", "root")}

        def wide(a):
            return a.unsqueeze(2).to_broadcast([P, GT, D])

        def norm_centre(own, b):
            own(nc.vector.tensor_reduce(stat[b][:, 0, :], xb[b][:, :, :], AX, ALU.add))
            own(nc.vector.tensor_scalar(stat[b][:, 1, :], stat[b][:, 0, :], 1.0 / D, None, ALU.mult))
            nc.vector.tensor_tensor(xc[b][:, :, :], xb[b][:, :, :], wide(stat[b][:, 1, :]),
                                    ALU.subtract).then_inc(ln["centred"], 1)

        def norm_sum(dve, b, count):
            dve.wait_ge(ln["squared"], count)
            nc.vector.tensor_reduce(stat[b][:, 3, :], sq[:, :, :], AX, ALU.add).then_inc(ln["summed"], 1)

        def norm_scale(dve, own, b, count, scale):
            dve.wait_ge(ln["root"], count)
            own(nc.vector.reciprocal(stat[b][:, 2, :], stat[b][:, 3, :]))
            if scale is not None:
                own(nc.vector.tensor_tensor(stat[b][:, 2, :], stat[b][:, 2, :], scale, ALU.mult))
            return nc.vector.scalar_tensor_tensor(h[b][:, :, :], xc[b][:, :, :], 0.0, wide(stat[b][:, 2, :]),
                                                  ALU.max, ALU.mult)

        def norm_square(act, b, count):
            act.wait_ge(ln["centred"], count)
            nc.scalar.activation(sq[:, :, :], xc[b][:, :, :], ACT.Square).then_inc(ln["squared"], 1)

        def norm_root(act, b, count):
            act.wait_ge(ln["summed"], count)
            nc.scalar.activation(stat[b][:, 3, :], stat[b][:, 3, :], ACT.Sqrt, bias=eps_t[:, :],
                                 scale=1.0 / D).then_inc(ln["root"], 1)

        def transpose_h(pe, b, done):
            for k in range(4):
                last = nc.tensor.transpose(ps[3 * b][:, P * k:P * k + P],
                                           h[b][:, 2 * k:2 * k + 2, :].rearrange("p a c -> p (a c)"), ident[:, :])
            last.then_inc(done, 1)

        def evacuate_hT(b, done):
            nc.scalar.activation(hT[b][:, :, :], ps[3 * b][:, :].rearrange("p (k c) -> p k c", c=P), ACT.Copy).then_inc(done, 1)

        loaded = {n: sem(f"loaded_{n}") for n in ("weights", "edges", "attr", "lane", "node", "starts", "shift")}
        made = {n: sem(f"made_{n}") for n in ("const", "pads", "wsT_ps", "wsT", "c0_ps", "hbias", "c0", "srcs",
                                              "node_copy", "sign", "keys", "starts", "messages")}
        starts_out = sem("starts_out")
        filled = sem("filled")
        sent_lane = [sem(f"sent_lane{b}") for b in range(2)]
        sent_node = [sem(f"sent_node{b}") for b in range(2)]
        r_lane, r_dst, r_node = ranking("lane"), ranking("dst"), ranking("node")
        hg = {s: sem(f"hist_{s}") for s in ("oh", "used", "rows", "base")}
        MG = FG + 1
        gathered = [sem(f"gathered{b}") for b in range(2)]
        x_kept = [sem(f"x_kept{b}") for b in range(2)]

        def edge_load(eng, tile, source):
            eng.dma_start(tile[:, 0:FT], source[0:FT * P].rearrange("(p t) -> p t", p=P)).then_inc(loaded["edges"], 16)
            eng.dma_start(tile[0:TAIL, FT:FT + 1],
                          source[FT * P:E].rearrange("(p o) -> p o", o=1)).then_inc(loaded["edges"], 16)

        with nc.Block() as block:
            @block.sync
            def _(sp):
                sp.wait_ge(made["pads"], 1)
                edge_load(sp, src_i, src)
                edge_load(sp, dst_i, dst)
                edge_load(sp, ew, weight)
                sp.dma_start(next_i[:, 0:FT], dst[1:FT * P + 1].rearrange("(p t) -> p t", p=P)).then_inc(loaded["edges"], 16)
                sp.dma_start(next_i[0:TAIL - 1, FT:FT + 1],
                             dst[FT * P + 1:E].rearrange("(p o) -> p o", o=1)).then_inc(loaded["edges"], 16)
                sp.dma_start(wn2[0:D, 0:D], w_neigh).then_inc(loaded["weights"], 16)
                sp.dma_start(wn2[D:P, D:P], w_neigh).then_inc(loaded["weights"], 16)
                for n in range(2):
                    sp.dma_start(ws_raw[:, n, :], w_self).then_inc(loaded["weights"], 16)
                sp.dma_start(w1_sb[:, :], w1[0:KU, :]).then_inc(loaded["weights"], 16)
                sp.dma_start(w1u[:, :], w1[KU, :].rearrange("(p o) -> p o", o=1)).then_inc(loaded["weights"], 16)
                sp.dma_start(b1c[:, :], b1.rearrange("(p o) -> p o", o=1)).then_inc(loaded["weights"], 16)
                sp.dma_start(u0[:, :], u[0:1, :].to_broadcast([P, 1])).then_inc(loaded["weights"], 16)
                sp.dma_start(w2_sb[:, :], w2).then_inc(loaded["weights"], 16)
                sp.dma_start(b2b[:, :], b2.unsqueeze(0).to_broadcast([P, D])).then_inc(loaded["weights"], 16)
                sp.dma_start(bnb[:, :], b_neigh.unsqueeze(0).to_broadcast([P, D])).then_inc(loaded["weights"], 16)
                sp.dma_start(rows[:, 0:FT, 0:DE],
                             attr[0:FT * P, :].rearrange("(p t) c -> p t c", p=P)).then_inc(loaded["attr"], 16)
                sp.dma_start(rows[0:TAIL, FT, 0:DE], attr[FT * P:E, :]).then_inc(loaded["attr"], 16)
                for table in (message[E:ROWS, :], message[ROWS + E:2 * ROWS, :], mlp_row[E:ROWS, :]):
                    sp.dma_start(table.rearrange("(p a) c -> p a c", a=2), fill[:, :, :]).then_inc(filled, 16)

                def keep(g, b, count):
                    sp.wait_ge(gathered[b], count * (16 * GT))
                    sp.sem_inc(paced["sp"], 1)
                    sp.dma_start(x_of_src[:, bass.ds(g * GT, GT), :], xb[b][:, :, :]).then_inc(x_kept[b], 16)

                sp.wait_ge(made["const"], 1)
                prime(sp, x_kept)
                with sp.Fori(0, FG // 2) as i:
                    for b in range(2):
                        keep(i * 2 + b, b, i + 1)
                keep(FG, 0, FG // 2 + 1)
                sp.wait_ge(x_kept[0], 16 * (FG // 2 + 2))
                sp.wait_ge(x_kept[1], 16 * (FG // 2 + 1))
                sp.wait_ge(loaded["weights"], 16 * 11)
                sp.wait_ge(loaded["edges"], 16 * 8)
                sp.wait_ge(loaded["attr"], 32)
                sp.wait_ge(filled, 16 * 3)

            @block.gpsimd
            def _(pool):
                own = own_waits(pool, "pool")
                nc.gpsimd.memset(src_i[:, :], -1)
                nc.gpsimd.memset(dst_i[:, :], -1)
                nc.gpsimd.memset(code_i[:, :], -1)
                nc.gpsimd.memset(next_i[:, :], N)
                nc.gpsimd.memset(ew[:, :], 0.0)
                nc.gpsimd.memset(wn2[:, :], 0.0)
                nc.gpsimd.memset(wsT2[:, :], 0.0)
                nc.gpsimd.memset(fill[:, :, :], 0.0)
                own(nc.gpsimd.memset(rows[:, :, :], 0.0))
                own(nc.gpsimd.memset(fill[:, :, D:RM], -1.0))
                pool.sem_inc(made["pads"], 1)
                for t, full in ((ident, False), (identb, False), (identh, False), (later, True)):
                    own(nc.gpsimd.memset(t[:, :], 2048.0 if full else 0.0))
                    if full:
                        own(nc.gpsimd.affine_select(out=t[:, :], in_=t[:, :], compare_op=ALU.is_ge, fill=0.0,
                                                    base=0, pattern=[[-1, P]], channel_multiplier=1))
                    else:
                        own(nc.gpsimd.affine_select(out=t[:, :], in_=t[:, :], compare_op=ALU.not_equal, fill=1.0,
                                                    base=0, pattern=[[-1, P]], channel_multiplier=1))
                own(nc.gpsimd.memset(before[:, :], 1.0))
                own(nc.gpsimd.affine_select(out=before[:, :], in_=before[:, :], compare_op=ALU.is_gt, fill=0.0,
                                            base=0, pattern=[[1, DIGIT]], channel_multiplier=-1))
                for t, pattern in ((iota_d, [[1, DIGIT]]), (iota_n, [[1, P]]), (first_of, [[P, NW + GT]])):
                    own(nc.gpsimd.iota(t[:, :], pattern, base=0, channel_multiplier=0,
                                       allow_small_or_imprecise_dtypes=True))
                own(nc.gpsimd.memset(chain_mask[:, :, :], 1.0))
                own(nc.gpsimd.memset(chain_mask[:, :, 0:1], 0.0))
                own(nc.gpsimd.memset(eps_t[:, :], EPS))
                own(nc.gpsimd.memset(ones[:, :], 1.0))
                own(nc.gpsimd.memset(ones_b[:, :], 1.0))
                for b in range(2):
                    own(nc.gpsimd.memset(a_st[b][:, :, :], 1.0))
                pool.sem_inc(made["const"], 3)

                def gather(g, b, count):
                    pool.wait_ge(x_kept[b], count * 16)
                    pool.sem_inc(paced["pool"], 1)
                    own(nc.gpsimd.tensor_copy(gx_idx[b][:, :], idx_src[:, bass.ds(g * GT, GT)]))
                    for k in range(GT):
                        nc.gpsimd.indirect_dma_start(
                            out=xb[b][:, k, :], out_offset=None, in_=x,
                            in_offset=bass.IndirectOffsetOnAxis(ap=gx_idx[b][:, k:k + 1], axis=0)).then_inc(gathered[b], 16)

                pool.wait_ge(made["srcs"], 1)
                with pool.Fori(0, FG // 2) as i:
                    own.loop(i, 2)
                    for b in range(2):
                        gather(i * 2 + b, b, i + 1)
                    own.end(FG // 2)
                gather(FG, 0, FG // 2 + 1)

            @block.vector
            def _(dve):
                own = own_waits(dve, "dve")
                dve.wait_ge(loaded["edges"], 16 * 8)
                own(nc.vector.tensor_scalar(idx_src[:, :], src_i[:, 0:NT], 0.0, None, ALU.max))
                dve.sem_inc(made["srcs"], 1)
                dve.wait_ge(made["const"], 1)
                nc.vector.tensor_scalar(code_i[:, 0:FT], src_i[:, 0:FT], P - 1, None, ALU.bitwise_and)
                own(nc.vector.tensor_scalar(code_i[0:TAIL, FT:FT + 1], src_i[0:TAIL, FT:FT + 1], P - 1, None,
                                            ALU.bitwise_and))
                digits_of(own, "lane", code_i)
                own(nc.vector.tensor_scalar(code_i[:, :], src_i[:, :], 7, None, ALU.arith_shift_right))
                digits_of(own, "node", code_i)
                own(nc.vector.tensor_scalar(code_i[:, :], dst_i[:, :], 7, None, ALU.arith_shift_right))
                digits_of(own, "dst", code_i)
                own(nc.vector.tensor_scalar(next_i[:, :], next_i[:, :], 7, None, ALU.arith_shift_right))
                own(nc.vector.tensor_tensor(near_f[:, :], next_i[:, :], code_i[:, 0:NT], ALU.is_lt))
                own(nc.vector.tensor_reduce(falls[:, :], near_f[:, :], AX, ALU.add))
                nc.vector.tensor_copy(src_f[:, :], src_i[:, 0:NT])
                own(nc.vector.tensor_copy(dst_f[:, :], dst_i[:, 0:NT]))
                with dve.Fori(0, TRIPS) as i:
                    for b in range(2):
                        g = i * 2 + b
                        dve.wait_ge(hg["used"], g + 1)
                        for c, name in enumerate(CODES):
                            last = one_hots(g, b, name, c)
                        last.then_inc(hg["oh"], 1)
                dve.wait_ge(hg["used"], NG + 2)
                for c, name in enumerate(CODES):
                    own(nc.vector.tensor_copy(total[name][:, :], ps[c][0:DIGIT, 0:DIGIT]))
                    own(nc.vector.tensor_reduce(row_total[:, c:c + 1], total[name][:, :], AX, ALU.add))
                dve.sem_inc(hg["rows"], 1)
                dve.wait_ge(hg["base"], 1)
                nc.vector.tensor_scalar(unsorted_f[:, :], ps[4][0:DIGIT, 0:1], 1.0, None, ALU.min)
                own(nc.vector.tensor_copy(row_base[:, :], ps[3][0:DIGIT, 0:3]))
                nc.vector.tensor_scalar(table_off[:, :], unsorted_f[:, :], float(ROWS), None, ALU.mult)
                nc.vector.tensor_copy(unsorted_i[:, :], unsorted_f[0:1, :])
                for c, name in enumerate(CODES):
                    own(nc.vector.tensor_tensor_scan(inclusive[name][:, :], ones[0:DIGIT, 0:DIGIT], total[name][:, :],
                                                     row_base[:, c:c + 1], ALU.mult, ALU.add))
                    own(nc.vector.tensor_tensor(start0[name][:, :], inclusive[name][:, :], total[name][:, :], ALU.subtract))
                nc.vector.tensor_scalar(start_i["dst"][:, :], start0["dst"][:, :], table_off[:, :], None, ALU.add)
                own(nc.vector.tensor_copy(start_i["node"][:, :], start0["node"][:, :]))
                dve.sem_inc(made["starts"], 1)
                rank_dve(dve, own, r_lane, "lane", idx_lane)
                dve.wait_ge(loaded["weights"], 16 * 11)
                own(nc.vector.tensor_tensor(hbias[:, :], w1u[:, :], u0[:, :], ALU.mult))
                own(nc.vector.tensor_tensor(hbias[:, :], hbias[:, :], b1c[:, :], ALU.add))
                own(nc.vector.tensor_scalar(hrelu[:, :], hbias[:, :], 0.0, None, ALU.max))
                own(nc.vector.tensor_copy(hrelu_b[:, :], hrelu[:, :].to_broadcast([P, P])))
                dve.sem_inc(made["hbias"], 1)
                dve.wait_ge(made["wsT_ps"], 1)
                for half in (0, D):
                    own(nc.vector.tensor_copy(wsT2[half:half + D, half:half + D], ps[0][half:half + D, 0:D]))
                dve.wait_ge(made["c0_ps"], 1)
                own(nc.vector.tensor_copy(c0b[:, :], ps[1][:, 0:D]))
                own(nc.vector.tensor_tensor(biasb[:, :], b2b[:, :], bnb[:, :], ALU.add))
                own(nc.vector.tensor_tensor(biasb[:, :], biasb[:, :], c0b[:, :], ALU.add))
                dve.wait_ge(loaded["attr"], 32)
                own(nc.vector.tensor_copy(rows[:, :, DE], src_f[:, :]))

            @block.tensor
            def _(pe):
                def tally(g, b, first=False, final=False):
                    pe.wait_ge(hg["oh"], g + 1)
                    for c in range(3):
                        for k in range(GT):
                            last = nc.tensor.matmul(ps[c][0:DIGIT, 0:DIGIT], oh_hi[b][:, c, k, :], oh_lo[b][:, c, k, :],
                                                    start=(first and k == 0), stop=(final and k == GT - 1))
                    last.then_inc(hg["used"], 1)

                pe.wait_ge(made["const"], 1)
                pe.sem_inc(hg["used"], 2)
                tally(0, 0, first=True)
                with pe.Fori(0, TRIPS - 1) as i:
                    for j in range(2):
                        tally(i * 2 + (j + 1), 1 - j)
                tally(NG - 1, 1, final=True)
                pe.wait_ge(hg["rows"], 1)
                nc.tensor.matmul(ps[3][0:DIGIT, 0:3], before[0:DIGIT, :], row_total[:, :], start=True, stop=True)
                nc.tensor.matmul(ps[4][0:DIGIT, 0:1], ones[:, 0:DIGIT], falls[:, :],
                                 start=True, stop=True).then_inc(hg["base"], 1)
                rank_pe(pe, r_lane)
                pe.wait_ge(loaded["weights"], 16 * 11)
                pe.wait_ge(made["hbias"], 1)
                nc.tensor.matmul(ps[0][:, 0:D], ws_raw[:, :, :].rearrange("p a c -> p (a c)"), ident[0:D, 0:D],
                                 start=True, stop=True).then_inc(made["wsT_ps"], 1)
                nc.tensor.matmul(ps[1][:, 0:D], hrelu_b[:, :], w2_sb[:, :], start=True, stop=True).then_inc(made["c0_ps"], 1)

            @block.scalar
            def _(act):
                own = own_waits(act, "act")
                rank_act(act, own, r_lane)

        msg = {n: sem(f"msg_{n}") for n in ("x_used", "h", "hT_ps", "hT", "m_ps", "row", "key")}
        x_msg = [sem(f"x_msg{b}") for b in range(2)]
        msg_out = [sem(f"msg_out{b}") for b in range(2)]
        again_in, again_out = sem("again_in"), sem("again_out")
        again_own = sem("again_own")
        message_pt = message[0:FT * P, :].rearrange("(p t) c -> p t c", p=P)

        WG = -(-NW // GT)
        WF = (N // P) // GT
        WR = N // P - WF * GT
        assert WG % 2 == 0 and WF == WG - 1

        def window_pass(name):
            s = {n: sem(f"{name}_{n}") for n in ("x_used", "rows_used", "xs", "pick", "h", "hT_ps", "hT", "o_ps", "y")}
            s["x_in"] = [sem(f"{name}_x_in{b}") for b in range(2)]
            s["rows_in"] = [sem(f"{name}_rows_in{b}") for b in range(2)]
            s["y_out"] = [sem(f"{name}_y_out{b}") for b in range(2)]
            return s

        def over_steps(eng, n, step):
            step(0, 0, 1)
            with eng.Fori(0, n // 2 - 1) as i:
                for b in (1, 0):
                    step(i * 2 + (2 - b), b, i + (2 - b))
            step(n - 1, 1, n // 2)

        def over_windows(eng, step):
            over_steps(eng, WG, step)

        def nodes_of(table, g):
            return table[bass.ds(g * (GT * P), GT * P), :].rearrange("(k p) c -> p k c", p=P)

        def last_nodes(table):
            return (table[WF * GT * P:(WF * GT + WR) * P, :].rearrange("(k p) c -> p k c", p=P), table[N - N % P:N, :])

        def load_windows(sp, s, n, nodes, table):
            sp.sem_inc(s["x_used"], 2)
            sp.sem_inc(s["rows_used"], 2)
            at = [sp.alloc_register(f"at{n}_{k}") for k in range(GT)]

            def step(g, b, count):
                sp.reg_load(at, starts[0:1, n, bass.ds(g * GT, GT)])
                sp.wait_ge(s["x_used"], g + 1)
                sp.sem_inc(paced["sp"], 1)
                if isinstance(g, int) and g == WG - 1:
                    full, short = last_nodes(nodes)
                    sp.dma_start(xb[b][:, 0:WR, :], full).then_inc(s["x_in"][b], 16)
                    sp.dma_start(xb[b][0:N % P, WR, :], short).then_inc(s["x_in"][b], 16)
                else:
                    sp.dma_start(xb[b][:, :, :], nodes_of(nodes, g)).then_inc(s["x_in"][b], 16)
                sp.wait_ge(s["rows_used"], g + 1)
                sp.sem_inc(paced["sp"], 1)
                for k in range(GT):
                    sp.dma_start(mc[b][:, k, :], table[bass.ds(sp.snap(at[k]), P), :]).then_inc(s["rows_in"][b], 16)

            over_windows(sp, step)

        def store_windows(act, s, g, b, g1):
            act.wait_ge(s["y"], g1)
            act.sem_inc(paced["act"], 1)
            if isinstance(g, int) and g == WG - 1:
                full, short = last_nodes(out)
                act.dma_start(full, xs[b][:, 0:WR, :]).then_inc(s["y_out"][b], 16)
                act.dma_start(short, xs[b][0:N % P, WR, :]).then_inc(s["y_out"][b], 16)
            else:
                act.dma_start(nodes_of(out, g), xs[b][:, :, :]).then_inc(s["y_out"][b], 16)

        def pick_rows(own, s, g, b):
            own(nc.vector.tensor_tensor(near[b][:, :], mc[b][:, :, D], first_of[:, bass.ds(g * GT, GT)], ALU.subtract))
            nc.vector.tensor_tensor(pick[b][:, 0, :, :], iota_n[:, :].unsqueeze(1).to_broadcast([P, GT, P]),
                                    near[b][:, :].unsqueeze(2).to_broadcast([P, GT, P]), ALU.is_equal).then_inc(s["pick"], 1)

        def rows_needed(count, g):
            return count * 16 + (16 if isinstance(g, int) and g == WG - 1 else 0)

        l0 = window_pass("l0")
        with nc.Block() as block:
            @block.gpsimd
            def _(pool):
                own = own_waits(pool, "pool")
                scatter_rows(pool, own, r_lane, idx_lane, by_lane.rearrange("p t c -> (p t) c"), sent_lane)
                with pool.If(pool.value_load(unsorted_i[0:1, 0:1], min_val=0, max_val=1) > 0):
                    pool.wait_ge(r_dst["idx"], NG)
                    pool.wait_ge(made["messages"], 1)

                    def resend(g, n_in, count, parts):
                        pool.wait_ge(again_in, n_in)
                        pool.sem_inc(paced["pool"], 1)
                        nc.gpsimd.tensor_copy(idx_st[0][:, :], idx_msg[:, bass.ds(g * GT, GT)]).then_inc(again_own, 1)
                        pool.wait_ge(again_own, g + 1)
                        pool.sem_inc(paced["pool"], 1)
                        for k, part in enumerate(parts):
                            nc.gpsimd.indirect_dma_start(
                                out=message, out_offset=bass.IndirectOffsetOnAxis(ap=idx_st[0][0:part, k:k + 1], axis=0),
                                in_=m_row[0][0:part, k, :], in_offset=None).then_inc(again_out, 16)
                        pool.wait_ge(again_out, count)
                        pool.sem_inc(paced["pool"], 1)

                    with pool.Fori(0, FG) as g:
                        nc.gpsimd.dma_start(m_row[0][:, :, :], message_pt[:, bass.ds(g * GT, GT), :]).then_inc(again_in, 16)
                        resend(g, (g + 1) * 16, (g + 1) * (16 * GT), [P] * GT)
                    nc.gpsimd.dma_start(m_row[0][:, 0:RT, :], message_pt[:, FG * GT:FT, :]).then_inc(again_in, 16)
                    nc.gpsimd.dma_start(m_row[0][0:TAIL, RT, :], message[FT * P:E, :]).then_inc(again_in, 16)
                    resend(FG, (FG + 2) * 16, FG * 16 * GT + 16 * (RT + 1), [P] * RT + [TAIL])
                    pool.sem_inc(made["messages"], 1)
                with pool.Else():
                    pool.sem_inc(made["messages"], 1)

            @block.sync
            def _(sp):
                sp.wait_ge(made["starts"], 1)
                for n, name in enumerate(("dst", "node")):
                    sp.dma_start(starts_d[n, :].rearrange("(p l) -> p l", p=DIGIT), start_i[name][:, :]).then_inc(starts_out, 16)
                sp.wait_ge(starts_out, 32)
                sp.dma_start(starts[:, :, :], starts_d.unsqueeze(0)).then_inc(loaded["starts"], 16)

                def fetch(g, b):
                    sp.wait_ge(msg["x_used"], g + 1)
                    sp.sem_inc(paced["sp"], 1)
                    sp.dma_start(xb[b][:, :, :], x_of_src[:, bass.ds(g * GT, GT), :]).then_inc(x_msg[b], 16)

                def store(g, b):
                    sp.wait_ge(msg["row"], g + 1)
                    sp.sem_inc(paced["sp"], 1)
                    sp.dma_start(message_pt[:, bass.ds(g * GT, GT), :], m_row[b][:, :, :]).then_inc(msg_out[b], 16)

                sp.sem_inc(msg["x_used"], 2)
                prime(sp, msg_out)
                fetch(0, 0)
                with sp.Fori(0, FG // 2) as i:
                    for b in range(2):
                        fetch(i * 2 + (b + 1), 1 - b)
                        store(i * 2 + b, b)
                sp.wait_ge(msg["row"], MG)
                sp.dma_start(message_pt[:, FG * GT:FT, :], m_row[0][:, 0:RT, :]).then_inc(msg_out[0], 16)
                sp.dma_start(message[FT * P:E, :], m_row[0][0:TAIL, RT, :]).then_inc(msg_out[0], 16)
                sp.wait_ge(msg_out[0], 16 * (FG // 2 + 3))
                sp.wait_ge(msg_out[1], 16 * (FG // 2 + 1))
                sp.sem_inc(made["messages"], 1)
                sp.wait_ge(loaded["starts"], 16)
                with sp.If(sp.value_load(unsorted_i[0:1, 0:1], min_val=0, max_val=1) > 0):
                    sp.wait_ge(made["messages"], 2)
                    sp.sem_inc(paced["sp"], 1)
                with sp.Else():
                    sp.sem_inc(paced["sp"], 1)
                load_windows(sp, l0, 0, x, message)

            @block.vector
            def _(dve):
                own = own_waits(dve, "dve")

                def step(g, b, count, first=False):
                    dve.wait_ge(x_msg[b], count * 16)
                    norm_centre(own, b)
                    nc.vector.tensor_copy(m_key[b][:, :], dst_f[:, bass.ds(g * GT, GT)])
                    norm_sum(dve, b, g + 1)
                    norm_scale(dve, own, b, g + 1, ew[:, bass.ds(g * GT, GT)]).then_inc(msg["h"], 1)
                    dve.sem_inc(msg["x_used"], 1)

                with dve.Fori(0, FG // 2) as i:
                    own.loop(i, 8)
                    for b in range(2):
                        step(i * 2 + b, b, i + 1)
                    own.end(FG // 2)
                step(FG, 0, FG // 2 + 1)
                own.fold()
                before_if = own.done
                with dve.If(dve.value_load(unsorted_i[0:1, 0:1], min_val=0, max_val=1) > 0):
                    rank_dve(dve, own, r_dst, "dst", idx_msg)
                    own.fold()
                with dve.Else():
                    dve.sem_inc(own.sem, own.done - before_if)

                def finish(g, b, g1, count):
                    dve.wait_ge(l0["o_ps"], g1)
                    dve.wait_ge(l0["y_out"][b], count * 16)
                    own(nc.vector.tensor_tensor(xs[b][:, :, :], xb[b][:, :, :],
                                                ps[1 + b][:, :].rearrange("p (k c) -> p k c", c=D), ALU.add))
                    dve.sem_inc(l0["y"], 1)
                    dve.sem_inc(l0["rows_used"], 1)
                    dve.sem_inc(l0["x_used"], 1)

                def window(g, b, count):
                    own.step(g, 5)
                    dve.wait_ge(l0["x_in"][b], rows_needed(count, g))
                    norm_centre(own, b)
                    dve.wait_ge(l0["rows_in"][b], count * (16 * GT))
                    pick_rows(own, l0, g, b)
                    norm_sum(dve, b, g + (MG + 1))
                    if isinstance(g, int) and g == 0:
                        own.skip()
                    else:
                        finish(g - 1, 1 - b, g, count - (1 - b))
                    norm_scale(dve, own, b, g + (MG + 1), None).then_inc(l0["h"], 1)

                over_windows(dve, window)
                own.steps_end(WG)
                finish(WG - 1, 1, WG, WG // 2)

            @block.tensor
            def _(pe):
                def step(g, b):
                    pe.wait_ge(msg["h"], g + 1)
                    transpose_h(pe, b, msg["hT_ps"])
                    pe.wait_ge(msg["hT"], g + 1)
                    for k in range(4):
                        last = nc.tensor.matmul(ps[1 + b][:, P * k:P * k + P], hT[b][:, k, :], wn2[:, :],
                                                start=True, stop=True)
                    last.then_inc(msg["m_ps"], 1)

                with pe.Fori(0, FG // 2) as i:
                    for b in range(2):
                        step(i * 2 + b, b)
                step(FG, 0)
                pe.wait_ge(msg["row"], MG)
                with pe.If(pe.value_load(unsorted_i[0:1, 0:1], min_val=0, max_val=1) > 0):
                    rank_pe(pe, r_dst)
                with pe.Else():
                    pe.sem_inc(paced["pe"], 1)

                def window(g, b, count):
                    pe.wait_ge(l0["h"], g + 1)
                    transpose_h(pe, b, l0["hT_ps"])
                    pe.wait_ge(l0["pick"], g + 1)
                    pe.wait_ge(l0["hT"], g + 1)
                    for k in range(GT):
                        o = ps[1 + b][:, D * k:D * k + D]
                        half = D * (k % 2)
                        nc.tensor.matmul(o, hT[b][:, k // 2, :], wsT2[:, half:half + D], start=True, stop=False)
                        last = nc.tensor.matmul(o, pick[b][:, 0, k, :], mc[b][:, k, 0:D], start=False, stop=True)
                    last.then_inc(l0["o_ps"], 1)

                over_windows(pe, window)

            @block.scalar
            def _(act):
                own = own_waits(act, "act")

                def step(g, b, count):
                    norm_square(act, b, g + 1)
                    norm_root(act, b, g + 1)
                    act.wait_ge(msg["hT_ps"], g + 1)
                    evacuate_hT(b, msg["hT"])
                    act.wait_ge(msg["m_ps"], g + 1)
                    act.sem_inc(paced["act"], 1)
                    act.wait_ge(msg_out[b], count * 16)
                    act.sem_inc(paced["act"], 1)
                    nc.scalar.activation(m_row[b][:, :, D], m_key[b][:, :], ACT.Copy)
                    nc.scalar.activation(m_row[b][:, :, 0:D], ps[1 + b][:, :].rearrange("p (k c) -> p k c", c=D),
                                         ACT.Copy).then_inc(msg["row"], 1)

                with act.Fori(0, FG // 2) as i:
                    for b in range(2):
                        step(i * 2 + b, b, i + 1)
                step(FG, 0, FG // 2 + 1)
                own.fold()
                done = own.done
                with act.If(act.value_load(unsorted_i[0:1, 0:1], min_val=0, max_val=1) > 0):
                    rank_act(act, own, r_dst)
                    own.fold()
                with act.Else():
                    act.sem_inc(own.sem, own.done - done)
                prime(act, l0["y_out"])

                def window(g, b, count):
                    norm_square(act, b, g + (MG + 1))
                    norm_root(act, b, g + (MG + 1))
                    act.wait_ge(l0["hT_ps"], g + 1)
                    evacuate_hT(b, l0["hT"])
                    if not (isinstance(g, int) and g == 0):
                        store_windows(act, l0, g - 1, 1 - b, g)

                over_windows(act, window)
                store_windows(act, l0, WG - 1, 1, WG)
                act.wait_ge(l0["y_out"][0], 16 * (WG // 2 + 1))
                act.wait_ge(l0["y_out"][1], 16 * (WG // 2 + 2))

        with nc.Block() as block:
            @block.gpsimd
            def _(pool):
                own = own_waits(pool, "pool")
                pool.wait_ge(loaded["lane"], 32)
                scatter_rows(pool, own, r_node, idx_node, by_node.rearrange("p t c -> (p t) c"), sent_node)

            @block.sync
            def _(sp):
                sp.dma_start(rows[:, 0:FT, :], by_lane[:, 0:FT, :]).then_inc(loaded["lane"], 16)
                sp.dma_start(rows[0:TAIL, FT, :], by_lane[0:TAIL, FT, :]).then_inc(loaded["lane"], 16)
                sp.wait_ge(loaded["lane"], 32)

            @block.vector
            def _(dve):
                own = own_waits(dve, "dve")
                dve.wait_ge(loaded["lane"], 32)
                own(nc.vector.tensor_copy(code_i[:, 0:NT], rows[:, :, DE]))
                own(nc.vector.tensor_scalar(code_i[:, :], code_i[:, :], 7, None, ALU.arith_shift_right))
                digits_of(own, "node", code_i)
                rank_dve(dve, own, r_node, "node", idx_node)

            @block.tensor
            def _(pe):
                rank_pe(pe, r_node)

            @block.scalar
            def _(act):
                own = own_waits(act, "act")
                rank_act(act, own, r_node)

        QT = 4
        QG = -(-(FT + 1) // QT)
        QR = FT - (QG - 1) * QT
        q = {n: sem(f"q_{n}") for n in ("staged", "a_ps", "a_used", "s_used", "flags", "scanned", "run", "cnt_ps", "inv",
                                        "inv_ps", "u", "sums", "u_used", "h_ps", "hid", "v_ps", "row")}
        v_out = [sem(f"v_out{b}") for b in range(2)]
        assert QG % 2 == 0 and QG * QT + QT <= NT
        c_ps = [ps[4][:, QT * b:QT * b + QT] for b in range(2)]
        with nc.Block() as block:
            @block.sync
            def _(sp):
                sp.dma_start(rows[:, 0:FT, :], by_node[:, 0:FT, :]).then_inc(loaded["node"], 16)
                sp.dma_start(rows[0:TAIL, FT, :], by_node[0:TAIL, FT, :]).then_inc(loaded["node"], 16)
                sp.wait_ge(made["node_copy"], 1)
                sp.dma_start(near_f[1:P, :], node_f[0:P - 1, :]).then_inc(loaded["shift"], 16)
                sp.dma_start(near_f[0:1, 1:NT], node_f[P - 1:P, 0:NT - 1]).then_inc(loaded["shift"], 16)
                sp.wait_ge(made["sign"], 1)
                sp.dma_start(near_f[0:P - 1, :], node_f[1:P, :]).then_inc(loaded["shift"], 16)
                sp.dma_start(near_f[P - 1:P, 0:NT - 1], node_f[0:1, 1:NT]).then_inc(loaded["shift"], 16)

                def store(g, b):
                    sp.wait_ge(q["row"], g + 1)
                    sp.sem_inc(paced["sp"], 1)
                    sp.dma_start(mlp_row[bass.ds(g * (QT * P), QT * P), :].rearrange("(t p) c -> p t c", p=P),
                                 v_row[b][:, :, :]).then_inc(v_out[b], 16)

                prime(sp, v_out)
                with sp.Fori(0, QG // 2 - 1) as i:
                    for b in range(2):
                        store(i * 2 + b, b)
                store(QG - 2, 0)
                sp.wait_ge(q["row"], QG)
                sp.dma_start(mlp_row[(QG - 1) * QT * P:FT * P, :].rearrange("(t p) c -> p t c", p=P),
                             v_row[1][:, 0:QR, :]).then_inc(v_out[1], 16)
                sp.dma_start(mlp_row[FT * P:E, :], v_row[1][0:TAIL, QR, :]).then_inc(v_out[1], 16)
                sp.wait_ge(v_out[0], 16 * (QG // 2 + 1))
                sp.wait_ge(v_out[1], 16 * (QG // 2 + 2))

            @block.gpsimd
            def _(pool):
                own = own_waits(pool, "pool")

                def stage(g, b):
                    pool.wait_ge(q["a_used"], g + 1)
                    pool.sem_inc(paced["pool"], 1)
                    nc.gpsimd.tensor_copy(
                        s_st[b][:, :, :], sign_b[:, bass.ds(g * QT, QT)].unsqueeze(2).to_broadcast([P, QT, KU]))
                    own(nc.gpsimd.tensor_copy(
                        a_st[b][:, :, 0:2 * DE].rearrange("p t (n c) -> p t n c", n=2),
                        rows[:, bass.ds(g * QT, QT), 0:DE].unsqueeze(2).to_broadcast([P, QT, 2, DE])))
                    pool.sem_inc(q["staged"], 1)

                def sums(g, b):
                    pool.wait_ge(q["run"], g + 1)
                    pool.sem_inc(paced["pool"], 1)
                    pool.wait_ge(q["u_used"], g + 1)
                    pool.sem_inc(paced["pool"], 1)
                    own(nc.gpsimd.tensor_copy(uT[b][0:DE, :], run[b][0:DE, :]))
                    pool.sem_inc(q["sums"], 1)

                pool.wait_ge(made["keys"], 1)
                stage(0, 0)
                with pool.Fori(0, QG // 2) as i:
                    own.loop(i, 4)
                    for b in range(2):
                        stage(i * 2 + (b + 1), 1 - b)
                        sums(i * 2 + b, b)
                    own.end(QG // 2)

            @block.vector
            def _(dve):
                own = own_waits(dve, "dve")
                own(nc.vector.memset(near_f[0:1, 0:1], -3.0))
                dve.wait_ge(loaded["node"], 32)
                own(nc.vector.tensor_copy(node_f[:, :], rows[:, :, DE]))
                dve.sem_inc(made["node_copy"], 1)
                for t in (run[1], uT[1]):
                    own(nc.vector.memset(t[:, :], 0.0))
                dve.wait_ge(loaded["shift"], 32)
                own(nc.vector.tensor_tensor(near_f[:, :], near_f[:, :], node_f[:, :], ALU.is_equal))
                own(nc.vector.tensor_scalar(sign_b[:, :], near_f[:, :], 2.0, -1.0, ALU.mult, ALU.add))
                own(nc.vector.memset(near_f[:, :], -3.0))
                dve.sem_inc(made["sign"], 1)
                dve.wait_ge(loaded["shift"], 64)
                own(nc.vector.tensor_tensor(near_f[:, :], near_f[:, :], node_f[:, :], ALU.is_equal))
                own(nc.vector.tensor_scalar(key_v[:, :], node_f[:, :], 1.0, None, ALU.add))
                own(nc.vector.tensor_tensor(near_f[:, :], near_f[:, :], key_v[:, :], ALU.mult))
                own(nc.vector.tensor_tensor(key_v[:, :], node_f[:, :], near_f[:, :], ALU.subtract))
                dve.sem_inc(made["keys"], 1)

                def mean(g, b, g1):
                    dve.wait_ge(q["inv_ps"], g1)
                    own(nc.vector.tensor_tensor(uT[b][2 * DE:KU, :], run[b][0:DE, :], ps[5][0:DE, :], ALU.mult))
                    dve.sem_inc(q["u"], 1)

                def row(g, b, g1, count):
                    dve.wait_ge(q["v_ps"], g1)
                    dve.wait_ge(v_out[b], count * 16)
                    nc.vector.tensor_copy(v_row[b][:, :, D], key_v[:, bass.ds(g * QT, QT)])
                    own(nc.vector.tensor_tensor(v_row[b][:, :, 0:D], ps[6 + b][:, 0:QT * D].rearrange("p (k c) -> p k c", c=D),
                                                c0b[:, :].unsqueeze(1).to_broadcast([P, QT, D]), ALU.subtract))
                    dve.sem_inc(q["row"], 1)

                def step(g, b, count):
                    own.step(g, 5)
                    first = isinstance(g, int) and g == 0
                    c = 1 - b
                    dve.wait_ge(q["flags"], g + 1)
                    own(nc.vector.tensor_tensor_scan(run[b][:, :], keep[b][:, :], aT[b][:, :], run[c][:, 511:512],
                                                     ALU.mult, ALU.add))
                    dve.sem_inc(q["run"], 1)
                    if first:
                        own.skip()
                    else:
                        mean(g - 1, c, g)
                    own(nc.vector.tensor_tensor_scan(uT[b][DE:2 * DE, :], cut[b][DE:2 * DE, :], aT[b][DE:2 * DE, :],
                                                     uT[c][DE:2 * DE, 511:512], ALU.min, ALU.max))
                    dve.sem_inc(q["scanned"], 1)
                    dve.wait_ge(q["cnt_ps"], g + 1)
                    own(nc.vector.reciprocal(inv[b][:, :], c_ps[b]))
                    dve.sem_inc(q["inv"], 1)
                    if first:
                        own.skip()
                    else:
                        row(g - 1, c, g, count - c)

                own.fold()
                over_steps(dve, QG, step)
                own.steps_end(QG)
                mean(QG - 1, 1, QG)
                row(QG - 1, 1, QG, QG // 2)

            @block.tensor
            def _(pe):
                def transposes(g, b):
                    pe.wait_ge(q["staged"], g + 1)
                    pe.wait_ge(q["s_used"], g + 1)
                    for k in range(QT):
                        nc.tensor.matmul(ps[0][0:KU, P * k:P * k + P], a_st[b][:, k, :], ident[:, :], start=True, stop=True)
                    for k in range(QT):
                        last = nc.tensor.matmul(ps[1][0:KU, P * k:P * k + P], s_st[b][:, k, :], identb[:, :],
                                                start=True, stop=True)
                    last.then_inc(q["a_ps"], 1)

                def hidden(g, b, g1):
                    pe.wait_ge(q["u"], g1)
                    pe.wait_ge(q["sums"], g1)
                    nc.tensor.matmul(ps[2 + b][:, :], w1_sb[:, :], uT[b][:, :], start=True, stop=True).then_inc(q["h_ps"], 1)

                def outer(g, b, g1):
                    pe.wait_ge(q["hid"], g1)
                    for k in range(QT):
                        last = nc.tensor.matmul(ps[6 + b][:, D * k:D * k + D], hid[b][:, P * k:P * k + P], w2_sb[:, :],
                                                start=True, stop=True)
                    last.then_inc(q["v_ps"], 1)

                def step(g, b, count):
                    first = isinstance(g, int) and g == 0
                    pe.wait_ge(q["run"], g + 1)
                    for k in range(QT):
                        last = nc.tensor.matmul(c_ps[b][:, k:k + 1], run[b][2 * DE:2 * DE + 1, P * k:P * k + P],
                                                ones[2 * DE:2 * DE + 1, 0:1], start=True, stop=True)
                    last.then_inc(q["cnt_ps"], 1)
                    if not first:
                        hidden(g - 1, 1 - b, g)
                    transposes(g + 1, 1 - b)
                    pe.wait_ge(q["inv"], g + 1)
                    for k in range(QT):
                        last = nc.tensor.matmul(ps[5][0:DE, P * k:P * k + P], inv[b][:, k:k + 1].to_broadcast([P, DE]),
                                                ident[:, :], start=True, stop=True)
                    last.then_inc(q["inv_ps"], 1)
                    if not first:
                        outer(g - 1, 1 - b, g)

                transposes(0, 0)
                over_steps(pe, QG, step)
                hidden(QG - 1, 1, QG)
                outer(QG - 1, 1, QG)

            @block.scalar
            def _(act):
                own = own_waits(act, "act")
                act.sem_inc(q["a_used"], 2)
                act.sem_inc(q["s_used"], 1)
                act.sem_inc(q["scanned"], 2)
                act.sem_inc(q["u_used"], 2)

                def evacuate(g, b):
                    act.wait_ge(q["a_ps"], g + 1)
                    act.sem_inc(paced["act"], 1)
                    act.wait_ge(q["scanned"], g + 1)
                    act.sem_inc(paced["act"], 1)
                    nc.scalar.activation(aT[b][:, :], ps[0][0:KU, :], ACT.Copy)
                    nc.scalar.activation(keep[b][:, :], ps[1][0:KU, :], ACT.Relu)
                    own(nc.scalar.activation(cut[b][DE:2 * DE, :], ps[1][DE:2 * DE, :], ACT.Copy, scale=FLT_MAX))
                    act.sem_inc(q["flags"], 1)
                    act.sem_inc(q["s_used"], 1)
                    act.sem_inc(q["a_used"], 1)

                def relu(g, b, g1):
                    act.wait_ge(q["h_ps"], g1)
                    act.sem_inc(paced["act"], 1)
                    own(nc.scalar.activation(hid[b][:, :], ps[2 + b][:, :], ACT.Relu, bias=hbias[:, :]))
                    act.sem_inc(q["hid"], 1)
                    act.sem_inc(q["u_used"], 1)

                def step(g, b, count):
                    own.step(g, 2)
                    if isinstance(g, int) and g == 0:
                        own.skip()
                    else:
                        relu(g - 1, 1 - b, g)
                    evacuate(g + 1, 1 - b)

                evacuate(0, 0)
                own.fold()
                over_steps(act, QG, step)
                own.steps_end(QG)
                relu(QG - 1, 1, QG)

        l1 = window_pass("l1")
        with nc.Block() as block:
            @block.sync
            def _(sp):
                load_windows(sp, l1, 1, out, mlp_row)

            @block.gpsimd
            def _(pool):
                own = own_waits(pool, "pool")

                def window(g, b, count):
                    own.step(g, 1)
                    pool.wait_ge(l1["x_in"][b], rows_needed(count, g))
                    pool.sem_inc(paced["pool"], 1)
                    pool.wait_ge(l1["y_out"][b], count * 16)
                    pool.sem_inc(paced["pool"], 1)
                    own(nc.gpsimd.tensor_tensor(xs[b][:, :, :], xb[b][:, :, :],
                                                biasb[:, :].unsqueeze(1).to_broadcast([P, GT, D]), ALU.add))
                    pool.sem_inc(l1["xs"], 1)
                    pool.sem_inc(l1["x_used"], 1)

                own.fold()
                over_windows(pool, window)
                own.steps_end(WG)

            @block.vector
            def _(dve):
                own = own_waits(dve, "dve")

                def finish(g, b, g1):
                    dve.wait_ge(l1["o_ps"], g1)
                    dve.wait_ge(l1["xs"], g1)
                    own(nc.vector.tensor_tensor(xs[b][:, :, :], xs[b][:, :, :],
                                                ps[1 + b][:, :].rearrange("p (k c) -> p k c", c=D), ALU.add))
                    dve.sem_inc(l1["y"], 1)
                    dve.sem_inc(l1["rows_used"], 1)

                def window(g, b, count):
                    own.step(g, 2)
                    dve.wait_ge(l1["rows_in"][b], count * (16 * GT))
                    pick_rows(own, l1, g, b)
                    if isinstance(g, int) and g == 0:
                        own.skip()
                    else:
                        finish(g - 1, 1 - b, g)

                own.fold()
                over_windows(dve, window)
                own.steps_end(WG)
                finish(WG - 1, 1, WG)

            @block.tensor
            def _(pe):
                def window(g, b, count):
                    pe.wait_ge(l1["pick"], g + 1)
                    for k in range(GT):
                        last = nc.tensor.matmul(ps[1 + b][:, D * k:D * k + D], pick[b][:, 0, k, :], mc[b][:, k, 0:D],
                                                start=True, stop=True)
                    last.then_inc(l1["o_ps"], 1)

                over_windows(pe, window)

            @block.scalar
            def _(act):
                prime(act, l1["y_out"])

                def window(g, b, count):
                    store_windows(act, l1, g, b, g + 1)

                over_windows(act, window)
                act.wait_ge(l1["y_out"][0], 16 * (WG // 2 + 1))
                act.wait_ge(l1["y_out"][1], 16 * (WG // 2 + 2))

        tables = (message, mlp_row)
        more = {n: sem(f"more_{n}") for n in ("longest", "in", "near", "pick", "ps", "y", "out")}

        with nc.Block() as block:
            def beyond(eng, body):
                eng.wait_ge(more["longest"], 1)
                with eng.If(eng.value_load(longest[0:1, 0:1], min_val=0, max_val=E) > P):
                    each_beyond(eng, body)
                with eng.Else():
                    pass

            def each_beyond(eng, body):
                n_done = eng.alloc_register(f"further_{eng.engine}".replace(".", "_"))
                eng.reg_mov(n_done, 0)
                for n in range(2):
                    for lo, hi, closing in ((0, NW - 1, False), (NW - 1, NW, True)):
                        with eng.Fori(lo, hi) as v:
                            first = eng.value_load(starts[0:1, n, bass.ds(v, 1)], min_val=0, max_val=(ROWS + E, E)[n])
                            behind = eng.value_load(starts[0:1, n, bass.ds(v + 1, 1)], min_val=0, max_val=(ROWS + E, E)[n])
                            with eng.If(behind - first > P):
                                with eng.Fori(first + P, behind, P) as at:
                                    eng.reg_add(n_done, n_done, 1)
                                    body(n, at, v, closing, eng.snap(n_done))
                            with eng.Else():
                                pass

            @block.sync
            def _(sp):

                def body(n, at, v, closing, count):
                    row0 = N - P if closing else v * P
                    sp.dma_start(mc[0][:, 0, :], tables[n][bass.ds(at, P), :]).then_inc(more["in"], 16)
                    sp.dma_start(xs[0][:, 0, :], out[bass.ds(row0, P), :]).then_inc(more["in"], 16)
                    sp.wait_ge(more["y"], count)
                    sp.sem_inc(paced["sp"], 1)
                    sp.dma_start(out[bass.ds(row0, P), :], xs[0][:, 0, :]).then_inc(more["out"], 16)
                    sp.wait_ge(more["out"], count * 16)
                    sp.sem_inc(paced["sp"], 1)

                beyond(sp, body)

            @block.vector
            def _(dve):
                own = own_waits(dve, "dve")

                def body(n, at, v, closing, count):
                    dve.wait_ge(more["in"], count * 32)
                    if closing:
                        nc.vector.tensor_scalar(near[0][:, 0:1], mc[0][:, 0, D:RM], float(N - P), None,
                                                ALU.subtract).then_inc(more["near"], 1)
                    else:
                        nc.vector.tensor_tensor(near[0][:, 0:1], mc[0][:, 0, D:RM], first_of[:, bass.ds(v, 1)],
                                                ALU.subtract).then_inc(more["near"], 1)
                    dve.wait_ge(more["near"], count)
                    nc.vector.tensor_scalar(pick[0][:, 0, 0, :], iota_n[:, :], near[0][:, 0:1], None,
                                            ALU.is_equal).then_inc(more["pick"], 1)
                    dve.wait_ge(more["ps"], count)
                    nc.vector.tensor_tensor(xs[0][:, 0, :], xs[0][:, 0, :], ps[1][:, 0:D], ALU.add).then_inc(more["y"], 1)

                own(nc.vector.tensor_tensor(counts[:, :, :], starts[:, :, 1:NW + 1], starts[:, :, 0:NW], ALU.subtract))
                own(nc.vector.tensor_reduce(longest[:, :], counts[:, :, :].rearrange("p n l -> p (n l)"), AX, ALU.max))
                dve.sem_inc(more["longest"], 1)
                beyond(dve, body)

            @block.tensor
            def _(pe):
                own = own_waits(pe, "pe")

                def body(n, at, v, closing, count):
                    pe.wait_ge(more["pick"], count)
                    nc.tensor.matmul(ps[1][:, 0:D], pick[0][:, 0, 0, :], mc[0][:, 0, 0:D],
                                     start=True, stop=True).then_inc(more["ps"], 1)

                beyond(pe, body)


_INS = ['x', 'src', 'dst', 'edge_attr_32', 'edge_weight', 'L0_gnn_W_neigh', 'L0_gnn_b_neigh', 'L0_gnn_W_self',
        'L1_gnn_u', 'L1_gnn_W1', 'L1_gnn_b1', 'L1_gnn_W2', 'L1_gnn_b2']
_OUTS = [((100000, 64), 'float32')]


def kernel(**inputs):
    import numpy as _np
    import concourse.bacc as _bacc
    from concourse import mybir as _mybir
    from concourse.bass_utils import run_bass_kernel_spmd as _run

    nc = _bacc.Bacc("TRN2", target_bir_lowering=False, num_devices=1)
    arrays, args = {}, []
    for name in _INS:
        a = _np.ascontiguousarray(inputs[name])
        arrays[f"in_{name}_dram"] = a
        args.append(nc.dram_tensor(f"in_{name}_dram", a.shape, _mybir.dt.from_np(a.dtype), kind="ExternalInput").ap())
    for i, (shape, dtype) in enumerate(_OUTS):
        dt = _mybir.dt.from_np(_np.dtype(dtype))
        args.append(nc.dram_tensor(f"out_{i}_dram", shape, dt, kind="ExternalOutput").ap())
    graph_layers(nc, *args)
    r = _run(nc, [arrays], core_ids=[0])
    return r.results[0]["out_0_dram"]
```

```python
import math
from contextlib import ExitStack

import concourse.bass as bass
from concourse import mybir

F32 = mybir.dt.float32
BF16 = mybir.dt.bfloat16
F16 = mybir.dt.float16
I32 = mybir.dt.int32
U32 = mybir.dt.uint32
ALU = mybir.AluOpType
ACT = mybir.ActivationFunctionType
AX = mybir.AxisListType.X

P = 128
GT = 8
DIGIT = 32
FLT_MAX = 3.4028234663852886e38
EPS = 1e-5


class Own:

    def __init__(self, sem, paced):
        self.sem, self.paced, self.done, self.n, self.at, self.per = sem, paced, 0, 0, None, 0

    def fold(self):
        self.done += self.n
        self.at, self.n = None, 0

    def loop(self, i, per):
        self.fold()
        self.at, self.per = i, per

    def end(self, trips):
        assert self.n == self.per, (self.n, self.per)
        self.done += trips * self.per
        self.at, self.n = None, 0

    def step(self, g, per):
        assert self.at is None or self.n == self.per, (self.n, self.per)
        self.at, self.per, self.n = g, per, 0

    steps_end = end

    def skip(self):
        self.n += 1
        self.eng.sem_inc(self.sem, 1)

    def note(self, ins):
        self.n += 1
        ins.then_inc(self.sem, 1)
        value = self.done + self.n
        return value if self.at is None else self.at * self.per + value

    def __call__(self, ins):
        value = self.note(ins)
        self.eng.wait_ge(self.sem, value)
        if self.paced is not None and not isinstance(value, int):
            self.eng.sem_inc(self.paced, 1)


def graph_layers(nc, x, src, dst, attr, weight, w_neigh, b_neigh, w_self, u, w1, b1, w2, b2, out):
    N, D = x.shape
    E, DE = attr.shape
    HID = w1.shape[1]
    KU = 3 * DE
    FT = E // P
    TAIL = E - FT * P
    NW = -(-N // P)
    LASTN = N - (NW - 1) * P
    NG = 2 * (-(-(FT + 1) // (2 * GT)))
    NT = NG * GT
    FG = FT // GT
    RT = FT - FG * GT
    RE = DE + 1
    PARTS = 3
    KEY = PARTS * D // 2
    RM = KEY + 1
    LANES = DIGIT * DIGIT
    assert D == 64 and DE == 32 and HID == P and 0 < TAIL < P and NW <= LANES and FG % 2 == 0

    ctx = ExitStack()
    with ctx:
        def sb(name, shape, dt=F32):
            return ctx.enter_context(nc.sbuf_tensor(name, shape, dt))

        def sem(name):
            return ctx.enter_context(nc.semaphore(name))

        def dram(name, shape, dt=F32):
            return nc.dram_tensor(name, shape, dt, kind="Internal").ap()

        ROWS = E + P + 48
        by_lane = dram("by_lane", [P, NT, RE])
        by_node = dram("by_node", [P, NT, RE])
        message = dram("message", [2 * ROWS, RM])
        x_of_src = dram("x_of_src", [P, NT, D])
        mlp_row = dram("mlp_row", [ROWS, RM])
        spare = dram("spare", [16, 1])
        starts_d = dram("starts_d", [2, LANES], I32)

        ident = sb("ident", [P, P])
        identb = sb("identb", [P, P], BF16)
        identh = sb("identh", [P, P], F16)
        later = sb("later", [P, P], F16)
        before = sb("before", [P, DIGIT])
        iota_d = sb("iota_d", [P, DIGIT], BF16)
        iota_n = sb("iota_n", [P, P])
        first_of = sb("first_of", [P, NW + GT])
        chain_mask = sb("chain_mask", [DIGIT, DIGIT, GT + 1])
        ones = sb("ones", [P, 512])
        eps_t = sb("eps_t", [P, 1])
        root_eps = sb("root_eps", [P, 1])

        wn2 = sb("wn2", [P, P])
        ws_raw = sb("ws_raw", [D, 2, D])
        wsT2 = sb("wsT2", [P, P])
        w1_sb = sb("w1_sb", [KU, HID])
        w1u = sb("w1u", [P, 1])
        u0 = sb("u0", [P, 1])
        b1c = sb("b1c", [P, 1])
        hbias = sb("hbias", [P, 1])
        hrelu = sb("hrelu", [P, 1])
        hrelu_b = sb("hrelu_b", [P, P])
        w2_sb = sb("w2_sb", [P, D])
        b2b = sb("b2b", [P, D])
        bnb = sb("bnb", [P, D])
        c0b = sb("c0b", [P, D])
        biasb = sb("biasb", [P, D])

        src_i = sb("src_i", [P, NT + GT], I32)
        dst_i = sb("dst_i", [P, NT + GT], I32)
        ew = sb("ew", [P, NT])
        src_f = sb("src_f", [P, NT])
        dst_f = sb("dst_f", [P, NT])
        node_f = sb("node_f", [P, NT])
        near_f = sb("near_f", [P, NT])
        sign_b = sb("sign_b", [P, NT], BF16)
        key_v = sb("key_v", [P, NT])
        next_i = sb("next_i", [P, NT], I32)
        code_i = sb("code_i", [P, NT + GT], I32)
        digit_i = sb("digit_i", [P, NT + GT], I32)
        CODES = ("lane", "dst", "node")
        code_h = {n: sb(f"code_h_{n}", [P, NT + GT], F16) for n in CODES}
        hi_b = {n: sb(f"hi_b_{n}", [P, NT + GT], BF16) for n in CODES}
        lo_b = {n: sb(f"lo_b_{n}", [P, NT + GT], BF16) for n in CODES}
        idx_lane = sb("idx_lane", [P, NT], U32)
        idx_node = sb("idx_node", [P, NT], U32)
        idx_msg = sb("idx_msg", [P, NT], U32)
        idx_src = sb("idx_src", [P, NT], U32)
        rows = sb("rows", [P, NT, RE])

        oh_hi = [sb(f"oh_hi{b}", [P, 3, GT, DIGIT], BF16) for b in range(2)]
        oh_lo = [sb(f"oh_lo{b}", [P, 3, GT, DIGIT], BF16) for b in range(2)]
        code_s = [sb(f"code_s{b}", [P, GT], F16) for b in range(2)]
        ohT = [sb(f"ohT{b}", [DIGIT, GT, P], BF16) for b in range(2)]
        hist = [sb(f"hist{b}", [DIGIT, DIGIT, GT + 1]) for b in range(2)]
        begin = [sb(f"begin{b}", [DIGIT, DIGIT, GT + 1]) for b in range(2)]
        begin_p = [sb(f"begin_p{b}", [DIGIT, 2, DIGIT, GT + 1], BF16) for b in range(2)]
        same = [sb(f"same{b}", [P, GT, P], BF16) for b in range(2)]
        pos_base = sb("pos_base", [P, GT])
        pos_i = sb("pos_i", [P, GT], I32)
        pos_part = sb("pos_part", [P, 2, GT], I32)
        ones_b = sb("ones_b", [P, 2], BF16)
        prod = sb("prod", [P, GT, DIGIT])
        total = {n: sb(f"total_{n}", [DIGIT, DIGIT]) for n in CODES}
        row_total = sb("row_total", [DIGIT, 3])
        row_base = sb("row_base", [DIGIT, 3])
        inclusive = {n: sb(f"inclusive_{n}", [DIGIT, DIGIT]) for n in CODES}
        start0 = {n: sb(f"start0_{n}", [DIGIT, DIGIT]) for n in CODES}
        start_i = {n: sb(f"start_i_{n}", [DIGIT, DIGIT], I32) for n in ("dst", "node")}
        falls = sb("falls", [P, 1])
        unsorted_f = sb("unsorted_f", [DIGIT, 1])
        table_off = sb("table_off", [DIGIT, 1])
        unsorted_i = sb("unsorted_i", [1, 1], I32)
        starts = sb("starts", [1, 2, LANES], I32)
        counts = sb("counts", [1, 2, NW], I32)
        longest = sb("longest", [1, 1], I32)

        row_st = [sb(f"row_st{b}", [P, GT, RE]) for b in range(2)]
        idx_st = [sb(f"idx_st{b}", [P, GT], U32) for b in range(2)]
        gx_idx = [sb(f"gx_idx{b}", [P, GT], U32) for b in range(2)]
        xb = [sb(f"xb{b}", [P, GT, D]) for b in range(2)]
        rest = sb("rest", [P, GT, D])
        xc = [sb(f"xc{b}", [P, GT, D]) for b in range(2)]
        sq = sb("sq", [P, GT, D])
        stat = [sb(f"stat{b}", [P, 4, GT]) for b in range(2)]
        h = [sb(f"h{b}", [P, GT, D]) for b in range(2)]
        hT = [sb(f"hT{b}", [P, 4, P]) for b in range(2)]
        m_row = [sb(f"m_row{b}", [P, GT, RM]) for b in range(2)]
        far = sb("far", [P, RM])
        near = [sb(f"near{b}", [P, 2, GT]) for b in range(2)]
        work = [sb(f"work{b}", [P, 2, GT, P]) for b in range(2)]
        pick = [work[b][:, 0, :, :].rearrange("p k c -> p (k c)").bitcast(BF16).rearrange("p (n k c) -> p n k c", n=2, c=P)
                for b in range(2)]
        fill = sb("fill", [ROWS - E >> 1, 2, RM])

        a_st = [sb(f"a_st{b}", [P, 4, KU]) for b in range(2)]
        s_st = [sb(f"s_st{b}", [P, 4, KU], BF16) for b in range(2)]
        aT = [sb(f"aT{b}", [KU, 512]) for b in range(2)]
        inv = [sb(f"inv{b}", [P, 4]) for b in range(2)]
        uT = [sb(f"uT{b}", [KU, 512]) for b in range(2)]
        part = lambda b, n, k: work[b][:, n, k:k + 4, :].rearrange("p k c -> p (k c)")
        hid = [part(b, 0, 0) for b in range(2)]
        run = [part(b, 0, 4)[0:KU, :] for b in range(2)]
        cut = [part(b, 1, 0)[0:KU, :] for b in range(2)]
        keep = [part(b, 1, 4)[0:KU, :] for b in range(2)]
        v_row = [sb(f"v_row{b}", [P, 4, RM]) for b in range(2)]

        ps = [ctx.enter_context(nc.psum_tensor(f"ps{n}", [P, 512], F32)) for n in range(8)]

        paced = {e: sem(f"paced_{e}") for e in ("sp", "pool", "act", "dve", "pe")}
        owns = {e: Own(sem(f"own_{e}"), paced[e] if e in ("pool", "act") else None) for e in ("pool", "act", "dve", "pe")}

        def own_waits(eng, name):
            owns[name].eng = eng
            return owns[name]

        def over_steps(eng, n, step):
            step(0, 0, 1)
            with eng.Fori(0, n // 2 - 1) as i:
                for b in (1, 0):
                    step(i * 2 + (2 - b), b, i + (2 - b))
            step(n - 1, 1, n // 2)

        TRIPS = NG // 2
        h_ps = ps[6][0:DIGIT, 0:256].rearrange("p (k l) -> p k l", l=DIGIT)
        g_ps = ps[7][:, 0:256].rearrange("p (k l) -> p k l", l=DIGIT)
        e_ps = ps[7][:, 256:256 + GT]

        def ranking(name):
            return {s: sem(f"{name}_{s}") for s in (
                "oh", "done", "eq", "same", "h", "h_used", "t", "t_used", "ohT", "w", "begin", "look", "idx")}

        def digits_of(own, name, code):
            nc.vector.tensor_copy(code_h[name][:, :], code[:, :])
            own(nc.vector.tensor_scalar(digit_i[:, :], code[:, :], 5, None, ALU.arith_shift_right))
            own(nc.vector.tensor_copy(hi_b[name][:, :], digit_i[:, :]))
            own(nc.vector.tensor_scalar(digit_i[:, :], code[:, :], DIGIT - 1, None, ALU.bitwise_and))
            own(nc.vector.tensor_copy(lo_b[name][:, :], digit_i[:, :]))

        def one_hots(g, b, name, c):
            grid = iota_d[:, :].unsqueeze(1).to_broadcast([P, GT, DIGIT])
            hi = hi_b[name][:, bass.ds(g * GT, GT)].unsqueeze(2).to_broadcast([P, GT, DIGIT])
            lo = lo_b[name][:, bass.ds(g * GT, GT)].unsqueeze(2).to_broadcast([P, GT, DIGIT])
            nc.vector.tensor_tensor(oh_hi[b][:, c, :, :], grid, hi, ALU.is_equal)
            return nc.vector.tensor_tensor(oh_lo[b][:, c, :, :], grid, lo, ALU.is_equal)

        def ranked_tiles(g, b, name):
            nc.vector.tensor_copy(code_s[b][:, :], code_h[name][:, bass.ds(g * GT, GT)])
            return one_hots(g, b, name, 0)

        def rank_dve(dve, own, r, name, index):
            own(nc.vector.tensor_copy(begin[1][:, :, GT], start0[name][:, :]))
            own(ranked_tiles(0, 0, name))
            dve.sem_inc(r["oh"], 1)
            with dve.Fori(0, TRIPS) as i:
                own.loop(i, 16)
                for b in range(2):
                    g = i * 2 + b
                    dve.wait_ge(r["eq"], g + 1)
                    for half in range(2):
                        last = nc.vector.tensor_tensor(
                            same[b][:, 4 * half:4 * half + 4, :], ps[2 * b + half][:, :].rearrange("p (k c) -> p k c", c=P),
                            code_h[name][:, bass.ds(g * GT + 4 * half, 4)].unsqueeze(2).to_broadcast([P, 4, P]), ALU.is_equal)
                    last.then_inc(r["same"], 1)
                    dve.wait_ge(r["w"], g + 1)
                    own(nc.vector.tensor_copy(hist[b][:, :, 0], begin[1 - b][:, :, GT]))
                    scanned = own.note(nc.vector.tensor_tensor_scan(
                        begin[b][:, :, :].rearrange("p l k -> p (l k)"), chain_mask[:, :, :].rearrange("p l k -> p (l k)"),
                        hist[b][:, :, :].rearrange("p l k -> p (l k)"), 0.0, ALU.mult, ALU.add))
                    ranked_tiles(g + 1, 1 - b, name).then_inc(r["oh"], 1)
                    dve.wait_ge(own.sem, scanned)
                    own(nc.vector.tensor_copy(begin_p[b][:, 0, :, :], begin[b][:, :, :]))
                    nc.vector.tensor_tensor(begin_p[b][:, 1, :, :], begin[b][:, :, :], begin_p[b][:, 0, :, :],
                                            ALU.subtract).then_inc(r["begin"], 1)
                    dve.wait_ge(r["look"], g + 1)
                    own(nc.vector.tensor_tensor(prod[:, :, :], g_ps, oh_lo[b][:, 0, :, :], ALU.mult))
                    own(nc.vector.tensor_reduce(pos_base[:, :], prod[:, :, :], AX, ALU.add))
                    if name == "dst":
                        own(nc.vector.tensor_tensor(pos_i[:, :], pos_base[:, :], e_ps, ALU.add))
                        nc.vector.tensor_copy(pos_part[:, 0, :], pos_i[:, :])
                        own(nc.vector.tensor_copy(pos_part[:, 1, :], pos_i[:, :]))
                        own(nc.vector.tensor_scalar(index[:, bass.ds(g * GT, GT)], pos_i[:, :], float(ROWS), None, ALU.add))
                    else:
                        own(nc.vector.tensor_tensor(pos_i[:, :], pos_base[:, :], e_ps, ALU.add))
                        nc.vector.tensor_scalar(pos_part[:, 0, :], pos_i[:, :], P - 1, None, ALU.bitwise_and)
                        own(nc.vector.tensor_scalar(pos_part[:, 1, :], pos_i[:, :], 7, None, ALU.arith_shift_right))
                        own(nc.vector.scalar_tensor_tensor(index[:, bass.ds(g * GT, GT)], pos_part[:, 0, :], float(NT),
                                                           pos_part[:, 1, :], ALU.mult, ALU.add))
                    dve.sem_inc(r["idx"], 1)
                    dve.sem_inc(r["done"], 1)
                own.end(TRIPS)

        def rank_pe(pe, r):
            with pe.Fori(0, TRIPS) as i:
                for b in range(2):
                    g = i * 2 + b
                    pe.wait_ge(r["oh"], g + 1)
                    pe.wait_ge(r["done"], g + 1)
                    for half in range(2):
                        bank = ps[2 * b + half]
                        nc.tensor.matmul(bank[:, :].rearrange("p (k c) -> p k c", c=P), identh[:, :],
                                         later[:, :].unsqueeze(1).to_broadcast([P, 4, P]), start=True, stop=False)
                        for k in range(4):
                            last = nc.tensor.matmul(
                                bank[:, P * k:P * k + P],
                                code_s[b][:, 4 * half + k:4 * half + k + 1].to_broadcast([P, P]),
                                identh[:, :], start=False, stop=(k == 3))
                    last.then_inc(r["eq"], 1)
                    pe.wait_ge(r["h_used"], g + 1)
                    for k in range(GT):
                        last = nc.tensor.matmul(h_ps[:, k, :], oh_hi[b][:, 0, k, :], oh_lo[b][:, 0, k, :],
                                                start=True, stop=True)
                    last.then_inc(r["h"], 1)
                    pe.wait_ge(r["t_used"], g + 1)
                    for k in range(GT):
                        last = nc.tensor.matmul(ps[4 + k // 4][0:DIGIT, P * (k % 4):P * (k % 4) + P],
                                                oh_hi[b][:, 0, k, :], identb[:, :], start=True, stop=True)
                    last.then_inc(r["t"], 1)
                    pe.wait_ge(r["same"], g + 1)
                    for k in range(GT):
                        nc.tensor.matmul(e_ps[:, k:k + 1], same[b][:, k, :], ones_b[:, 0:1], start=True, stop=True)
                    pe.wait_ge(r["ohT"], g + 1)
                    pe.wait_ge(r["begin"], g + 1)
                    for k in range(GT):
                        for part in range(2):
                            last = nc.tensor.matmul(g_ps[:, k, :], ohT[b][:, k, :], begin_p[b][:, part, :, k],
                                                    start=(part == 0), stop=(part == 1))
                    last.then_inc(r["look"], 1)

        def rank_act(act, own, r, stage=None):
            act.sem_inc(r["done"], 2)
            act.sem_inc(r["t_used"], 1)
            act.sem_inc(r["h_used"], 1)
            own.fold()

            def step(g, b, count):
                own.step(g, 2 + (stage is not None))
                act.wait_ge(r["h"], g + 1)
                act.sem_inc(paced["act"], 1)
                act.wait_ge(r["done"], g + 1)
                act.sem_inc(paced["act"], 1)
                own(nc.scalar.activation(hist[b][:, :, 1:GT + 1], h_ps.rearrange("p k l -> p l k"), ACT.Copy))
                act.sem_inc(r["w"], 1)
                act.sem_inc(r["h_used"], 1)
                act.wait_ge(r["t"], g + 1)
                act.sem_inc(paced["act"], 1)
                nc.scalar.activation(ohT[b][:, 0:4, :], ps[4][0:DIGIT, :].rearrange("p (k c) -> p k c", c=P), ACT.Copy)
                own(nc.scalar.activation(ohT[b][:, 4:8, :], ps[5][0:DIGIT, :].rearrange("p (k c) -> p k c", c=P), ACT.Copy))
                act.sem_inc(r["ohT"], 1)
                act.sem_inc(r["t_used"], 1)
                if stage is not None:
                    if isinstance(g, int) and g == 0:
                        own.skip()
                    else:
                        stage(g - 1, 1 - b, count - (1 - b))

            over_steps(act, NG, step)
            own.steps_end(NG)

        spare_rows = list(range(spare.shape[0]))

        def prime(eng, sems):
            for s in sems:
                n = spare_rows.pop()
                eng.dma_start(spare[n:n + 1, :], eps_t[0:1, 0:1]).then_inc(s, 16)
                eng.wait_ge(s, 16)

        def stage_rows(act, own, index, sc, g, b, count):
            act.wait_ge(sc["sent"][b], (count - 1) * (16 * GT) + 16)
            act.sem_inc(paced["act"], 1)
            nc.scalar.activation(idx_st[b][:, :], index[:, bass.ds(g * GT, GT)], ACT.Copy)
            own(nc.scalar.activation(row_st[b][:, :, :], rows[:, bass.ds(g * GT, GT), :], ACT.Copy))
            act.sem_inc(sc["staged"], 1)

        def scatter_rows(pool, table, sc):
            def send(b, k, parts):
                nc.gpsimd.indirect_dma_start(
                    out=table, out_offset=bass.IndirectOffsetOnAxis(ap=idx_st[b][0:parts, k:k + 1], axis=0),
                    in_=row_st[b][0:parts, k, :], in_offset=None).then_inc(sc["sent"][b], 16)

            prime(pool, sc["sent"])
            with pool.Fori(0, FG // 2) as i:
                for b in range(2):
                    pool.wait_ge(sc["staged"], i * 2 + (b + 1))
                    pool.sem_inc(paced["pool"], 1)
                    for k in range(GT):
                        send(b, k, P)
            pool.wait_ge(sc["staged"], FG + 1)
            for k in range(RT):
                send(0, k, P)
            send(0, RT, TAIL)
            pool.wait_ge(sc["sent"][0], FG // 2 * 16 * GT + 16 + 16 * (RT + 1))
            pool.wait_ge(sc["sent"][1], FG // 2 * 16 * GT + 16)

        ln = {s: sem(f"ln_{s}") for s in ("centred", "squared", "summed", "root")}

        def wide(a):
            return a.unsqueeze(2).to_broadcast([P, GT, D])

        def norm_centre(own, b, x):
            own(nc.vector.tensor_reduce(stat[b][:, 0, :], x[:, :, :], AX, ALU.add))
            own(nc.vector.tensor_scalar(stat[b][:, 1, :], stat[b][:, 0, :], 1.0 / D, None, ALU.mult))
            nc.vector.tensor_tensor(xc[b][:, :, :], x[:, :, :], wide(stat[b][:, 1, :]),
                                    ALU.subtract).then_inc(ln["centred"], 1)

        def norm_sum(dve, b, count):
            dve.wait_ge(ln["squared"], count)
            nc.vector.tensor_reduce(stat[b][:, 3, :], sq[:, :, :], AX, ALU.add).then_inc(ln["summed"], 1)

        def norm_scale(dve, own, b, count, scale):
            dve.wait_ge(ln["root"], count)
            own(nc.vector.reciprocal(stat[b][:, 2, :], stat[b][:, 3, :]))
            if scale is not None:
                own(nc.vector.tensor_tensor(stat[b][:, 2, :], stat[b][:, 2, :], scale, ALU.mult))
            return nc.vector.scalar_tensor_tensor(h[b][:, :, :], xc[b][:, :, :], 0.0, wide(stat[b][:, 2, :]),
                                                  ALU.max, ALU.mult)

        def norm_square(act, b, count):
            act.wait_ge(ln["centred"], count)
            nc.scalar.activation(sq[:, :, :], xc[b][:, :, :], ACT.Square).then_inc(ln["squared"], 1)

        def norm_root(act, b, count):
            act.wait_ge(ln["summed"], count)
            nc.scalar.activation(stat[b][:, 3, :], stat[b][:, 3, :], ACT.Sqrt, bias=eps_t[:, :],
                                 scale=1.0 / D).then_inc(ln["root"], 1)

        def transpose_h(pe, b, done):
            for k in range(4):
                last = nc.tensor.transpose(ps[3 * b][:, P * k:P * k + P],
                                           h[b][:, 2 * k:2 * k + 2, :].rearrange("p a c -> p (a c)"), ident[:, :])
            last.then_inc(done, 1)

        def evacuate_hT(b, done):
            nc.scalar.activation(hT[b][:, :, :], ps[3 * b][:, :].rearrange("p (k c) -> p k c", c=P), ACT.Copy).then_inc(done, 1)

        def split(own, row, value, left):
            part = row[:, :, 0:KEY].bitcast(BF16).rearrange("p k (s c) -> p k s c", s=PARTS)
            own(nc.vector.tensor_copy(part[:, :, 0, :], value))
            own(nc.vector.tensor_tensor(left, value, part[:, :, 0, :], ALU.subtract))
            own(nc.vector.tensor_copy(part[:, :, 1, :], left))
            return nc.vector.tensor_tensor(part[:, :, 2, :], left, part[:, :, 1, :], ALU.subtract)

        loaded = {n: sem(f"loaded_{n}") for n in ("weights", "src", "edges", "attr", "lane", "node", "starts", "shift")}
        made = {n: sem(f"made_{n}") for n in ("const", "pads", "wsT_ps", "wsT", "c0_ps", "hbias", "c0", "srcs",
                                              "node_copy", "sign", "keys", "starts", "messages")}
        starts_out = sem("starts_out")
        filled = sem("filled")
        to_lane, to_node = ({"staged": sem(f"{n}_staged"), "sent": [sem(f"{n}_sent{b}") for b in range(2)]}
                            for n in ("lane_rows", "node_rows"))
        r_lane, r_dst, r_node = ranking("lane"), ranking("dst"), ranking("node")
        hg = {s: sem(f"hist_{s}") for s in ("oh", "used", "rows", "base")}
        ATTR_LOADS = FG // 2 + 2
        MG = FG + 1
        gathered = [sem(f"gathered{b}") for b in range(2)]
        x_kept = [sem(f"x_kept{b}") for b in range(2)]

        def edge_load(eng, tile, source, what):
            eng.dma_start(tile[:, 0:FT], source[0:FT * P].rearrange("(p t) -> p t", p=P)).then_inc(loaded[what], 16)
            eng.dma_start(tile[0:TAIL, FT:FT + 1],
                          source[FT * P:E].rearrange("(p o) -> p o", o=1)).then_inc(loaded[what], 16)

        with nc.Block() as block:
            @block.sync
            def _(sp):
                sp.wait_ge(made["pads"], 1)
                edge_load(sp, src_i, src, "src")
                edge_load(sp, dst_i, dst, "edges")
                edge_load(sp, ew, weight, "edges")
                sp.dma_start(next_i[:, 0:FT], dst[1:FT * P + 1].rearrange("(p t) -> p t", p=P)).then_inc(loaded["edges"], 16)
                sp.dma_start(next_i[0:TAIL - 1, FT:FT + 1],
                             dst[FT * P + 1:E].rearrange("(p o) -> p o", o=1)).then_inc(loaded["edges"], 16)
                sp.dma_start(wn2[0:D, 0:D], w_neigh).then_inc(loaded["weights"], 16)
                sp.dma_start(wn2[D:P, D:P], w_neigh).then_inc(loaded["weights"], 16)
                for n in range(2):
                    sp.dma_start(ws_raw[:, n, :], w_self).then_inc(loaded["weights"], 16)
                sp.dma_start(w1_sb[:, :], w1[0:KU, :]).then_inc(loaded["weights"], 16)
                sp.dma_start(w1u[:, :], w1[KU, :].rearrange("(p o) -> p o", o=1)).then_inc(loaded["weights"], 16)
                sp.dma_start(b1c[:, :], b1.rearrange("(p o) -> p o", o=1)).then_inc(loaded["weights"], 16)
                sp.dma_start(u0[:, :], u[0:1, :].to_broadcast([P, 1])).then_inc(loaded["weights"], 16)
                sp.dma_start(w2_sb[:, :], w2).then_inc(loaded["weights"], 16)
                sp.dma_start(b2b[:, :], b2.unsqueeze(0).to_broadcast([P, D])).then_inc(loaded["weights"], 16)
                sp.dma_start(bnb[:, :], b_neigh.unsqueeze(0).to_broadcast([P, D])).then_inc(loaded["weights"], 16)
                for table in (message[E:ROWS, :], message[ROWS + E:2 * ROWS, :], mlp_row[E:ROWS, :]):
                    sp.dma_start(table.rearrange("(p a) c -> p a c", a=2), fill[:, :, :]).then_inc(filled, 16)

                def keep(g, b, count):
                    sp.wait_ge(gathered[b], count * (16 * GT))
                    sp.sem_inc(paced["sp"], 1)
                    sp.dma_start(x_of_src[:, bass.ds(g * GT, GT), :], xb[b][:, :, :]).then_inc(x_kept[b], 16)

                sp.wait_ge(made["const"], 1)
                prime(sp, x_kept)
                attr_pt = attr[0:FT * P, :].rearrange("(p t) c -> p t c", p=P)
                with sp.Fori(0, FG // 2) as i:
                    sp.dma_start(rows[:, bass.ds(i * (2 * GT), 2 * GT), 0:DE],
                                 attr_pt[:, bass.ds(i * (2 * GT), 2 * GT), :]).then_inc(loaded["attr"], 16)
                    for b in range(2):
                        keep(i * 2 + b, b, i + 1)
                sp.dma_start(rows[:, FG * GT:FT, 0:DE], attr_pt[:, FG * GT:FT, :]).then_inc(loaded["attr"], 16)
                sp.dma_start(rows[0:TAIL, FT, 0:DE], attr[FT * P:E, :]).then_inc(loaded["attr"], 16)
                keep(FG, 0, FG // 2 + 1)
                sp.wait_ge(x_kept[0], 16 * (FG // 2 + 2))
                sp.wait_ge(x_kept[1], 16 * (FG // 2 + 1))
                sp.wait_ge(loaded["weights"], 16 * 11)
                sp.wait_ge(loaded["edges"], 16 * 6)
                sp.wait_ge(loaded["attr"], ATTR_LOADS * 16)
                sp.wait_ge(filled, 16 * 3)

            @block.gpsimd
            def _(pool):
                own = own_waits(pool, "pool")
                nc.gpsimd.memset(src_i[:, :], -1)
                nc.gpsimd.memset(dst_i[:, :], -1)
                nc.gpsimd.memset(code_i[:, :], -1)
                nc.gpsimd.memset(next_i[:, :], N)
                nc.gpsimd.memset(ew[:, :], 0.0)
                nc.gpsimd.memset(wn2[:, :], 0.0)
                nc.gpsimd.memset(wsT2[:, :], 0.0)
                nc.gpsimd.memset(fill[:, :, :], 0.0)
                own(nc.gpsimd.memset(rows[:, FT:NT, :], 0.0))
                own(nc.gpsimd.memset(fill[:, :, KEY:RM], -1.0))
                pool.sem_inc(made["pads"], 1)
                for t, full in ((ident, False), (identb, False), (identh, False), (later, True)):
                    own(nc.gpsimd.memset(t[:, :], 2048.0 if full else 0.0))
                    if full:
                        own(nc.gpsimd.affine_select(out=t[:, :], in_=t[:, :], compare_op=ALU.is_ge, fill=0.0,
                                                    base=0, pattern=[[-1, P]], channel_multiplier=1))
                    else:
                        own(nc.gpsimd.affine_select(out=t[:, :], in_=t[:, :], compare_op=ALU.not_equal, fill=1.0,
                                                    base=0, pattern=[[-1, P]], channel_multiplier=1))
                own(nc.gpsimd.memset(before[:, :], 1.0))
                own(nc.gpsimd.affine_select(out=before[:, :], in_=before[:, :], compare_op=ALU.is_gt, fill=0.0,
                                            base=0, pattern=[[1, DIGIT]], channel_multiplier=-1))
                for t, pattern in ((iota_d, [[1, DIGIT]]), (iota_n, [[1, P]]), (first_of, [[P, NW + GT]])):
                    own(nc.gpsimd.iota(t[:, :], pattern, base=0, channel_multiplier=0,
                                       allow_small_or_imprecise_dtypes=True))
                own(nc.gpsimd.memset(chain_mask[:, :, :], 1.0))
                own(nc.gpsimd.memset(chain_mask[:, :, 0:1], 0.0))
                own(nc.gpsimd.memset(eps_t[:, :], EPS))
                own(nc.gpsimd.memset(ones[:, :], 1.0))
                own(nc.gpsimd.memset(ones_b[:, :], 1.0))
                for b in range(2):
                    own(nc.gpsimd.memset(a_st[b][:, :, :], 1.0))
                pool.sem_inc(made["const"], 3)

                def gather(g, b, count):
                    pool.wait_ge(x_kept[b], count * 16)
                    pool.sem_inc(paced["pool"], 1)
                    own(nc.gpsimd.tensor_copy(gx_idx[b][:, :], idx_src[:, bass.ds(g * GT, GT)]))
                    for k in range(GT):
                        nc.gpsimd.indirect_dma_start(
                            out=xb[b][:, k, :], out_offset=None, in_=x,
                            in_offset=bass.IndirectOffsetOnAxis(ap=gx_idx[b][:, k:k + 1], axis=0)).then_inc(gathered[b], 16)

                pool.wait_ge(made["srcs"], 1)
                with pool.Fori(0, FG // 2) as i:
                    own.loop(i, 2)
                    for b in range(2):
                        gather(i * 2 + b, b, i + 1)
                    own.end(FG // 2)
                gather(FG, 0, FG // 2 + 1)

            @block.vector
            def _(dve):
                own = own_waits(dve, "dve")
                dve.wait_ge(loaded["src"], 32)
                own(nc.vector.tensor_scalar(idx_src[:, :], src_i[:, 0:NT], 0.0, None, ALU.max))
                dve.sem_inc(made["srcs"], 1)
                dve.wait_ge(loaded["edges"], 16 * 6)
                dve.wait_ge(made["const"], 1)
                nc.vector.tensor_scalar(code_i[:, 0:FT], src_i[:, 0:FT], P - 1, None, ALU.bitwise_and)
                own(nc.vector.tensor_scalar(code_i[0:TAIL, FT:FT + 1], src_i[0:TAIL, FT:FT + 1], P - 1, None,
                                            ALU.bitwise_and))
                digits_of(own, "lane", code_i)
                own(nc.vector.tensor_scalar(code_i[:, :], src_i[:, :], 7, None, ALU.arith_shift_right))
                digits_of(own, "node", code_i)
                own(nc.vector.tensor_scalar(code_i[:, :], dst_i[:, :], 7, None, ALU.arith_shift_right))
                digits_of(own, "dst", code_i)
                own(nc.vector.tensor_scalar(next_i[:, :], next_i[:, :], 7, None, ALU.arith_shift_right))
                own(nc.vector.tensor_tensor(near_f[:, :], next_i[:, :], code_i[:, 0:NT], ALU.is_lt))
                own(nc.vector.tensor_reduce(falls[:, :], near_f[:, :], AX, ALU.add))
                nc.vector.tensor_copy(src_f[:, :], src_i[:, 0:NT])
                own(nc.vector.tensor_copy(dst_f[:, :], dst_i[:, 0:NT]))
                with dve.Fori(0, TRIPS) as i:
                    for b in range(2):
                        g = i * 2 + b
                        dve.wait_ge(hg["used"], g + 1)
                        for c, name in enumerate(CODES):
                            last = one_hots(g, b, name, c)
                        last.then_inc(hg["oh"], 1)
                dve.wait_ge(hg["used"], NG + 2)
                for c, name in enumerate(CODES):
                    own(nc.vector.tensor_copy(total[name][:, :], ps[c][0:DIGIT, 0:DIGIT]))
                    own(nc.vector.tensor_reduce(row_total[:, c:c + 1], total[name][:, :], AX, ALU.add))
                dve.sem_inc(hg["rows"], 1)
                dve.wait_ge(hg["base"], 1)
                nc.vector.tensor_scalar(unsorted_f[:, :], ps[4][0:DIGIT, 0:1], 1.0, None, ALU.min)
                own(nc.vector.tensor_copy(row_base[:, :], ps[3][0:DIGIT, 0:3]))
                nc.vector.tensor_scalar(table_off[:, :], unsorted_f[:, :], float(ROWS), None, ALU.mult)
                nc.vector.tensor_copy(unsorted_i[:, :], unsorted_f[0:1, :])
                for c, name in enumerate(CODES):
                    own(nc.vector.tensor_tensor_scan(inclusive[name][:, :], ones[0:DIGIT, 0:DIGIT], total[name][:, :],
                                                     row_base[:, c:c + 1], ALU.mult, ALU.add))
                    own(nc.vector.tensor_tensor(start0[name][:, :], inclusive[name][:, :], total[name][:, :], ALU.subtract))
                nc.vector.tensor_scalar(start_i["dst"][:, :], start0["dst"][:, :], table_off[:, :], None, ALU.add)
                own(nc.vector.tensor_copy(start_i["node"][:, :], start0["node"][:, :]))
                dve.sem_inc(made["starts"], 1)
                rank_dve(dve, own, r_lane, "lane", idx_lane)
                dve.wait_ge(loaded["weights"], 16 * 11)
                own(nc.vector.tensor_tensor(hbias[:, :], w1u[:, :], u0[:, :], ALU.mult))
                own(nc.vector.tensor_tensor(hbias[:, :], hbias[:, :], b1c[:, :], ALU.add))
                own(nc.vector.tensor_scalar(hrelu[:, :], hbias[:, :], 0.0, None, ALU.max))
                own(nc.vector.tensor_copy(hrelu_b[:, :], hrelu[:, :].to_broadcast([P, P])))
                dve.sem_inc(made["hbias"], 1)
                dve.wait_ge(made["wsT_ps"], 1)
                for half in (0, D):
                    own(nc.vector.tensor_copy(wsT2[half:half + D, half:half + D], ps[0][half:half + D, 0:D]))
                dve.wait_ge(made["c0_ps"], 1)
                own(nc.vector.tensor_copy(c0b[:, :], ps[1][:, 0:D]))
                own(nc.vector.tensor_tensor(biasb[:, :], b2b[:, :], bnb[:, :], ALU.add))
                own(nc.vector.tensor_tensor(biasb[:, :], biasb[:, :], c0b[:, :], ALU.add))
                dve.wait_ge(loaded["attr"], ATTR_LOADS * 16)
                own(nc.vector.tensor_copy(rows[:, :, DE], src_f[:, :]))

            @block.tensor
            def _(pe):
                def tally(g, b, first=False, final=False):
                    pe.wait_ge(hg["oh"], g + 1)
                    for c in range(3):
                        for k in range(GT):
                            last = nc.tensor.matmul(ps[c][0:DIGIT, 0:DIGIT], oh_hi[b][:, c, k, :], oh_lo[b][:, c, k, :],
                                                    start=(first and k == 0), stop=(final and k == GT - 1))
                    last.then_inc(hg["used"], 1)

                pe.wait_ge(made["const"], 1)
                pe.sem_inc(hg["used"], 2)
                tally(0, 0, first=True)
                with pe.Fori(0, TRIPS - 1) as i:
                    for j in range(2):
                        tally(i * 2 + (j + 1), 1 - j)
                tally(NG - 1, 1, final=True)
                pe.wait_ge(hg["rows"], 1)
                nc.tensor.matmul(ps[3][0:DIGIT, 0:3], before[0:DIGIT, :], row_total[:, :], start=True, stop=True)
                nc.tensor.matmul(ps[4][0:DIGIT, 0:1], ones[:, 0:DIGIT], falls[:, :],
                                 start=True, stop=True).then_inc(hg["base"], 1)
                rank_pe(pe, r_lane)
                pe.wait_ge(loaded["weights"], 16 * 11)
                pe.wait_ge(made["hbias"], 1)
                nc.tensor.matmul(ps[0][:, 0:D], ws_raw[:, :, :].rearrange("p a c -> p (a c)"), ident[0:D, 0:D],
                                 start=True, stop=True).then_inc(made["wsT_ps"], 1)
                nc.tensor.matmul(ps[1][:, 0:D], hrelu_b[:, :], w2_sb[:, :], start=True, stop=True).then_inc(made["c0_ps"], 1)

            @block.scalar
            def _(act):
                own = own_waits(act, "act")
                rank_act(act, own, r_lane)

        msg = {n: sem(f"msg_{n}") for n in ("x_used", "h", "hT_ps", "hT", "m_ps", "row")}
        x_msg = [sem(f"x_msg{b}") for b in range(2)]
        msg_out = [sem(f"msg_out{b}") for b in range(2)]
        again_in, again_out = sem("again_in"), sem("again_out")
        again_own = sem("again_own")
        message_pt = message[0:FT * P, :].rearrange("(p t) c -> p t c", p=P)

        with nc.Block() as block:
            @block.gpsimd
            def _(pool):
                own = own_waits(pool, "pool")
                scatter_rows(pool, by_lane.rearrange("p t c -> (p t) c"), to_lane)
                with pool.If(pool.value_load(unsorted_i[0:1, 0:1], min_val=0, max_val=1) > 0):
                    pool.wait_ge(r_dst["idx"], NG)
                    pool.wait_ge(made["messages"], 1)

                    def resend(g, n_in, count, parts):
                        pool.wait_ge(again_in, n_in)
                        pool.sem_inc(paced["pool"], 1)
                        nc.gpsimd.tensor_copy(idx_st[0][:, :], idx_msg[:, bass.ds(g * GT, GT)]).then_inc(again_own, 1)
                        pool.wait_ge(again_own, g + 1)
                        pool.sem_inc(paced["pool"], 1)
                        for k, part in enumerate(parts):
                            nc.gpsimd.indirect_dma_start(
                                out=message, out_offset=bass.IndirectOffsetOnAxis(ap=idx_st[0][0:part, k:k + 1], axis=0),
                                in_=m_row[0][0:part, k, :], in_offset=None).then_inc(again_out, 16)
                        pool.wait_ge(again_out, count)
                        pool.sem_inc(paced["pool"], 1)

                    with pool.Fori(0, FG) as g:
                        nc.gpsimd.dma_start(m_row[0][:, :, :], message_pt[:, bass.ds(g * GT, GT), :]).then_inc(again_in, 16)
                        resend(g, (g + 1) * 16, (g + 1) * (16 * GT), [P] * GT)
                    nc.gpsimd.dma_start(m_row[0][:, 0:RT, :], message_pt[:, FG * GT:FT, :]).then_inc(again_in, 16)
                    nc.gpsimd.dma_start(m_row[0][0:TAIL, RT, :], message[FT * P:E, :]).then_inc(again_in, 16)
                    resend(FG, (FG + 2) * 16, FG * 16 * GT + 16 * (RT + 1), [P] * RT + [TAIL])
                with pool.Else():
                    pass

            @block.sync
            def _(sp):
                sp.wait_ge(made["starts"], 1)
                for n, name in enumerate(("dst", "node")):
                    sp.dma_start(starts_d[n, :].rearrange("(p l) -> p l", p=DIGIT), start_i[name][:, :]).then_inc(starts_out, 16)
                sp.wait_ge(starts_out, 32)
                sp.dma_start(starts[:, :, :], starts_d.unsqueeze(0)).then_inc(loaded["starts"], 16)

                def fetch(g, b):
                    sp.wait_ge(msg["x_used"], g + 1)
                    sp.sem_inc(paced["sp"], 1)
                    sp.dma_start(xb[b][:, :, :], x_of_src[:, bass.ds(g * GT, GT), :]).then_inc(x_msg[b], 16)

                def store(g, b):
                    sp.wait_ge(msg["row"], g + 1)
                    sp.sem_inc(paced["sp"], 1)
                    sp.dma_start(message_pt[:, bass.ds(g * GT, GT), :], m_row[b][:, :, :]).then_inc(msg_out[b], 16)

                sp.sem_inc(msg["x_used"], 2)
                prime(sp, msg_out)
                fetch(0, 0)
                fetch(1, 1)
                with sp.Fori(0, FG // 2 - 1) as i:
                    for b in range(2):
                        fetch(i * 2 + (b + 2), b)
                        store(i * 2 + b, b)
                fetch(FG, 0)
                store(FG - 2, 0)
                store(FG - 1, 1)
                sp.wait_ge(msg["row"], MG)
                sp.dma_start(message_pt[:, FG * GT:FT, :], m_row[0][:, 0:RT, :]).then_inc(msg_out[0], 16)
                sp.dma_start(message[FT * P:E, :], m_row[0][0:TAIL, RT, :]).then_inc(msg_out[0], 16)
                sp.wait_ge(msg_out[0], 16 * (FG // 2 + 3))
                sp.wait_ge(msg_out[1], 16 * (FG // 2 + 1))
                sp.sem_inc(made["messages"], 1)
                sp.wait_ge(loaded["starts"], 16)

            @block.vector
            def _(dve):
                own = own_waits(dve, "dve")

                def keep(g, b, count):
                    dve.wait_ge(msg["m_ps"], g + 1)
                    dve.wait_ge(msg_out[b], count * 16)
                    nc.vector.tensor_copy(m_row[b][:, :, KEY], dst_f[:, bass.ds(g * GT, GT)])
                    split(own, m_row[b][:, :, :], ps[1 + b][:, :].rearrange("p (k c) -> p k c", c=D),
                          rest[:, :, :]).then_inc(msg["row"], 1)

                def step(g, b, count):
                    own.step(g, 7)
                    dve.wait_ge(x_msg[b], count * 16)
                    norm_centre(own, b, xb[b])
                    norm_sum(dve, b, g + 1)
                    norm_scale(dve, own, b, g + 1, ew[:, bass.ds(g * GT, GT)]).then_inc(msg["h"], 1)
                    dve.sem_inc(msg["x_used"], 1)
                    if isinstance(g, int) and g == 0:
                        for _ in range(3):
                            own.skip()
                    else:
                        keep(g - 1, 1 - b, count - (1 - b))

                own.fold()
                step(0, 0, 1)
                with dve.Fori(0, FG // 2) as i:
                    for b in (1, 0):
                        step(i * 2 + (2 - b), b, i + (2 - b))
                own.steps_end(MG)
                keep(FG, 0, FG // 2 + 1)
                own.fold()
                before_if = own.done
                with dve.If(dve.value_load(unsorted_i[0:1, 0:1], min_val=0, max_val=1) > 0):
                    rank_dve(dve, own, r_dst, "dst", idx_msg)
                    own.fold()
                with dve.Else():
                    dve.sem_inc(own.sem, own.done - before_if)

            @block.tensor
            def _(pe):
                def step(g, b):
                    pe.wait_ge(msg["h"], g + 1)
                    transpose_h(pe, b, msg["hT_ps"])
                    pe.wait_ge(msg["hT"], g + 1)
                    for k in range(4):
                        last = nc.tensor.matmul(ps[1 + b][:, P * k:P * k + P], hT[b][:, k, :], wn2[:, :],
                                                start=True, stop=True)
                    last.then_inc(msg["m_ps"], 1)

                with pe.Fori(0, FG // 2) as i:
                    for b in range(2):
                        step(i * 2 + b, b)
                step(FG, 0)
                pe.wait_ge(msg["row"], MG)
                with pe.If(pe.value_load(unsorted_i[0:1, 0:1], min_val=0, max_val=1) > 0):
                    rank_pe(pe, r_dst)
                with pe.Else():
                    pe.sem_inc(paced["pe"], 1)

            @block.scalar
            def _(act):
                own = own_waits(act, "act")

                def step(g, b, count):
                    norm_square(act, b, g + 1)
                    norm_root(act, b, g + 1)
                    act.wait_ge(msg["hT_ps"], g + 1)
                    evacuate_hT(b, msg["hT"])

                nc.scalar.activation(root_eps[:, :], eps_t[:, :], ACT.Sqrt)
                stage_rows(act, own, idx_lane, to_lane, 0, 0, 1)
                with act.Fori(0, FG // 2) as i:
                    own.loop(i, 2)
                    for b in range(2):
                        step(i * 2 + b, b, i + 1)
                        stage_rows(act, own, idx_lane, to_lane, i * 2 + (b + 1), 1 - b, i + (b + 1))
                    own.end(FG // 2)
                step(FG, 0, FG // 2 + 1)
                own.fold()
                done = own.done
                with act.If(act.value_load(unsorted_i[0:1, 0:1], min_val=0, max_val=1) > 0):
                    rank_act(act, own, r_dst)
                    own.fold()
                with act.Else():
                    act.sem_inc(own.sem, own.done - done)

        with nc.Block() as block:
            @block.gpsimd
            def _(pool):
                own = own_waits(pool, "pool")
                scatter_rows(pool, by_node.rearrange("p t c -> (p t) c"), to_node)

            @block.sync
            def _(sp):
                sp.dma_start(rows[:, 0:FT, :], by_lane[:, 0:FT, :]).then_inc(loaded["lane"], 16)
                sp.dma_start(rows[0:TAIL, FT, :], by_lane[0:TAIL, FT, :]).then_inc(loaded["lane"], 16)
                sp.wait_ge(loaded["lane"], 32)

            @block.vector
            def _(dve):
                own = own_waits(dve, "dve")
                dve.wait_ge(loaded["lane"], 32)
                own(nc.vector.tensor_copy(code_i[:, 0:NT], rows[:, :, DE]))
                own(nc.vector.tensor_scalar(code_i[:, :], code_i[:, :], 7, None, ALU.arith_shift_right))
                digits_of(own, "node", code_i)
                rank_dve(dve, own, r_node, "node", idx_node)

            @block.tensor
            def _(pe):
                rank_pe(pe, r_node)

            @block.scalar
            def _(act):
                own = own_waits(act, "act")

                def stage(g, b, count):
                    act.wait_ge(r_node["idx"], g + 1)
                    act.sem_inc(paced["act"], 1)
                    stage_rows(act, own, idx_node, to_node, g, b, count)

                act.wait_ge(loaded["lane"], 32)
                rank_act(act, own, r_node, stage)

        QT = 4
        QG = -(-(FT + 1) // QT)
        QR = FT - (QG - 1) * QT
        q = {n: sem(f"q_{n}") for n in ("staged", "a_ps", "a_used", "s_used", "flags", "scanned", "run", "cnt_ps", "inv",
                                        "inv_ps", "u", "sums", "h_ps", "hid", "v_ps", "row")}
        v_out = [sem(f"v_out{b}") for b in range(2)]
        assert QG % 2 == 0 and QG * QT + QT <= NT
        c_ps = [ps[4][:, QT * b:QT * b + QT] for b in range(2)]

        def over_edges(eng, step):
            step(0, 0, 1)
            step(1, 1, 1)
            with eng.Fori(0, QG // 2 - 2) as i:
                for b in range(2):
                    step(i * 2 + (2 + b), b, i + 2)
            step(QG - 2, 0, QG // 2)
            step(QG - 1, 1, QG // 2)

        with nc.Block() as block:
            @block.sync
            def _(sp):
                sp.dma_start(rows[:, 0:FT, :], by_node[:, 0:FT, :]).then_inc(loaded["node"], 16)
                sp.dma_start(rows[0:TAIL, FT, :], by_node[0:TAIL, FT, :]).then_inc(loaded["node"], 16)
                sp.wait_ge(made["node_copy"], 1)
                sp.dma_start(near_f[1:P, :], node_f[0:P - 1, :]).then_inc(loaded["shift"], 16)
                sp.dma_start(near_f[0:1, 1:NT], node_f[P - 1:P, 0:NT - 1]).then_inc(loaded["shift"], 16)
                sp.wait_ge(made["sign"], 1)
                sp.dma_start(near_f[0:P - 1, :], node_f[1:P, :]).then_inc(loaded["shift"], 16)
                sp.dma_start(near_f[P - 1:P, 0:NT - 1], node_f[0:1, 1:NT]).then_inc(loaded["shift"], 16)

                def store(g, b):
                    sp.wait_ge(q["row"], g + 1)
                    sp.sem_inc(paced["sp"], 1)
                    sp.dma_start(mlp_row[bass.ds(g * (QT * P), QT * P), :].rearrange("(t p) c -> p t c", p=P),
                                 v_row[b][:, :, :]).then_inc(v_out[b], 16)

                prime(sp, v_out)
                with sp.Fori(0, QG // 2 - 1) as i:
                    for b in range(2):
                        store(i * 2 + b, b)
                store(QG - 2, 0)
                sp.wait_ge(q["row"], QG)
                sp.dma_start(mlp_row[(QG - 1) * QT * P:FT * P, :].rearrange("(t p) c -> p t c", p=P),
                             v_row[1][:, 0:QR, :]).then_inc(v_out[1], 16)
                sp.dma_start(mlp_row[FT * P:E, :], v_row[1][0:TAIL, QR, :]).then_inc(v_out[1], 16)
                sp.wait_ge(v_out[0], 16 * (QG // 2 + 1))
                sp.wait_ge(v_out[1], 16 * (QG // 2 + 2))

            @block.gpsimd
            def _(pool):
                own = own_waits(pool, "pool")

                def stage(g, b):
                    pool.wait_ge(q["a_used"], g + 1)
                    pool.sem_inc(paced["pool"], 1)
                    nc.gpsimd.tensor_copy(
                        s_st[b][:, :, :], sign_b[:, bass.ds(g * QT, QT)].unsqueeze(2).to_broadcast([P, QT, KU]))
                    own(nc.gpsimd.tensor_copy(
                        a_st[b][:, :, 0:2 * DE].rearrange("p t (n c) -> p t n c", n=2),
                        rows[:, bass.ds(g * QT, QT), 0:DE].unsqueeze(2).to_broadcast([P, QT, 2, DE])))
                    pool.sem_inc(q["staged"], 1)

                pool.wait_ge(made["keys"], 1)
                stage(0, 0)
                with pool.Fori(0, QG // 2) as i:
                    own.loop(i, 2)
                    for b in range(2):
                        stage(i * 2 + (b + 1), 1 - b)
                    own.end(QG // 2)

            @block.vector
            def _(dve):
                own = own_waits(dve, "dve")
                own(nc.vector.memset(near_f[0:1, 0:1], -3.0))
                dve.wait_ge(loaded["node"], 32)
                own(nc.vector.tensor_copy(node_f[:, :], rows[:, :, DE]))
                dve.sem_inc(made["node_copy"], 1)
                for t in (run[1], uT[1]):
                    own(nc.vector.memset(t[:, :], 0.0))
                dve.wait_ge(loaded["shift"], 32)
                own(nc.vector.tensor_tensor(near_f[:, :], near_f[:, :], node_f[:, :], ALU.is_equal))
                own(nc.vector.tensor_scalar(sign_b[:, :], near_f[:, :], 2.0, -1.0, ALU.mult, ALU.add))
                own(nc.vector.memset(near_f[:, :], -3.0))
                dve.sem_inc(made["sign"], 1)
                dve.wait_ge(loaded["shift"], 64)
                own(nc.vector.tensor_tensor(near_f[:, :], near_f[:, :], node_f[:, :], ALU.is_equal))
                own(nc.vector.tensor_scalar(key_v[:, :], node_f[:, :], 1.0, None, ALU.add))
                own(nc.vector.tensor_tensor(near_f[:, :], near_f[:, :], key_v[:, :], ALU.mult))
                own(nc.vector.tensor_tensor(key_v[:, :], node_f[:, :], near_f[:, :], ALU.subtract))
                dve.sem_inc(made["keys"], 1)

                def mean(g, b, g1):
                    dve.wait_ge(q["inv_ps"], g1)
                    own(nc.vector.tensor_tensor(uT[b][2 * DE:KU, :], run[b][0:DE, :], ps[5][0:DE, :], ALU.mult))
                    dve.sem_inc(q["u"], 1)

                def row_value(g, b, g1, count):
                    dve.wait_ge(q["v_ps"], g1)
                    dve.wait_ge(v_out[b], count * 16)
                    nc.vector.tensor_copy(v_row[b][:, :, KEY], key_v[:, bass.ds(g * QT, QT)])
                    return own.note(nc.vector.tensor_tensor(
                        sq[:, 0:QT, :], ps[6 + b][:, 0:QT * D].rearrange("p (k c) -> p k c", c=D),
                        c0b[:, :].unsqueeze(1).to_broadcast([P, QT, D]), ALU.subtract))

                def row_parts(b, valued):
                    dve.wait_ge(own.sem, valued)
                    split(own, v_row[b][:, :, :], sq[:, 0:QT, :], rest[:, 0:QT, :]).then_inc(q["row"], 1)

                def step(g, b, count):
                    own.step(g, 8)
                    first = isinstance(g, int) and g == 0
                    c = 1 - b
                    dve.wait_ge(q["flags"], g + 1)
                    own(nc.vector.tensor_tensor_scan(run[b][:, :], keep[b][:, :], aT[b][:, :], run[c][:, 511:512],
                                                     ALU.mult, ALU.add))
                    dve.sem_inc(q["run"], 1)
                    if first:
                        own.skip()
                    else:
                        mean(g - 1, c, g)
                    maxed = own.note(nc.vector.tensor_tensor_scan(
                        uT[b][DE:2 * DE, :], cut[b][DE:2 * DE, :], aT[b][DE:2 * DE, :], uT[c][DE:2 * DE, 511:512],
                        ALU.min, ALU.max))
                    early = isinstance(g, int) and g < 2
                    if early:
                        own.skip()
                    else:
                        valued = row_value(g - 2, b, g - 1, count - 1)
                    dve.wait_ge(own.sem, maxed)
                    dve.sem_inc(q["scanned"], 1)
                    dve.wait_ge(q["cnt_ps"], g + 1)
                    own(nc.vector.reciprocal(inv[b][:, :], c_ps[b]))
                    dve.sem_inc(q["inv"], 1)
                    if early:
                        for _ in range(3):
                            own.skip()
                    else:
                        row_parts(b, valued)

                own.fold()
                over_edges(dve, step)
                own.steps_end(QG)
                mean(QG - 1, 1, QG)
                for b in range(2):
                    row_parts(b, row_value(QG - 2 + b, b, QG - 1 + b, QG // 2))

            @block.tensor
            def _(pe):
                def transposes(g, b):
                    pe.wait_ge(q["staged"], g + 1)
                    pe.wait_ge(q["s_used"], g + 1)
                    for k in range(QT):
                        nc.tensor.matmul(ps[0][0:KU, P * k:P * k + P], a_st[b][:, k, :], ident[:, :], start=True, stop=True)
                    for k in range(QT):
                        last = nc.tensor.matmul(ps[1][0:KU, P * k:P * k + P], s_st[b][:, k, :], identb[:, :],
                                                start=True, stop=True)
                    last.then_inc(q["a_ps"], 1)

                def hidden(g, b, g1):
                    pe.wait_ge(q["u"], g1)
                    pe.wait_ge(q["sums"], g1)
                    nc.tensor.matmul(ps[2 + b][:, :], w1_sb[:, :], uT[b][:, :], start=True, stop=True).then_inc(q["h_ps"], 1)

                def outer(g, b, g1):
                    pe.wait_ge(q["hid"], g1)
                    for k in range(QT):
                        last = nc.tensor.matmul(ps[6 + b][:, D * k:D * k + D], hid[b][:, P * k:P * k + P], w2_sb[:, :],
                                                start=True, stop=True)
                    last.then_inc(q["v_ps"], 1)

                def step(g, b, count):
                    pe.wait_ge(q["run"], g + 1)
                    for k in range(QT):
                        last = nc.tensor.matmul(c_ps[b][:, k:k + 1], run[b][2 * DE:2 * DE + 1, P * k:P * k + P],
                                                ones[2 * DE:2 * DE + 1, 0:1], start=True, stop=True)
                    last.then_inc(q["cnt_ps"], 1)
                    if not (isinstance(g, int) and g < 2):
                        outer(g - 2, b, g - 1)
                    if not (isinstance(g, int) and g == 0):
                        hidden(g - 1, 1 - b, g)
                    pe.wait_ge(q["inv"], g + 1)
                    for k in range(QT):
                        last = nc.tensor.matmul(ps[5][0:DE, P * k:P * k + P], inv[b][:, k:k + 1].to_broadcast([P, DE]),
                                                ident[:, :], start=True, stop=True)
                    last.then_inc(q["inv_ps"], 1)
                    if not (isinstance(g, int) and g == QG - 1):
                        transposes(g + 2, b)

                transposes(0, 0)
                transposes(1, 1)
                over_edges(pe, step)
                outer(QG - 2, 0, QG - 1)
                hidden(QG - 1, 1, QG)
                outer(QG - 1, 1, QG)

            @block.scalar
            def _(act):
                own = own_waits(act, "act")
                act.sem_inc(q["a_used"], 2)
                act.sem_inc(q["s_used"], 1)
                act.sem_inc(q["scanned"], 2)

                def evacuate(g, b):
                    act.wait_ge(q["a_ps"], g + 1)
                    act.sem_inc(paced["act"], 1)
                    act.wait_ge(q["scanned"], g + 1)
                    act.sem_inc(paced["act"], 1)
                    nc.scalar.activation(aT[b][:, :], ps[0][0:KU, :], ACT.Copy)
                    nc.scalar.activation(keep[b][:, :], ps[1][0:KU, :], ACT.Relu)
                    own(nc.scalar.activation(cut[b][DE:2 * DE, :], ps[1][DE:2 * DE, :], ACT.Copy, scale=FLT_MAX))
                    act.sem_inc(q["flags"], 1)
                    act.sem_inc(q["s_used"], 1)
                    act.sem_inc(q["a_used"], 1)

                def relu(g, b, g1):
                    act.wait_ge(q["h_ps"], g1)
                    act.sem_inc(paced["act"], 1)
                    own(nc.scalar.activation(hid[b][:, :], ps[2 + b][:, :], ACT.Relu, bias=hbias[:, :]))
                    act.sem_inc(q["hid"], 1)

                def sums(g, b):
                    act.wait_ge(q["run"], g + 1)
                    act.sem_inc(paced["act"], 1)
                    own(nc.scalar.activation(uT[b][0:DE, :], run[b][0:DE, :], ACT.Copy))
                    act.sem_inc(q["sums"], 1)

                def step(g, b, count):
                    own.step(g, 3)
                    sums(g, b)
                    if isinstance(g, int) and g == 0:
                        own.skip()
                    else:
                        relu(g - 1, 1 - b, g)
                    if isinstance(g, int) and g == QG - 1:
                        own.skip()
                    else:
                        evacuate(g + 2, b)

                evacuate(0, 0)
                evacuate(1, 1)
                own.fold()
                over_edges(act, step)
                own.steps_end(QG)
                relu(QG - 1, 1, QG)

        RING = 4
        WG = -(-NW // GT)
        WF = (N // P) // GT
        WR = N // P - WF * GT
        MEAN = -(-E * P // N)
        CH = min(P, -(-(MEAN + 4 * math.isqrt(MEAN)) // 32) * 32)
        OWN_CHUNKS = 5
        ACT_CHUNKS = GT - OWN_CHUNKS
        AHEAD = RING - 1
        assert WF == WG - 1 and (WG - 2) % RING == 0
        tables = (message, mlp_row)

        def in_rows(at, shape, dt=F32):
            size = shape[0] * shape[1] * (shape[2] if len(shape) > 2 else 1)
            flat = rows[:, :, :].rearrange("p t c -> p (t c)")[:, at:at + size]
            if dt == BF16:
                flat = flat.bitcast(BF16)
            if len(shape) == 2:
                return flat.rearrange("p (k c) -> p k c", k=shape[0])
            return flat.rearrange("p (n k c) -> p n k c", n=shape[0], k=shape[1])

        XW, MW = GT * D, 2 * GT * RM
        x_in = [in_rows(b * XW, (GT, D)) for b in range(RING)]
        y = [in_rows((RING + b) * XW, (GT, D)) for b in range(RING)]
        chunk = [in_rows(2 * RING * XW + b * MW, (2, GT, RM)) for b in range(RING)]
        parts = [in_rows(2 * RING * XW + b * MW, (2, GT, RM), BF16) for b in range(RING)]
        assert 2 * RING * XW + RING * MW <= NT * RE

        w = {n: sem(f"win_{n}") for n in ("x_short", "rows_used", "biased", "pick0", "pick1", "h", "hT_ps", "hT", "o_ps", "y")}
        x_loaded = [sem(f"win_x_loaded{b}") for b in range(RING)]
        rows_loaded = [sem(f"win_rows_loaded{b}") for b in range(RING)]
        own_loaded = [sem(f"win_own_loaded{b}") for b in range(RING)]
        stored = [sem(f"win_stored{b}") for b in range(RING)]

        def over_windows(eng, step, before=2, after=0):
            for g in range(before):
                step(g, g % RING, g // RING + 1)
            with eng.Fori(0, (WG - before - after) // RING) as i:
                for j in range(before, before + RING):
                    step(i * RING + j, j % RING, i + (j // RING + 1))
            for g in range(WG - after, WG):
                step(g, g % RING, g // RING + 1)

        def nodes_of(table, g):
            return table[bass.ds(g * (GT * P), GT * P), :].rearrange("(k p) c -> p k c", p=P)

        def last_nodes(table):
            return (table[WF * GT * P:(WF * GT + WR) * P, :].rearrange("(k p) c -> p k c", p=P), table[N - N % P:N, :])

        with nc.Block() as block:
            @block.sync
            def _(sp):
                at = [sp.alloc_register(f"at{k}") for k in range(GT)]

                def step(g, b, count):
                    sp.reg_load(at, starts[0:1, 0, bass.ds(g * GT, GT)])
                    sp.wait_ge(ln["centred"], g + (MG + 1 - RING))
                    sp.sem_inc(paced["sp"], 1)
                    sp.wait_ge(w["biased"], g + 1)
                    sp.sem_inc(paced["sp"], 1)
                    if isinstance(g, int) and g == WG - 1:
                        full, short = last_nodes(x)
                        sp.dma_start(x_in[b][0:N % P, WR, :], short).then_inc(w["x_short"], 16)
                        sp.wait_ge(w["x_short"], 16)
                        sp.dma_start(x_in[b][:, 0:WR, :], full).then_inc(x_loaded[b], 16)
                    else:
                        sp.dma_start(x_in[b][:, :, :], nodes_of(x, g)).then_inc(x_loaded[b], 16)
                    sp.wait_ge(w["rows_used"], g + 1)
                    sp.sem_inc(paced["sp"], 1)
                    for k in range(GT):
                        sp.dma_start(chunk[b][0:CH, 0, k, :], message[bass.ds(sp.snap(at[k]), CH), :]).then_inc(rows_loaded[b], 16)

                over_windows(sp, step, 1, 1)

            @block.gpsimd
            def _(pool):
                at = [pool.alloc_register(f"own_at{k}") for k in range(OWN_CHUNKS)]
                pool.sem_inc(w["biased"], RING)

                def load(g, b):
                    k0 = GT - OWN_CHUNKS
                    pool.reg_load(at, starts[0:1, 1, bass.ds(g * GT + k0, OWN_CHUNKS)])
                    pool.wait_ge(w["rows_used"], g + 1)
                    pool.sem_inc(paced["pool"], 1)
                    for k in range(OWN_CHUNKS):
                        pool.dma_start(chunk[b][0:CH, 1, k0 + k, :], mlp_row[bass.ds(pool.snap(at[k]), CH), :]).then_inc(own_loaded[b], 16)

                def step(g, b, count):
                    if not (isinstance(g, int) and g + AHEAD >= WG):
                        load(g + AHEAD, (b + AHEAD) % RING)
                    pool.wait_ge(x_loaded[b], count * 16)
                    pool.sem_inc(paced["pool"], 1)
                    pool.wait_ge(stored[b], count * 16)
                    pool.sem_inc(paced["pool"], 1)
                    nc.gpsimd.tensor_tensor(y[b][:, :, :], x_in[b][:, :, :], biasb[:, :].unsqueeze(1).to_broadcast([P, GT, D]),
                                            ALU.add).then_inc(w["biased"], 1)

                for g in range(AHEAD):
                    load(g, g)
                over_windows(pool, step, 0, 2 + RING)

            @block.vector
            def _(dve):
                own = own_waits(dve, "dve")

                def finish(g, b, g1):
                    dve.wait_ge(w["o_ps"], g1)
                    dve.wait_ge(w["biased"], g1 + RING)
                    nc.vector.tensor_tensor(y[b][:, :, :], y[b][:, :, :], ps[4 + b][:, :].rearrange("p (k c) -> p k c", c=D),
                                            ALU.add).then_inc(w["y"], 1)

                def one_hot(n, c):
                    nc.vector.tensor_tensor(pick[c][0:CH, n, :, :], iota_n[0:CH, :].unsqueeze(1).to_broadcast([CH, GT, P]),
                                            near[c][0:CH, n, :].unsqueeze(2).to_broadcast([CH, GT, P]),
                                            ALU.is_equal).then_inc(w[f"pick{n}"], 1)

                def step(g, b, count):
                    own.step(g, 4)
                    c = b % 2
                    dve.wait_ge(x_loaded[b], count * 16)
                    norm_centre(own, c, x_in[b])
                    dve.wait_ge(rows_loaded[b], count * (16 * (2 * GT - OWN_CHUNKS)))
                    dve.wait_ge(own_loaded[b], count * (16 * OWN_CHUNKS))
                    own(nc.vector.tensor_tensor(
                        near[c][0:CH, :, :], chunk[b][0:CH, :, :, KEY],
                        first_of[0:CH, bass.ds(g * GT, GT)].unsqueeze(1).to_broadcast([CH, 2, GT]), ALU.subtract))
                    one_hot(0, c)
                    norm_sum(dve, c, g + (MG + 1))
                    if not (isinstance(g, int) and g < 2):
                        finish(g - 2, (b - 2) % RING, g - 1)
                    one_hot(1, c)
                    norm_scale(dve, own, c, g + (MG + 1), None).then_inc(w["h"], 1)

                own.fold()
                over_windows(dve, step)
                own.steps_end(WG)
                for g in (WG - 2, WG - 1):
                    finish(g, g % RING, g + 1)

            @block.tensor
            def _(pe):
                pe.sem_inc(w["rows_used"], RING)

                def selves(g, b):
                    pe.wait_ge(w["hT"], g + 1)
                    for k in range(4):
                        last = nc.tensor.matmul(ps[4 + b][:, P * k:P * k + P], hT[b % 2][:, k, :], wsT2[:, :],
                                                start=False, stop=(k == 3))
                    last.then_inc(w["o_ps"], 1)

                def step(g, b, count):
                    for n in range(2):
                        if n == 1 and not (isinstance(g, int) and g == 0):
                            selves(g - 1, (b - 1) % RING)
                        pe.wait_ge(w[f"pick{n}"], g + 1)
                        for k in range(GT):
                            for part in range(PARTS):
                                last = nc.tensor.matmul(
                                    ps[4 + b][:, D * k:D * k + D], pick[b % 2][0:CH, n, k, :], parts[b][0:CH, n, k, D * part:D * part + D],
                                    start=(n == 0 and k == 0 and part == 0), stop=False)
                    last.then_inc(w["rows_used"], 1)
                    pe.wait_ge(w["h"], g + 1)
                    transpose_h(pe, b % 2, w["hT_ps"])

                over_windows(pe, step)
                selves(WG - 1, (WG - 1) % RING)

            @block.scalar
            def _(act):
                prime(act, stored)

                def store(g, b, g1):
                    act.wait_ge(w["y"], g1)
                    act.sem_inc(paced["act"], 1)
                    if isinstance(g, int) and g == WG - 1:
                        full, short = last_nodes(out)
                        act.dma_start(full, y[b][:, 0:WR, :]).then_inc(stored[b], 16)
                        act.dma_start(short, y[b][0:N % P, WR, :]).then_inc(stored[b], 16)
                    else:
                        act.dma_start(nodes_of(out, g), y[b][:, :, :]).then_inc(stored[b], 16)

                at = [act.alloc_register(f"act_at{k}") for k in range(ACT_CHUNKS)]

                def load(g, b):
                    act.reg_load(at, starts[0:1, 1, bass.ds(g * GT, ACT_CHUNKS)])
                    act.wait_ge(w["rows_used"], g + 1)
                    act.sem_inc(paced["act"], 1)
                    for k in range(ACT_CHUNKS):
                        act.dma_start(chunk[b][0:CH, 1, k, :], mlp_row[bass.ds(act.snap(at[k]), CH), :]).then_inc(rows_loaded[b], 16)

                def step(g, b, count):
                    norm_square(act, b % 2, g + (MG + 1))
                    norm_root(act, b % 2, g + (MG + 1))
                    if not (isinstance(g, int) and g + AHEAD >= WG):
                        load(g + AHEAD, (b + AHEAD) % RING)
                    if not (isinstance(g, int) and g < 2):
                        store(g - 2, (b - 2) % RING, g - 1)
                    act.wait_ge(w["hT_ps"], g + 1)
                    evacuate_hT(b % 2, w["hT"])

                for g in range(AHEAD):
                    load(g, g)
                over_windows(act, step, 2, RING)
                for g in (WG - 2, WG - 1):
                    store(g, g % RING, g + 1)
                for b in range(RING):
                    steps = len(range(b, WG, RING))
                    act.wait_ge(stored[b], 16 * (steps + 1 + (b == (WG - 1) % RING)))

        more = {n: sem(f"more_{n}") for n in ("longest", "in", "near", "pick", "ps", "y", "out")}

        with nc.Block() as block:
            def beyond(eng, body):
                eng.wait_ge(more["longest"], 1)
                with eng.If(eng.value_load(longest[0:1, 0:1], min_val=0, max_val=E) > CH):
                    each_beyond(eng, body)
                with eng.Else():
                    pass

            def each_beyond(eng, body):
                n_done = eng.alloc_register(f"further_{eng.engine}".replace(".", "_"))
                eng.reg_mov(n_done, 0)
                for n in range(2):
                    for lo, hi, closing in ((0, NW - 1, False), (NW - 1, NW, True)):
                        with eng.Fori(lo, hi) as v:
                            first = eng.value_load(starts[0:1, n, bass.ds(v, 1)], min_val=0, max_val=(ROWS + E, E)[n])
                            behind = eng.value_load(starts[0:1, n, bass.ds(v + 1, 1)], min_val=0, max_val=(ROWS + E, E)[n])
                            with eng.If(behind - first > CH):
                                with eng.Fori(first + CH, behind, CH) as at:
                                    eng.reg_add(n_done, n_done, 1)
                                    body(n, at, v, closing, eng.snap(n_done))
                            with eng.Else():
                                pass

            @block.sync
            def _(sp):

                def body(n, at, v, closing, count):
                    row0 = N - P if closing else v * P
                    sp.dma_start(far[0:CH, :], tables[n][bass.ds(at, CH), :]).then_inc(more["in"], 16)
                    sp.dma_start(rest[:, 0, :], out[bass.ds(row0, P), :]).then_inc(more["in"], 16)
                    sp.wait_ge(more["y"], count)
                    sp.sem_inc(paced["sp"], 1)
                    sp.dma_start(out[bass.ds(row0, P), :], rest[:, 0, :]).then_inc(more["out"], 16)
                    sp.wait_ge(more["out"], count * 16)
                    sp.sem_inc(paced["sp"], 1)

                beyond(sp, body)

            @block.vector
            def _(dve):
                own = own_waits(dve, "dve")

                def body(n, at, v, closing, count):
                    dve.wait_ge(more["in"], count * 32)
                    if closing:
                        nc.vector.tensor_scalar(near[0][0:CH, 0, 0:1], far[0:CH, KEY:RM], float(N - P), None,
                                                ALU.subtract).then_inc(more["near"], 1)
                    else:
                        nc.vector.tensor_tensor(near[0][0:CH, 0, 0:1], far[0:CH, KEY:RM], first_of[0:CH, bass.ds(v, 1)],
                                                ALU.subtract).then_inc(more["near"], 1)
                    dve.wait_ge(more["near"], count)
                    nc.vector.tensor_scalar(pick[0][0:CH, 0, 0, :], iota_n[0:CH, :], near[0][0:CH, 0, 0:1], None,
                                            ALU.is_equal).then_inc(more["pick"], 1)
                    dve.wait_ge(more["ps"], count)
                    nc.vector.tensor_tensor(rest[:, 0, :], rest[:, 0, :], ps[1][:, 0:D], ALU.add).then_inc(more["y"], 1)

                own(nc.vector.tensor_tensor(counts[:, :, :], starts[:, :, 1:NW + 1], starts[:, :, 0:NW], ALU.subtract))
                own(nc.vector.tensor_reduce(longest[:, :], counts[:, :, :].rearrange("p n l -> p (n l)"), AX, ALU.max))
                dve.sem_inc(more["longest"], 1)
                beyond(dve, body)

            @block.tensor
            def _(pe):
                own = own_waits(pe, "pe")

                far_parts = far[:, 0:KEY].bitcast(BF16)

                def body(n, at, v, closing, count):
                    pe.wait_ge(more["pick"], count)
                    for part in range(PARTS):
                        last = nc.tensor.matmul(ps[1][:, 0:D], pick[0][0:CH, 0, 0, :], far_parts[0:CH, D * part:D * part + D],
                                                start=(part == 0), stop=(part == PARTS - 1))
                    last.then_inc(more["ps"], 1)

                beyond(pe, body)


_INS = ['x', 'src', 'dst', 'edge_attr_32', 'edge_weight', 'L0_gnn_W_neigh', 'L0_gnn_b_neigh', 'L0_gnn_W_self',
        'L1_gnn_u', 'L1_gnn_W1', 'L1_gnn_b1', 'L1_gnn_W2', 'L1_gnn_b2']
_OUTS = [((100000, 64), 'float32')]


def kernel(**inputs):
    import numpy as _np
    import concourse.bacc as _bacc
    from concourse import mybir as _mybir
    from concourse.bass_utils import run_bass_kernel_spmd as _run

    nc = _bacc.Bacc("TRN2", target_bir_lowering=False, num_devices=1)
    arrays, args = {}, []
    for name in _INS:
        a = _np.ascontiguousarray(inputs[name])
        arrays[f"in_{name}_dram"] = a
        args.append(nc.dram_tensor(f"in_{name}_dram", a.shape, _mybir.dt.from_np(a.dtype), kind="ExternalInput").ap())
    for i, (shape, dtype) in enumerate(_OUTS):
        dt = _mybir.dt.from_np(_np.dtype(dtype))
        args.append(nc.dram_tensor(f"out_{i}_dram", shape, dt, kind="ExternalOutput").ap())
    graph_layers(nc, *args)
    r = _run(nc, [arrays], core_ids=[0])
    return r.results[0]["out_0_dram"]
```
